# Optimizing a Trainium2 kernel written in Bass

```python
import numpy as np
import jax
import jax.numpy as jnp

def _softmax(x, axis=-1):
    return jax.nn.softmax(x, axis=axis)

def _gelu(x):
    return jax.nn.gelu(x, approximate=True)

def _silu(x):
    return jax.nn.silu(x)

def _sigmoid(x):
    return jax.nn.sigmoid(x)

def _layernorm(x, axis=-1, eps=1e-05):
    m = jnp.mean(x, axis=axis, keepdims=True)
    v = jnp.var(x, axis=axis, keepdims=True)
    return (x - m) / jnp.sqrt(v + eps)

def _scatter_add(tgt, idx, src, axis=0):
    return tgt.at[idx].add(src)

def _segment_sum(src, seg, n):
    return jax.ops.segment_sum(src, seg, n)
kernel_name = 'mk_macaron_d1_jaxref_r4_942f94'

def setup_inputs(seed: int=0):
    np.random.seed(seed)
    _w = jnp.asarray

    def _L0_attn_setup():
        import jax, jax.numpy as jnp
        import numpy as np
        D = 256
        M = 16
        H = D // M
        EPS = 1e-05

        def _rmsnorm(x, w, eps=EPS):
            var = jnp.mean(jnp.square(x), axis=-1, keepdims=True)
            return x * jax.lax.rsqrt(var + eps) * w
        key = jax.random.key(seed)
        ks = jax.random.split(key, 5)
        B, T = (4, 256)
        x = jax.random.normal(ks[0], (B, T, D), dtype=jnp.float32)
        norm_w = jnp.ones((D,), dtype=jnp.float32)
        s = 1.0 / np.sqrt(D)
        W_v = jax.random.uniform(ks[1], (D, D), dtype=jnp.float32, minval=-s, maxval=s)
        W_a = jax.random.uniform(ks[2], (H * M * (M + 1), D), dtype=jnp.float32, minval=-s, maxval=s)
        W_out = jax.random.uniform(ks[3], (D, D), dtype=jnp.float32, minval=-s, maxval=s)
        return {'x': x, 'norm_w': norm_w, 'W_v': W_v, 'W_a': W_a, 'W_out': W_out}
    _L0_attn_in = _L0_attn_setup()

    def _L0_ffn_setup():
        import jax, jax.numpy as jnp
        import numpy as np
        D, H, E, K, S = (256, 512, 8, 2, 1)
        B, L = (4, 512)
        key = jax.random.key(seed)
        ks = jax.random.split(key, 9)
        std = 0.02
        return {'x': jax.random.normal(ks[0], (B, L, D), dtype=jnp.float32), 'router_w': jax.random.normal(ks[1], (E, D), dtype=jnp.float32) * std, 'experts_bias': jnp.zeros((E,), dtype=jnp.float32), 'w1': jax.random.normal(ks[2], (E, D, H), dtype=jnp.float32) * std, 'w3': jax.random.normal(ks[3], (E, D, H), dtype=jnp.float32) * std, 'w2': jax.random.normal(ks[4], (E, H, D), dtype=jnp.float32) * std, 'sw1': jax.random.normal(ks[5], (S, D, H), dtype=jnp.float32) * std, 'sw3': jax.random.normal(ks[6], (S, D, H), dtype=jnp.float32) * std, 'sw2': jax.random.normal(ks[7], (S, H, D), dtype=jnp.float32) * std}
    _L0_ffn_in = _L0_ffn_setup()
    _d = {'L0_attn_x': _L0_attn_in['x'], 'L0_attn_norm_w': _L0_attn_in['norm_w'], 'L0_attn_W_v': _L0_attn_in['W_v'], 'L0_attn_W_a': _L0_attn_in['W_a'], 'L0_attn_W_out': _L0_attn_in['W_out'], 'L0_ffn_router_w': _L0_ffn_in['router_w'], 'L0_ffn_experts_bias': _L0_ffn_in['experts_bias'], 'L0_ffn_w1': _L0_ffn_in['w1'], 'L0_ffn_w3': _L0_ffn_in['w3'], 'L0_ffn_w2': _L0_ffn_in['w2'], 'L0_ffn_sw1': _L0_ffn_in['sw1'], 'L0_ffn_sw3': _L0_ffn_in['sw3'], 'L0_ffn_sw2': _L0_ffn_in['sw2']}
    _x0 = _d['L0_attn_x']
    _d['L0_attn_x'] = jax.random.normal(jax.random.fold_in(jax.random.key(seed), 1), (8, 512, 256), dtype=_x0.dtype)
    del _x0
    return _d

def reference(L0_attn_x, L0_attn_norm_w, L0_attn_W_v, L0_attn_W_a, L0_attn_W_out, L0_ffn_router_w, L0_ffn_experts_bias, L0_ffn_w1, L0_ffn_w3, L0_ffn_w2, L0_ffn_sw1, L0_ffn_sw3, L0_ffn_sw2):

    def _L0_attn_ref(x, norm_w, W_v, W_a, W_out):
        import jax, jax.numpy as jnp
        import numpy as np
        D = 256
        M = 16
        H = D // M
        EPS = 1e-05

        def _rmsnorm(x, w, eps=EPS):
            var = jnp.mean(jnp.square(x), axis=-1, keepdims=True)
            return x * jax.lax.rsqrt(var + eps) * w
        B, T, _ = x.shape
        h = _rmsnorm(x, norm_w)
        v = (h @ W_v.T).reshape(B, T, H, M)
        gate_logits = (h @ W_a.T).reshape(B, T, H, M, M + 1)
        gates = jax.nn.softmax(gate_logits, axis=-1)
        a0 = gates[..., 0]
        A = gates[..., 1:]
        A_t = jnp.moveaxis(A, 1, 0)
        u_t = jnp.moveaxis(a0 * v, 1, 0)

        def step(state, inp):
            At, ut = inp
            new = jnp.einsum('bhij,bhj->bhi', At, state) + ut
            return (new, new)
        init = jnp.zeros((B, H, M), dtype=x.dtype)
        _, ys = jax.lax.scan(step, init, (A_t, u_t))
        h_out = jnp.moveaxis(ys, 0, 1).reshape(B, T, D)
        return x + h_out @ W_out.T

    def _L0_ffn_ref(x, router_w, experts_bias, w1, w3, w2, sw1, sw3, sw2):
        import jax, jax.numpy as jnp
        import numpy as np
        D, H, E, K, S = (256, 512, 8, 2, 1)
        B, L = (4, 512)
        b, l, d = x.shape
        xf = x.reshape(-1, d)
        sg = jnp.einsum('td,sdh->tsh', xf, sw1)
        su = jnp.einsum('td,sdh->tsh', xf, sw3)
        shared_out = jnp.einsum('tsh,shd->td', jax.nn.silu(sg) * su, sw2)
        logits = xf @ router_w.T + experts_bias
        rw, sel = jax.lax.top_k(logits, K)
        rw = jax.nn.softmax(rw.astype(jnp.float32), axis=-1).astype(x.dtype)
        cw = (jax.nn.one_hot(sel, E, dtype=x.dtype) * rw[..., None]).sum(axis=1)
        g = jnp.einsum('td,edh->teh', xf, w1)
        u = jnp.einsum('td,edh->teh', xf, w3)
        eo = jax.nn.silu(g) * u
        moe_out = jnp.einsum('te,teh,ehd->td', cw, eo, w2)
        return (moe_out + shared_out).reshape(b, l, d)
    x = L0_attn_x
    x = x + 0.5 * _L0_ffn_ref(_layernorm(x, axis=-1), L0_ffn_router_w, L0_ffn_experts_bias, L0_ffn_w1, L0_ffn_w3, L0_ffn_w2, L0_ffn_sw1, L0_ffn_sw3, L0_ffn_sw2)
    x = x + _L0_attn_ref(_layernorm(x, axis=-1), L0_attn_norm_w, L0_attn_W_v, L0_attn_W_a, L0_attn_W_out)
    x = x + 0.5 * _L0_ffn_ref(_layernorm(x, axis=-1), L0_ffn_router_w, L0_ffn_experts_bias, L0_ffn_w1, L0_ffn_w3, L0_ffn_w2, L0_ffn_sw1, L0_ffn_sw3, L0_ffn_sw2)
    return x

_drawn_inputs = setup_inputs


def setup_inputs(seed=0):
    import zlib

    import numpy as np

    out = dict(_drawn_inputs(seed))
    spreads = {'L0_attn_norm_w': (1.0, 0.6), 'L0_ffn_experts_bias': (0.0, 0.8)}
    factors = {'L0_attn_W_v': 3.719,
     'L0_attn_W_a': 7.025,
     'L0_attn_W_out': 3.529,
     'L0_ffn_router_w': 5.204,
     'L0_ffn_w1': 4.477,
     'L0_ffn_w3': 4.433,
     'L0_ffn_w2': 4.428,
     'L0_ffn_sw1': 3.185,
     'L0_ffn_sw3': 3.133,
     'L0_ffn_sw2': 3.151}
    for name, (base, spread) in spreads.items():
        noise = np.random.default_rng([zlib.crc32(name.encode()), seed]).standard_normal(out[name].shape)
        drawn = base * np.exp(spread * noise) if base else spread * noise
        out[name] = jnp.asarray(drawn.astype(out[name].dtype))
    for name, factor in factors.items():
        out[name] = (out[name] * factor).astype(out[name].dtype)
    return out
```

```python
from contextlib import ExitStack

import concourse.bass as bass
from concourse import mybir

F32 = mybir.dt.float32
F16 = mybir.dt.float16
I32 = mybir.dt.int32
U32 = mybir.dt.uint32
ALU = mybir.AluOpType
ACT = mybir.ActivationFunctionType
AX = mybir.AxisListType

P = 128
BATCH, TIME, D = 8, 512, 256
STEPS = P // BATCH
TILES = TIME // STEPS
KD = D // P
HID = 512
HC = HID // P
NE = 8
ITEM = 256
SHARED = BATCH * TIME // ITEM
SPARSE = 2 * BATCH * TIME // ITEM + NE - 1
HEADS, M = 16, 16
GATE = M * (M + 1)
ROW = GATE + M
WS = 64.0
AS = 4.0
EPS = 1e-5
WEXP = 2 * (2 * KD * HID + HC * D)
O1H, O1L = 0, KD * HID
O3H, O3L = 2 * KD * HID, 3 * KD * HID
O2H, O2L = 4 * KD * HID, 4 * KD * HID + HC * D
KEPT = 2


class Core:
    pass


def load_inputs(nc, g, a):
    with ExitStack() as ctx:
        sem = lambda n: ctx.enter_context(nc.semaphore(n))
        x_in, small_in, iotas, tri, ident_z, consts, zero_ready = map(sem, (
            "x_in", "small_in", "iotas", "tri", "ident_z", "consts", "zero_ready"))
        raw_in = [sem("raw_in0"), sem("raw_in1")]
        w_hi, w_lo, w_kept, slots_zeroed = map(sem, ("w_hi", "w_lo", "w_kept", "slots_zeroed"))
        raw = [g.late[:, r * 3072:(r + 1) * 3072] for r in range(2)]
        order = [NE] + list(range(NE))
        block = ctx.enter_context(nc.Block())

        @block.sync
        def _(sp):
            for n, e in enumerate(order):
                r = raw[n % 2]
                w1, w3, w2 = (a["sw1"][0], a["sw3"][0], a["sw2"][0]) if e == NE else (
                    a["w1"][e], a["w3"][e], a["w2"][e])
                if n >= 2:
                    sp.wait_ge(w_hi, n - 1)
                    sp.wait_ge(w_lo, n - 1)
                c = KD * HID
                sp.dma_start(r[:, 0:c].rearrange("p (k n) -> p k n", k=KD),
                             w1.rearrange("(k p) n -> p k n", p=P)).then_inc(raw_in[n % 2], 16)
                sp.dma_start(r[:, c:2 * c].rearrange("p (k n) -> p k n", k=KD),
                             w3.rearrange("(k p) n -> p k n", p=P)).then_inc(raw_in[n % 2], 16)
                sp.dma_start(r[:, 2 * c:2 * c + HC * D].rearrange("p (k n) -> p k n", k=HC),
                             w2.rearrange("(k p) n -> p k n", p=P)).then_inc(raw_in[n % 2], 16)
            sp.wait_ge(w_hi, len(order))
            sp.wait_ge(w_lo, len(order))
            sp.dma_start(g.w_dram, g.wf[:, KEPT * WEXP:NE * WEXP]).then_inc(w_kept, 16)
            sp.wait_ge(w_kept, 16)

        @block.gpsimd
        def _(pool):
            for b in range(BATCH):
                pool.dma_start(g.x[b * STEPS:(b + 1) * STEPS],
                               a["x"][b].rearrange("(n t) d -> t n d", t=STEPS)).then_inc(x_in, 16)
            with nc.allow_non_contiguous_dma(reason="2304 words, once"):
                for k in range(KD):
                    pool.dma_start(g.rw_raw[:, k],
                                   a["router_w"][:, k * P:(k + 1) * P].rearrange("e p -> p e")).then_inc(small_in, 16)
                pool.dma_start(g.nw, a["norm_w"].rearrange("(k p) -> p k", p=P)).then_inc(small_in, 16)
            pool.dma_start(g.bias, a["bias"].partition_broadcast(P)).then_inc(small_in, 16)
            pool.memset(g.ident, 0.0).then_inc(ident_z, 1)
            pool.memset(g.ones, 1.0).then_inc(ident_z, 1)
            pool.memset(g.before, 1.0).then_inc(ident_z, 1)
            pool.memset(g.work[:, 0:2 * D], 0.0).then_inc(zero_ready, 1)
            pool.memset(g.eps, EPS).then_inc(tri, 1)
            pool.iota(g.iota_i[:, 0:NE], pattern=[[1, NE]], base=0, channel_multiplier=0).then_inc(iotas, 1)
            pool.iota(g.iota_i[:, NE:NE + SHARED], pattern=[[ITEM, SHARED]], base=0, channel_multiplier=0).then_inc(iotas, 1)
            pool.iota(g.iota_i[:, NE + SHARED:], pattern=[[1, SPARSE]], base=0, channel_multiplier=0).then_inc(iotas, 1)
            pool.wait_ge(ident_z, 3)
            pool.affine_select(out=g.ident, in_=g.ident, compare_op=ALU.not_equal, fill=1.0, base=0,
                               pattern=[[-1, P]], channel_multiplier=1).then_inc(tri, 1)
            pool.affine_select(out=g.before, in_=g.before, compare_op=ALU.is_gt, fill=0.0, base=0,
                               pattern=[[1, P]], channel_multiplier=-1).then_inc(tri, 1)
            pool.wait_ge(zero_ready, 1)
            for n in range(SPARSE):
                pool.dma_start(g.slots[n * ITEM:(n + 1) * ITEM].rearrange("(s p) d -> p s d", p=P),
                               g.work[:, 0:2 * D].rearrange("p (s d) -> p s d", s=2)).then_inc(slots_zeroed, 16)
            pool.wait_ge(slots_zeroed, 16 * SPARSE)
            pool.wait_ge(x_in, 16 * BATCH)
            pool.wait_ge(tri, 3)

        @block.scalar
        def _(act):
            act.wait_ge(small_in, 16 * (KD + 2))
            act.activation(g.rw[:, 0], g.rw_raw, ACT.Copy, scale=WS).then_inc(consts, 1)
            for n, e in enumerate(order):
                act.wait_ge(raw_in[n % 2], 48 * (n // 2 + 1))
                for o_hi, o_raw in ((O1H, 0), (O3H, KD * HID), (O2H, 2 * KD * HID)):
                    last = act.activation(g.wf[:, e * WEXP + o_hi:e * WEXP + o_hi + KD * HID],
                                          raw[n % 2][:, o_raw:o_raw + KD * HID], ACT.Copy, scale=WS)
                last.then_inc(w_hi, 1)

        @block.vector
        def _(dve):
            dve.wait_ge(consts, 1)
            dve.scalar_tensor_tensor(out=g.rw[:, 1], in0=g.rw_raw, scalar=WS, in1=g.rw[:, 0],
                                     op0=ALU.mult, op1=ALU.subtract)
            dve.wait_ge(iotas, 3)
            dve.tensor_copy(g.iota, g.iota_i)
            for n, e in enumerate(order):
                dve.wait_ge(w_hi, n + 1)
                for o_hi, o_lo, o_raw in ((O1H, O1L, 0), (O3H, O3L, KD * HID), (O2H, O2L, 2 * KD * HID)):
                    w = e * WEXP
                    last = dve.scalar_tensor_tensor(
                        out=g.wf[:, w + o_lo:w + o_lo + KD * HID], in0=raw[n % 2][:, o_raw:o_raw + KD * HID],
                        scalar=WS, in1=g.wf[:, w + o_hi:w + o_hi + KD * HID], op0=ALU.mult, op1=ALU.subtract)
                last.then_inc(w_lo, 1)


def token_statistics(nc, g, dve, stat):
    with dve.Fori(0, TILES) as t:
        dve.bn_stats(g.stats[:, bass.ds(t * 6, 6)], g.x2[:, bass.ds(t * D, D)]).then_inc(stat, 1)
    dve.wait_ge(stat, TILES)
    for t in range(TILES):
        last = dve.bn_aggr(g.mv3[:, t], g.stats[:, t * 6:(t + 1) * 6])
    last.then_inc(stat, 1)


def ffn(nc, g, tag, reload):
    with ExitStack() as ctx:
        def sem(n):
            return ctx.enter_context(nc.semaphore(f"{tag}_{n}"))

        w = g.work
        rows = [w[:, r * 512:(r + 1) * 512] for r in range(2)]
        xt = [w[:, 1024 + r * 512:1536 + r * 512].bitcast(F16).rearrange("p (l k t) -> p l k t", l=2, k=KD) for r in range(2)]
        th = [w[:, 2048 + r * 512:2560 + r * 512] for r in range(2)]
        hid = [w[:, 3072 + r * 512:3584 + r * 512] for r in range(2)]
        hb = [w[:, 4096 + r * 512:4608 + r * 512].bitcast(F16).rearrange("p (l c t) -> p l c t", l=2, c=2) for r in range(4)]
        yst = [g.late[:, 8192 + r * 512:8704 + r * 512] for r in range(2)]
        gat = [g.late[:, 8192 + r * 256:8448 + r * 256] for r in range(4)]
        at = [3072]

        def temp(n):
            at[0] += n
            assert at[0] <= 6144
            return w[:, at[0] - n:at[0]]

        logit, best, oh0, oh1 = temp(256), temp(256), temp(256), temp(256)
        besti = temp(256).bitcast(U32)
        chosen = temp(64)
        member = temp(128).bitcast(F16)
        cum, slot_of, prod = temp(256), temp(256), temp(256)
        fills = temp(NE * SHARED)
        ntile, tend, count = temp(NE), temp(NE), temp(NE)
        passed = temp(SPARSE * NE)
        slot_f, ediff = temp(64), temp(32)
        logit3, best3, besti3 = (v.rearrange("p (t e) -> p t e", e=NE) for v in (logit, best, besti))
        chosen3 = chosen.rearrange("p (k t) -> p k t", k=2)

        gp, up_, yp = (g.psum[:, 0:2], g.psum[:, 2:4], g.psum[:, 4:6])
        tp, rp = g.psum[:, 6], g.psum[:, 7]
        router_ps = rp[:, 0:256]

        (stat, var_ok, std, r_rows, r_t, r_hi, r_lo, r_mm, xn_copied, logits_ok, rt, diff_ok, e_ok,
         member_ok, rank_ok, slots_ok, scattered, rows_sh, t_done, x_hi, x_lo, up_done, tanh_ok,
         s_ok, hid_ok, h_hi, h_lo, dn_done, y_sh, y_sp, gathered, added, texp_ok, w_back) = map(sem, (
             "stat", "var_ok", "std", "r_rows", "r_t", "r_hi", "r_lo", "r_mm", "xn_copied", "logits_ok",
             "rt", "diff_ok", "e_ok", "member_ok", "rank_ok", "slots_ok", "scattered", "rows_sh", "t_done",
             "x_hi", "x_lo", "up_done", "tanh_ok", "s_ok", "hid_ok", "h_hi", "h_lo", "dn_done", "y_sh",
             "y_sp", "gathered", "added", "texp_ok", "w_back"))
        rows_sp = [sem("rows_sp0"), sem("rows_sp1")]
        y_out = [sem("y_out0"), sem("y_out1")]
        gat_in = [sem(f"gat_in{r}") for r in range(4)]
        block = ctx.enter_context(nc.Block())

        @block.tensor
        def _(pe):
            def transposes(par, done):
                for k in range(KD):
                    for s in range(2):
                        c = (k * 2 + s) * P
                        last = pe.transpose(tp[:, c:c + P], rows[par][:, s * D + k * P:s * D + (k + 1) * P], g.ident)
                last.then_inc(done, 1)

            def router(n, par):
                pe.wait_ge(r_rows, n + 1)
                transposes_wait = n
                pe.wait_ge(r_lo, transposes_wait)
                transposes(par, r_t)
                pe.wait_ge(r_lo, n + 1)
                for s in range(2):
                    col = n * 2 * NE + s * NE
                    i = 0
                    for k in range(KD):
                        for lx, lw in ((0, 0), (0, 1), (1, 0)):
                            last = pe.matmul(router_ps[:, bass.ds(col, NE)], xt[par][:, lx, k, s * P:(s + 1) * P],
                                             g.rw[:, lw, k], start=(i == 0), stop=(i == 5))
                            i += 1
                last.then_inc(r_mm, 1)

            with pe.Fori(0, SHARED // 2) as q:
                router(2 * q, 0)
                router(2 * q + 1, 1)

            pe.wait_ge(member_ok, 1)
            pe.matmul(rp[:, 0:256], g.before, member, start=True, stop=True)
            pe.matmul(rp[:, 256:512], g.ones, member, start=True, stop=True).then_inc(rank_ok, 1)

            def first_rows(gi, par):
                pe.wait_ge(rows_sh, gi + 1)
                if not (isinstance(gi, int) and gi == 0):
                    pe.wait_ge(x_lo, gi)
                transposes(par, t_done)

            def sparse_rows(gi, half, par):
                pe.wait_ge(rows_sp[par], 16 * (half - SHARED // 2) + 16)
                pe.wait_ge(x_lo, gi)
                transposes(par, t_done)

            def up(gi, par, h, wbase):
                m = 2 * gi + h
                if h == 0:
                    pe.wait_ge(x_lo, gi + 1)
                if not (isinstance(gi, int) and gi == 0):
                    pe.wait_ge(hid_ok, m - 1)
                for ps, o_hi, o_lo in ((gp, O1H, O1L), (up_, O3H, O3L)):
                    for c in range(2):
                        i = 0
                        for k in range(KD):
                            for lx, o in ((0, o_hi), (0, o_lo), (1, o_hi)):
                                off = o + k * HID + (2 * h + c) * P
                                last = pe.matmul(ps[:, h, c * ITEM:(c + 1) * ITEM], g.wf[:, bass.ds(wbase + off, P)],
                                                 xt[par][:, lx, k], start=(i == 0), stop=(i == 5))
                                i += 1
                last.then_inc(up_done, 1)

            def down(gi, par, h, wbase):
                m = 2 * gi + h
                pe.wait_ge(h_lo, m + 1)
                i = 0
                for c in range(2):
                    for lh, o in ((0, O2H), (0, O2L), (1, O2H)):
                        for s in range(2):
                            off = o + (2 * h + c) * D
                            last = pe.matmul(yp[:, par, s * D:(s + 1) * D],
                                             hb[2 * par + h][:, lh, c, s * P:(s + 1) * P],
                                             g.wf[:, bass.ds(wbase + off, D)],
                                             start=(h == 0 and i == 0), stop=(h == 1 and c == 1 and lh == 1),
                                             skip_group_check=True)
                            i += 1
                last.then_inc(dn_done, 1)

            def item(gi, par, wu, wd, rows_next, y_free):
                up(gi, par, 0, wu)
                rows_next()
                if wd is not None:
                    y_free()
                    down(gi - 1, 1 - par, 0, wd)
                up(gi, par, 1, wu)
                if wd is not None:
                    down(gi - 1, 1 - par, 1, wd)

            ws = NE * WEXP
            nothing = lambda: None
            first_rows(0, 0)
            item(0, 0, ws, None, lambda: first_rows(1, 1), nothing)
            item(1, 1, ws, ws, lambda: first_rows(2, 0), nothing)
            item(2, 0, ws, ws, lambda: first_rows(3, 1), nothing)
            with pe.Fori(0, (SHARED - 4) // 2) as q:
                a, b = 2 * q + 3, 2 * q + 4
                item(a, 1, ws, ws, lambda: first_rows(a + 1, 0), lambda: pe.wait_ge(y_sh, a - 2))
                item(b, 0, ws, ws, lambda: first_rows(b + 1, 1), lambda: pe.wait_ge(y_sh, b - 2))
            gi = SHARED - 1
            item(gi, 1, ws, ws, lambda: sparse_rows(SHARED, SHARED // 2, 0), lambda: pe.wait_ge(y_sh, gi - 2))

            def expert(n):
                return pe.snap(pe.value_load(g.texp[0:1, bass.ds(n, 1)], min_val=0, max_val=NE - 1)) * WEXP

            pe.wait_ge(texp_ok, 1)
            if reload:
                pe.wait_ge(w_back, 16)
            gi = SHARED
            e0 = expert(0)
            item(gi, 0, e0, ws, lambda: sparse_rows(gi + 1, gi // 2, 1), lambda: pe.wait_ge(y_sh, gi - 2))
            item(gi + 1, 1, expert(1), expert(0), lambda: sparse_rows(gi + 2, gi // 2 + 1, 0), lambda: pe.wait_ge(y_sh, gi - 1))
            item(gi + 2, 0, expert(2), expert(1), lambda: sparse_rows(gi + 3, gi // 2 + 1, 1), lambda: pe.wait_ge(y_sh, gi))
            with pe.Fori(0, (SPARSE - 5) // 2) as q:
                for u in range(2):
                    n = 2 * q + 3 + u
                    a = SHARED + n
                    if u == 0:
                        item(a, 1, expert(n), expert(n - 1), lambda: sparse_rows(a + 1, q + SHARED // 2 + 2, 0),
                             lambda: pe.wait_ge(y_sp, n - 2))
                    else:
                        item(a, 0, expert(n), expert(n - 1),
                             lambda: sparse_rows(a + 1, q + SHARED // 2 + 2, 1), lambda: pe.wait_ge(y_sp, n - 2))
            n, gi = SPARSE - 2, SHARED + SPARSE - 2
            item(gi, 1, expert(n), expert(n - 1), lambda: sparse_rows(gi + 1, (gi + 1) // 2, 0), lambda: pe.wait_ge(y_sp, n - 2))
            last_e = expert(n + 1)
            item(gi + 1, 0, last_e, expert(n), nothing, lambda: pe.wait_ge(y_sp, n - 1))
            pe.wait_ge(y_sp, n)
            down(gi + 1, 0, 0, last_e)
            down(gi + 1, 0, 1, last_e)

        @block.scalar
        def _(act):
            act.wait_ge(var_ok, 1)
            act.activation(g.std, g.mv3[:, :, 1], ACT.Sqrt, bias=g.eps, scale=1.0).then_inc(std, 1)

            def router(n, par):
                act.wait_ge(r_t, n + 1)
                if not (isinstance(n, int) and n < 2):
                    act.wait_ge(r_mm, n - 1)
                act.activation(xt[par][:, 0].rearrange("p k t -> p (k t)"), tp, ACT.Copy).then_inc(r_hi, 1)

            router(0, 0)
            router(1, 1)
            with act.Fori(1, SHARED // 2) as q:
                router(2 * q, 0)
                router(2 * q + 1, 1)
            act.wait_ge(diff_ok, 1)
            act.activation(ediff, ediff, ACT.Exp).then_inc(e_ok, 1)

            def x_high(gi, par, last_up):
                act.wait_ge(t_done, gi + 1)
                if last_up is not None:
                    act.wait_ge(up_done, last_up)
                act.activation(xt[par][:, 0].rearrange("p k t -> p (k t)"), tp, ACT.Copy).then_inc(x_hi, 1)

            def half(gi, par, h):
                m = 2 * gi + h
                act.wait_ge(up_done, m + 1)
                if not (isinstance(gi, int) and gi == 0):
                    act.wait_ge(hid_ok, m - 1)
                act.activation(th[h], gp[:, h], ACT.Tanh, scale=0.5 / WS).then_inc(tanh_ok, 1)

            def hid_high(gi, par, h):
                m = 2 * gi + h
                act.wait_ge(hid_ok, m + 1)
                if not (isinstance(gi, int) and gi < 2):
                    act.wait_ge(dn_done, m - 3)
                act.activation(hb[2 * par + h][:, 0].rearrange("p c t -> p (c t)"), hid[h], ACT.Copy).then_inc(h_hi, 1)

            def item(gi, par, nxt, y_copy):
                half(gi, par, 0)
                if nxt:
                    x_high(gi + 1, 1 - par, None if isinstance(gi, int) and gi == 0 else 2 * gi)
                hid_high(gi, par, 0)
                half(gi, par, 1)
                hid_high(gi, par, 1)
                y_copy()

            def y_stage(gi, par, n, first):
                act.wait_ge(dn_done, 2 * gi + 2)
                if not first:
                    act.wait_ge(y_out[par], first_free(n))
                act.activation(yst[par], yp[:, par], ACT.Copy).then_inc(y_sp, 1)

            def first_free(nh):
                return 16 * nh

            nothing = lambda: None
            x_high(0, 0, None)
            item(0, 0, True, nothing)
            item(1, 1, True, nothing)
            item(2, 0, True, nothing)
            with act.Fori(0, (SHARED - 4) // 2) as q:
                item(2 * q + 3, 1, True, nothing)
                item(2 * q + 4, 0, True, nothing)
            item(SHARED - 1, 1, True, nothing)
            gi = SHARED
            item(gi, 0, True, nothing)
            item(gi + 1, 1, True, lambda: y_stage(gi, 0, 0, True))
            item(gi + 2, 0, True, lambda: y_stage(gi + 1, 1, 0, True))
            with act.Fori(0, (SPARSE - 5) // 2) as q:
                b = SHARED + 2 * q + 3
                item(b, 1, True, lambda: y_stage(b - 1, 0, q + 1, False))
                item(b + 1, 0, True, lambda: y_stage(b, 1, q + 1, False))
            gi = SHARED + SPARSE - 2
            item(gi, 1, True, lambda: y_stage(gi - 1, 0, SPARSE // 2 - 1, False))
            item(gi + 1, 0, False, lambda: y_stage(gi, 1, SPARSE // 2 - 1, False))
            y_stage(SHARED + SPARSE - 1, 0, SPARSE // 2, False)

        @block.vector
        def _(dve):
            token_statistics(nc, g, dve, stat)
            dve.wait_ge(stat, TILES + 1)
            dve.engine_nop().then_inc(var_ok, 1)
            dve.wait_ge(std, 1)
            dve.reciprocal(g.rstd, g.std).then_inc(rt, 1)
            dve.wait_ge(rt, 1)

            def normalise(par, n, done):
                for s in range(2):
                    t = 2 * n + s
                    last = dve.tensor_scalar(rows[par][:, s * D:(s + 1) * D], g.x2[:, bass.ds(t * D, D)],
                                             g.mv[:, bass.ds(2 * t, 1)], g.rstd[:, bass.ds(t, 1)], ALU.subtract, ALU.mult)
                last.then_inc(done, 1)

            def low(par, hi_done, n, lo_done):
                dve.wait_ge(hi_done, n + 1)
                dve.tensor_tensor(xt[par][:, 1].rearrange("p k t -> p (k t)"), tp,
                                  xt[par][:, 0].rearrange("p k t -> p (k t)"), ALU.subtract).then_inc(lo_done, 1)

            normalise(0, 0, r_rows)
            normalise(1, 1, r_rows)
            with dve.Fori(0, SHARED // 2 - 1) as q:
                for u in range(2):
                    n = 2 * q + u
                    low(u, r_hi, n, r_lo)
                    dve.wait_ge(xn_copied, n + 1)
                    normalise(u, n + 2, r_rows)
            low(0, r_hi, SHARED - 2, r_lo)
            low(1, r_hi, SHARED - 1, r_lo)

            chain = [1]

            def then(ins):
                ins.then_inc(rt, 1)
                chain[0] += 1
                dve.wait_ge(rt, chain[0])

            dve.wait_ge(r_mm, SHARED)
            then(dve.scalar_tensor_tensor(out=logit3, in0=router_ps.rearrange("p (t e) -> p t e", e=NE), scalar=1.0 / WS,
                                          in1=g.bias.unsqueeze(1).broadcast_to((P, TILES, NE)), op0=ALU.mult, op1=ALU.add))
            for t in range(TILES):
                last = dve.max(best3[:, t], logit3[:, t])
            then(last)
            for t in range(TILES):
                last = dve.max_index(besti3[:, t], best3[:, t], logit3[:, t])
            then(last)
            dve.tensor_tensor(ediff, best3[:, :, 1], best3[:, :, 0], ALU.subtract).then_inc(diff_ok, 1)
            then(dve.tensor_copy(chosen3, besti3[:, :, 0:2].rearrange("p t k -> p k t")))
            iota_e = g.iota[:, 0:NE].unsqueeze(1).broadcast_to((P, TILES, NE))
            for k, oh in ((0, oh0), (1, oh1)):
                then(dve.tensor_tensor(oh.rearrange("p (t e) -> p t e", e=NE), iota_e,
                                       chosen3[:, k].unsqueeze(2).broadcast_to((P, TILES, NE)), ALU.is_equal))
            dve.tensor_tensor(member, oh0, oh1, ALU.add).then_inc(member_ok, 1)
            dve.wait_ge(e_ok, 1)
            then(dve.tensor_scalar(slot_f[:, 0:TILES], ediff, 1.0, None, ALU.add))
            then(dve.reciprocal(slot_f[:, 32:32 + TILES], slot_f[:, 0:TILES]))
            then(dve.tensor_scalar(g.cw[:, 0:TILES], slot_f[:, 32:32 + TILES], 0.5 / (WS * AS), None, ALU.mult))
            then(dve.tensor_tensor(g.cw[:, TILES:2 * TILES], g.cw[:, 0:TILES], ediff, ALU.mult))
            dve.wait_ge(rank_ok, 1)
            tot3 = rp[:, 256:512].rearrange("p (t e) -> p e t", e=NE)
            cum3 = cum.rearrange("p (e t) -> p e t", e=NE)
            then(dve.memset(prod[:, 0:TILES], 0.0))
            for e in range(NE):
                last = dve.tensor_tensor_scan(cum3[:, e], tot3[:, e], prod[:, 0:TILES], 0.0, ALU.add, ALU.add)
            then(last)
            then(dve.tensor_copy(count, cum3[:, :, TILES - 1]))
            fills3 = fills.rearrange("p (e j) -> p e j", e=NE)
            then(dve.tensor_tensor(fills3, count.unsqueeze(2).broadcast_to((P, NE, SHARED)),
                                   g.iota[:, NE:NE + SHARED].unsqueeze(1).broadcast_to((P, NE, SHARED)), ALU.is_gt))
            then(dve.tensor_reduce(ntile, fills3, AX.X, ALU.add))
            then(dve.tensor_tensor_scan(tend, ntile, prod[:, 0:NE], 0.0, ALU.add, ALU.add))
            then(dve.tensor_tensor(count, tend, ntile, ALU.subtract))
            slot3 = slot_of.rearrange("p (t e) -> p t e", e=NE)
            then(dve.tensor_tensor(slot3, cum3.rearrange("p e t -> p t e"), rp[:, 256:512].rearrange("p (t e) -> p t e", e=NE), ALU.subtract))
            then(dve.tensor_tensor(slot3, slot3, rp[:, 0:256].rearrange("p (t e) -> p t e", e=NE), ALU.add))
            then(dve.scalar_tensor_tensor(out=slot3, in0=count.unsqueeze(1).broadcast_to((P, TILES, NE)), scalar=float(ITEM),
                                          in1=slot3, op0=ALU.mult, op1=ALU.add))
            for k, oh in ((0, oh0), (1, oh1)):
                then(dve.tensor_tensor(prod, oh, slot_of, ALU.mult))
                then(dve.tensor_reduce(slot_f[:, k * TILES:(k + 1) * TILES], prod.rearrange("p (t e) -> p t e", e=NE), AX.X, ALU.add))
            then(dve.tensor_copy(g.slot, slot_f))
            dve.engine_nop().then_inc(slots_ok, 1)
            passed3 = passed.rearrange("p (n e) -> p n e", e=NE)
            then(dve.tensor_tensor(passed3, g.iota[:, NE + SHARED:].unsqueeze(2).broadcast_to((P, SPARSE, NE)),
                                   tend.unsqueeze(1).broadcast_to((P, SPARSE, NE)), ALU.is_ge))
            then(dve.tensor_reduce(prod[:, 0:SPARSE], passed3, AX.X, ALU.add))
            then(dve.tensor_scalar(g.texp, prod[:, 0:SPARSE], NE - 1.0, None, ALU.min))
            dve.engine_nop().then_inc(texp_ok, 1)

            def half(gi, par, h):
                m = 2 * gi + h
                dve.wait_ge(tanh_ok, m + 1)
                dve.scalar_tensor_tensor(out=th[h], in0=th[h], scalar=1.0, in1=gp[:, h], op0=ALU.add, op1=ALU.mult).then_inc(s_ok, 1)
                dve.wait_ge(s_ok, m + 1)
                dve.scalar_tensor_tensor(out=hid[h], in0=th[h], scalar=AS / (2 * WS * WS), in1=up_[:, h],
                                         op0=ALU.mult, op1=ALU.mult).then_inc(hid_ok, 1)

            def hid_low(gi, par, h):
                m = 2 * gi + h
                dve.wait_ge(h_hi, m + 1)
                dve.tensor_tensor(hb[2 * par + h][:, 1].rearrange("p c t -> p (c t)"), hid[h],
                                  hb[2 * par + h][:, 0].rearrange("p c t -> p (c t)"), ALU.subtract).then_inc(h_lo, 1)

            def add_y(gi, par):
                dve.wait_ge(dn_done, 2 * gi + 2)
                xs = g.x2[:, bass.ds(gi * 2 * D, 2 * D)]
                dve.scalar_tensor_tensor(out=xs, in0=yp[:, par], scalar=0.5 / (WS * AS), in1=xs,
                                         op0=ALU.mult, op1=ALU.add).then_inc(y_sh, 1)

            def item(gi, par, nxt, rows_after, add):
                half(gi, par, 0)
                if nxt:
                    low(1 - par, x_hi, gi + 1, x_lo)
                hid_low(gi, par, 0)
                half(gi, par, 1)
                if rows_after:
                    dve.wait_ge(t_done, gi + 1)
                    normalise(par, gi + 2, rows_sh)
                hid_low(gi, par, 1)
                if add:
                    add_y(gi - 1, 1 - par)

            dve.wait_ge(xn_copied, SHARED)
            normalise(0, 0, rows_sh)
            normalise(1, 1, rows_sh)
            low(0, x_hi, 0, x_lo)
            item(0, 0, True, True, False)
            with dve.Fori(0, (SHARED - 4) // 2) as q:
                item(2 * q + 1, 1, True, True, True)
                item(2 * q + 2, 0, True, True, True)
            item(SHARED - 3, 1, True, True, True)
            item(SHARED - 2, 0, True, False, True)
            item(SHARED - 1, 1, True, False, True)
            item(SHARED, 0, True, False, True)
            with dve.Fori(0, (SPARSE - 3) // 2) as q:
                b = SHARED + 2 * q + 1
                item(b, 1, True, False, False)
                item(b + 1, 0, True, False, False)
            item(SHARED + SPARSE - 2, 1, True, False, False)
            item(SHARED + SPARSE - 1, 0, False, False, False)

            def combine(t, r, k, cnt):
                dve.wait_ge(gat_in[r], cnt)
                xs = g.x2[:, bass.ds(t * D, D)]
                if k == 1:
                    dve.wait_ge(added, 2 * t + 1)
                dve.scalar_tensor_tensor(out=xs, in0=gat[r], scalar=g.cw[:, bass.ds(t + k * TILES, 1)], in1=xs,
                                         op0=ALU.mult, op1=ALU.add).then_inc(added, 1)

            with dve.Fori(0, TILES // 2) as q:
                for u in range(2):
                    for k in range(2):
                        combine(2 * q + u, 2 * u + k, k, 16 * q + 16)

        @block.gpsimd
        def _(pool):
            def copy_rows(n, par):
                pool.wait_ge(r_rows, n + 1)
                pool.tensor_copy(g.xn[:, bass.ds(n * 2 * D, 2 * D)], rows[par]).then_inc(xn_copied, 1)

            with pool.Fori(0, SHARED // 2) as q:
                copy_rows(2 * q, 0)
                copy_rows(2 * q + 1, 1)
            pool.wait_ge(xn_copied, SHARED)
            pool.wait_ge(slots_ok, 1)
            for t in range(TILES):
                for k in range(2):
                    pool.indirect_dma_start(g.slots, bass.IndirectOffsetOnAxis(ap=g.slot[:, k * TILES + t:k * TILES + t + 1], axis=0),
                                            g.xn[:, t * D:(t + 1) * D], None).then_inc(scattered, 16)
            pool.wait_ge(y_out[0], 16 * (SPARSE // 2 + 1))
            pool.wait_ge(y_out[1], 16 * (SPARSE // 2))
            for t in range(TILES):
                for k in range(2):
                    r = 2 * (t % 2) + k
                    if t >= 2:
                        pool.wait_ge(added, 2 * (t - 2) + k + 1)
                    pool.indirect_dma_start(gat[r], None, g.outs,
                                            bass.IndirectOffsetOnAxis(ap=g.slot[:, k * TILES + t:k * TILES + t + 1], axis=0)
                                            ).then_inc(gat_in[r], 16)

        @block.sync
        def _(sp):
            if reload:
                sp.dma_start(g.wf[:, KEPT * WEXP:NE * WEXP], g.w_dram).then_inc(w_back, 16)
            sp.wait_ge(scattered, 16 * 2 * TILES)

            def load(n, par, gi):
                first = sp.snap(n * ITEM)
                sp.wait_ge(t_done, gi - 1)
                sp.dma_start(rows[par].rearrange("p (s d) -> p s d", s=2),
                             g.slots[bass.ds(first, ITEM)].rearrange("(s p) d -> p s d", p=P)).then_inc(rows_sp[par], 16)

            def store(n, par):
                first = sp.snap(n * ITEM)
                sp.wait_ge(y_sp, n + 1)
                sp.dma_start(g.outs[bass.ds(first, ITEM)].rearrange("(s p) d -> p s d", p=P),
                             yst[par].rearrange("p (s d) -> p s d", s=2)).then_inc(y_out[par], 16)

            load(0, 0, SHARED)
            load(1, 1, SHARED + 1)
            with sp.Fori(0, (SPARSE - 3) // 2) as q:
                n = 2 * q
                load(n + 2, 0, SHARED + n + 2)
                store(n, 0)
                load(n + 3, 1, SHARED + n + 3)
                store(n + 1, 1)
            load(SPARSE - 1, 0, SHARED + SPARSE - 1)
            store(SPARSE - 3, 0)
            store(SPARSE - 2, 1)
            store(SPARSE - 1, 0)
            sp.wait_ge(y_out[0], 16 * (SPARSE // 2 + 1))


def attention(nc, g, a):
    with ExitStack() as ctx:
        def sem(n):
            return ctx.enter_context(nc.semaphore(f"att_{n}"))

        w = g.work
        at = [0]

        def take(n):
            at[0] += n
            assert at[0] <= g.work_words
            return w[:, at[0] - n:at[0]]

        hrow = [take(D) for _ in range(2)]
        ht = [take(D).bitcast(F16).rearrange("p (l k t) -> p l k t", l=2, k=KD) for _ in range(2)]
        vs = [take(D) for _ in range(2)]
        mx = [take(D) for _ in range(2)]
        tree = take(64 * 8).rearrange("p (g c) -> p g c", c=8)
        zsum = take(D)
        prod = take(GATE).rearrange("p (i j) -> p i j", j=M + 1)
        dots = take(M)
        state = [take(STEPS * (M + 1)).rearrange("p (t j) -> p t j", j=M + 1) for _ in range(2)]
        yc = take(D)
        ho = take(D)
        ot = take(D).bitcast(F16).rearrange("p (l k t) -> p l k t", l=2, k=KD)
        over = g.wf[:, KEPT * WEXP:NE * WEXP].bitcast(F32)
        n_e = HEADS * ROW
        gate = [over[:, r * n_e:(r + 1) * n_e].rearrange("p (h c) -> p h c", h=HEADS) for r in range(2)]
        step_g = [over[:, (2 + r) * n_e:(3 + r) * n_e].rearrange("p (t c) -> p t c", t=STEPS) for r in range(2)]
        raw = [over[:, r * 512:(r + 1) * 512] for r in range(4)]
        late = g.late.bitcast(F16)
        na = HEADS * GATE
        wa = [late[:, l * KD * na:(l + 1) * KD * na].rearrange("p (k n) -> p k n", k=KD) for l in range(2)]
        o = 2 * KD * na
        wv = [late[:, o + l * KD * D:o + (l + 1) * KD * D].rearrange("p (k n) -> p k n", k=KD) for l in range(2)]
        o += 2 * KD * D
        wo = [late[:, o + l * KD * D:o + (l + 1) * KD * D].rearrange("p (k n) -> p k n", k=KD) for l in range(2)]
        lp = [g.psum[:, 2 * r:2 * r + 2] for r in range(3)]
        tp, vo = g.psum[:, 6], g.psum[:, 7]
        v_ps, o_ps = vo[:, 0:D], vo[:, D:2 * D]
        tph, tpo = tp[:, 0:D], tp[:, D:2 * D]
        groups = [("a", n) for n in range(na // 256)] + [("v", 0), ("o", 0)]
        src = {"a": a["W_a"], "v": a["W_v"], "o": a["W_out"]}
        dst = {"a": wa, "v": wv, "o": wo}

        raw_in = [sem(f"raw_in{r}") for r in range(4)]
        (p_t, p_hi, p_lo, stat, var_ok, std, rc, ms_ok, rms, h_ok, x_ok, ht_ps, ht_hi, ht_lo, v_ok,
         v_sb, l_ps, l_ev, mx_ok, sub_ok, ex_ok, z_ok, tr, zr_ok, e0_ok, sc, yc_ok, ot_ps, ot_hi,
         ot_lo, o_ok, x_add) = map(sem, (
             "p_t", "p_hi", "p_lo", "stat", "var_ok", "std", "rc", "ms_ok", "rms", "h_ok", "x_ok", "ht_ps",
             "ht_hi", "ht_lo", "v_ok", "v_sb", "l_ps", "l_ev", "mx_ok", "sub_ok", "ex_ok", "z_ok", "tr",
             "zr_ok", "e0_ok", "sc", "yc_ok", "ot_ps", "ot_hi", "ot_lo", "o_ok", "x_add"))
        g_out = [sem("g_out0"), sem("g_out1")]
        g_in = [sem("g_in0"), sem("g_in1")]
        y_out, y_in = sem("y_out"), sem("y_in")
        block = ctx.enter_context(nc.Block())

        LAG_R, LAG_S, LAG_O = 1, 3, 4

        def iterations(eng, body):
            for it in range(LAG_O):
                body(it, it // 2, it % 2)
            with eng.Fori(LAG_O // 2, TILES // 2 - 1) as q:
                body(2 * q, q, 0)
                body(2 * q + 1, q, 1)
            for it in range(TILES - 2, TILES + LAG_O):
                body(it, it // 2, it % 2)

        def on(it, lag):
            return not isinstance(it, int) or 0 <= it - lag < TILES

        def ahead(it):
            return not isinstance(it, int) or it + 1 < TILES

        @block.sync
        def _(sp):
            for n, (what, i) in enumerate(groups):
                r = n % 4
                if n >= 4:
                    sp.wait_ge(p_t, n - 3)
                sp.dma_start(raw[r].rearrange("p (s d) -> p s d", s=2),
                             src[what][i * 256:(i + 1) * 256].rearrange("(s p) d -> p s d", p=P)).then_inc(raw_in[r], 16)

            def body(it, q, par):
                if on(it, LAG_O):
                    k = it - LAG_O
                    read_back = 16 * BATCH * it - 16 * BATCH * LAG_O
                    sp.wait_ge(yc_ok, k + 1)
                    if not (isinstance(it, int) and k == 0):
                        sp.wait_ge(y_in, read_back)
                    sp.dma_start(g.y_dram, yc).then_inc(y_out, 16)
                    sp.wait_ge(y_out, 16 * k + 16)
                    if not (isinstance(it, int) and k == 0):
                        sp.wait_ge(ot_ps, k)
                    for b in range(BATCH):
                        sp.dma_start(ho[b * STEPS:(b + 1) * STEPS].rearrange("p (h i) -> p h i", h=HEADS),
                                     g.y_dram[b * STEPS:(b + 1) * STEPS].rearrange("h (t i) -> t h i", i=M)).then_inc(y_in, 16)
                if on(it, LAG_R):
                    k, kpar = it - LAG_R, 1 - par
                    uses = q - (1 if par == 0 else 0)
                    read_back = 8 * BATCH * it - 8 * BATCH * (2 - par)
                    sp.wait_ge(zr_ok, k + 1)
                    sp.wait_ge(e0_ok, k + 1)
                    if not (isinstance(it, int) and k < 2):
                        sp.wait_ge(g_in[kpar], read_back)
                    sp.dma_start(g.g_dram[kpar], gate[kpar].rearrange("p h c -> p (h c)")).then_inc(g_out[kpar], 16)
                    sp.wait_ge(g_out[kpar], 16 * uses + 16)
                    if not (isinstance(it, int) and k < 2):
                        sp.wait_ge(sc, 3 * STEPS * (k - 1))
                    for b in range(BATCH):
                        sp.dma_start(step_g[kpar][b * STEPS:(b + 1) * STEPS],
                                     g.g_dram[kpar][b * STEPS:(b + 1) * STEPS].rearrange("t (h c) -> h t c", h=HEADS)
                                     ).then_inc(g_in[kpar], 16)

            iterations(sp, body)

        @block.tensor
        def _(pe):
            for n, (what, i) in enumerate(groups):
                pe.wait_ge(raw_in[n % 4], 16 * (n // 4 + 1))
                if n >= 6:
                    pe.wait_ge(p_lo, n - 5)
                bank = g.psum[:, n % 6]
                for k in range(KD):
                    for s in range(2):
                        last = pe.transpose(bank[:, (k * 2 + s) * P:(k * 2 + s + 1) * P],
                                            raw[n % 4][:, s * D + k * P:s * D + (k + 1) * P], g.ident)
                last.then_inc(p_t, 1)

            def h_transpose(k, par):
                pe.wait_ge(h_ok, k + 1)
                if not (isinstance(k, int) and k < 6):
                    pe.wait_ge(ot_lo, k - 5)
                for c in range(KD):
                    last = pe.transpose(tph[:, c * P:(c + 1) * P], hrow[par][:, c * P:(c + 1) * P], g.ident)
                last.then_inc(ht_ps, 1)

            def product(out, left, right):
                i = 0
                for k in range(KD):
                    for l, r in ((0, 0), (0, 1), (1, 0)):
                        last = pe.matmul(out, left[:, l, k], right[r][:, k], start=(i == 0), stop=(i == 5))
                        i += 1
                return last

            pe.wait_ge(p_lo, len(groups))
            h_transpose(0, 0)

            def body(it, q, par):
                if on(it, 0):
                    pe.wait_ge(ht_lo, it + 1)
                    if not (isinstance(it, int) and it < 5):
                        pe.wait_ge(x_add, it - 4)
                    product(v_ps, ht[par], wv).then_inc(v_ok, 1)
                    if ahead(it):
                        h_transpose(it + 1, 1 - par)
                    for j in range(HEADS // 2):
                        slot = j % 3
                        done = it * 8 + j - (1 if j < 2 else 2)
                        if not (isinstance(done, int) and done < 1):
                            pe.wait_ge(l_ev, done)
                        for s in range(2):
                            h = 2 * j + s
                            last = product(lp[slot][:, s, 0:GATE], ht[par],
                                           [x[:, :, h * GATE:(h + 1) * GATE] for x in wa])
                        last.then_inc(l_ps, 1)
                if on(it, LAG_O):
                    k = it - LAG_O
                    pe.wait_ge(y_in, 16 * BATCH * (k + 1))
                    if isinstance(it, int) and it + 1 >= TILES:
                        pe.wait_ge(ht_lo, TILES)
                    else:
                        pe.wait_ge(ht_lo, it + 2)
                    for c in range(KD):
                        last = pe.transpose(tpo[:, c * P:(c + 1) * P], ho[:, c * P:(c + 1) * P], g.ident)
                    last.then_inc(ot_ps, 1)
                    pe.wait_ge(ot_lo, k + 1)
                    if isinstance(it, int) and it >= TILES:
                        pe.wait_ge(v_sb, TILES)
                    else:
                        pe.wait_ge(v_sb, it + 1)
                    product(o_ps, ot, wo).then_inc(o_ok, 1)

            iterations(pe, body)

        @block.scalar
        def _(act):
            for n, (what, i) in enumerate(groups):
                act.wait_ge(p_t, n + 1)
                last = act.activation(dst[what][0][:, :, i * 256:(i + 1) * 256],
                                      g.psum[:, n % 6].rearrange("p (k n) -> p k n", k=KD), ACT.Copy, scale=WS)
                last.then_inc(p_hi, 1)
            act.wait_ge(var_ok, 1)
            act.activation(g.std, g.mv3[:, :, 1], ACT.Sqrt, bias=g.eps, scale=1.0).then_inc(std, 1)
            act.wait_ge(ms_ok, 1)
            act.activation(g.rms, g.ms, ACT.Sqrt, bias=g.eps, scale=1.0).then_inc(rms, 1)

            def h_high(k, par):
                act.wait_ge(ht_ps, k + 1)
                if not (isinstance(k, int) and k < 2):
                    act.wait_ge(l_ps, 8 * k - 8)
                for c in range(KD):
                    last = act.activation(ht[par][:, 0, c], tph[:, c * P:(c + 1) * P], ACT.Copy, scale=g.nw[:, c:c + 1])
                last.then_inc(ht_hi, 1)

            h_high(0, 0)

            def body(it, q, par):
                if on(it, LAG_O):
                    k = it - LAG_O
                    act.wait_ge(sc, 3 * STEPS * (k + 1))
                    if not (isinstance(it, int) and k == 0):
                        act.wait_ge(y_out, 16 * k)
                    act.activation(yc.rearrange("p (t i) -> p t i", i=M), state[par][:, :, 1:], ACT.Copy).then_inc(yc_ok, 1)
                if on(it, 0):
                    act.wait_ge(v_ok, it + 1)
                    if not (isinstance(it, int) and it < 2):
                        act.wait_ge(e0_ok, it - 1)
                    act.activation(vs[par], v_ps, ACT.Copy, scale=1.0 / WS).then_inc(v_sb, 1)
                    if ahead(it):
                        h_high(it + 1, 1 - par)
                    if not (isinstance(it, int) and it < 2):
                        act.wait_ge(g_out[par], 16 * q)
                    for j in range(HEADS // 2):
                        act.wait_ge(l_ps, it * 8 + j + 1)
                        slot = j % 3
                        act.activation(gate[par][:, 2 * j:2 * j + 2, 0:GATE], lp[slot][:, :, 0:GATE],
                                       ACT.Copy, scale=1.0 / WS).then_inc(l_ev, 1)
                if on(it, LAG_O):
                    k = it - LAG_O
                    act.wait_ge(ot_ps, k + 1)
                    if not (isinstance(it, int) and k == 0):
                        act.wait_ge(o_ok, k)
                    act.activation(ot[:, 0].rearrange("p k t -> p (k t)"), tpo, ACT.Copy).then_inc(ot_hi, 1)
                if on(it, 0):
                    for j in range(4):
                        act.wait_ge(sub_ok, it * 4 + j + 1)
                        e = gate[par][:, 4 * j:4 * j + 4, 0:GATE]
                        act.activation(e, e, ACT.Exp).then_inc(ex_ok, 1)

            iterations(act, body)

        @block.gpsimd
        def _(pool):
            def body(it, q, par):
                if on(it, LAG_R):
                    k = it - LAG_R
                    gv = gate[1 - par][:, :, 0:GATE].rearrange("p h (i j) -> p h i j", j=M + 1)
                    for j in range(4):
                        pool.wait_ge(ex_ok, k * 4 + j + 1)
                        e = gv[:, 4 * j:4 * j + 4]
                        c = (k * 4 + j) * 4
                        t4 = tree.rearrange("p (h i) c -> p h i c", h=4)
                        pool.tensor_tensor(t4, e[:, :, :, 1:9], e[:, :, :, 9:17], ALU.add).then_inc(tr, 1)
                        for n, wd in enumerate((4, 2, 1)):
                            pool.wait_ge(tr, c + n + 1)
                            pool.tensor_tensor(tree[:, :, 0:wd], tree[:, :, 0:wd], tree[:, :, wd:2 * wd], ALU.add).then_inc(tr, 1)
                        pool.wait_ge(tr, c + 4)
                        if j == 0 and not (isinstance(it, int) and k == 0):
                            pool.wait_ge(zr_ok, k)
                        pool.tensor_tensor(zsum[:, 64 * j:64 * j + 64].rearrange("p (h i) -> p h i", h=4),
                                           t4[:, :, :, 0], e[:, :, :, 0], ALU.add).then_inc(z_ok, 1)
                        pool.wait_ge(z_ok, k * 4 + j + 1)
                if on(it, 0):
                    gv = gate[par][:, :, 0:GATE].rearrange("p h (i j) -> p h i j", j=M + 1)
                    for j in range(4):
                        pool.wait_ge(mx_ok, it * 8 + 2 * j + 2)
                        e = gv[:, 4 * j:4 * j + 4]
                        m = mx[par][:, 64 * j:64 * j + 64].rearrange("p (h i) -> p h i", h=4)
                        pool.tensor_tensor(e, e, m.unsqueeze(3).broadcast_to((P, 4, M, M + 1)), ALU.subtract).then_inc(sub_ok, 1)

            iterations(pool, body)

        @block.vector
        def _(dve):
            for r in range(2):
                dve.memset(state[r], 1.0).then_inc(rc, 1)
            dve.wait_ge(rc, 2)
            dve.memset(state[1][:, STEPS - 1, 1:], 0.0).then_inc(rc, 1)
            token_statistics(nc, g, dve, stat)
            dve.wait_ge(stat, TILES + 1)
            dve.engine_nop().then_inc(var_ok, 1)
            for n, (what, i) in enumerate(groups):
                dve.wait_ge(p_hi, n + 1)
                dve.scalar_tensor_tensor(out=dst[what][1][:, :, i * 256:(i + 1) * 256],
                                         in0=g.psum[:, n % 6].rearrange("p (k n) -> p k n", k=KD), scalar=WS,
                                         in1=dst[what][0][:, :, i * 256:(i + 1) * 256],
                                         op0=ALU.mult, op1=ALU.subtract).then_inc(p_lo, 1)
            chain = [3]

            def then(ins):
                ins.then_inc(rc, 1)
                chain[0] += 1
                dve.wait_ge(rc, chain[0])

            dve.wait_ge(std, 1)
            then(dve.reciprocal(g.rstd, g.std))
            then(dve.tensor_tensor(g.ms, g.rstd, g.rstd, ALU.mult))
            then(dve.tensor_tensor(g.ms, g.ms, g.mv3[:, :, 1], ALU.mult))
            dve.engine_nop().then_inc(ms_ok, 1)
            dve.wait_ge(rms, 1)
            then(dve.reciprocal(g.rms, g.rms))
            then(dve.tensor_tensor(g.hs, g.rms, g.rstd, ALU.mult))
            then(dve.tensor_scalar(g.xa, g.rstd, 1.0, None, ALU.add))
            then(dve.scalar_tensor_tensor(out=g.xb, in0=g.mv3[:, :, 0], scalar=-1.0, in1=g.rstd, op0=ALU.mult, op1=ALU.mult))

            def h_row(k, par):
                if not (isinstance(k, int) and k < 2):
                    dve.wait_ge(ht_ps, k - 1)
                dve.tensor_scalar(hrow[par], g.x2[:, bass.ds(k * D, D)], g.mv[:, bass.ds(2 * k, 1)],
                                  g.hs[:, bass.ds(k, 1)], ALU.subtract, ALU.mult).then_inc(h_ok, 1)

            def x_self(k):
                dve.wait_ge(h_ok, k + 1)
                xs = g.x2[:, bass.ds(k * D, D)]
                dve.tensor_scalar(xs, xs, g.xa[:, bass.ds(k, 1)], g.xb[:, bass.ds(k, 1)], ALU.mult, ALU.add).then_inc(x_ok, 1)

            def h_low(k, par):
                dve.wait_ge(ht_hi, k + 1)
                for c in range(KD):
                    last = dve.scalar_tensor_tensor(out=ht[par][:, 1, c], in0=tph[:, c * P:(c + 1) * P], scalar=g.nw[:, c:c + 1],
                                                    in1=ht[par][:, 0, c], op0=ALU.mult, op1=ALU.subtract)
                last.then_inc(ht_lo, 1)

            for k in range(2):
                h_row(k, k)
                x_self(k)
            h_low(0, 0)

            def body(it, q, par):
                fill = {}

                def row_next():
                    h_row(it + 2, par)

                def self_next():
                    x_self(it + 2)

                def low_next():
                    h_low(it + 1, 1 - par)

                def maximum(j):
                    dve.wait_ge(l_ev, it * 8 + j + 1)
                    if j == 0 and not (isinstance(it, int) and it < 2):
                        dve.wait_ge(sub_ok, 4 * it - 4)
                    dve.tensor_reduce(mx[par][:, 32 * j:32 * j + 32].rearrange("p (h i) -> p h i", h=2),
                                      gate[par][:, 2 * j:2 * j + 2, 0:GATE].rearrange("p h (i j) -> p h i j", j=M + 1),
                                      AX.X, ALU.max).then_inc(mx_ok, 1)

                def invert():
                    k = it - LAG_R
                    dve.wait_ge(z_ok, 4 * k + 4)
                    dve.reciprocal(gate[1 - par][:, :, GATE:ROW], zsum.rearrange("p (h i) -> p h i", h=HEADS)).then_inc(zr_ok, 1)

                def times_v():
                    k = it - LAG_R
                    dve.wait_ge(v_sb, k + 1)
                    e0 = gate[1 - par][:, :, 0:GATE:M + 1]
                    dve.tensor_tensor(e0, e0, vs[1 - par].rearrange("p (h i) -> p h i", h=HEADS), ALU.mult).then_inc(e0_ok, 1)

                def out_low():
                    k = it - LAG_O
                    dve.wait_ge(ot_hi, k + 1)
                    dve.tensor_tensor(ot[:, 1].rearrange("p k t -> p (k t)"), tpo, ot[:, 0].rearrange("p k t -> p (k t)"),
                                      ALU.subtract).then_inc(ot_lo, 1)

                def add_out():
                    k = it - LAG_O
                    dve.wait_ge(o_ok, k + 1)
                    dve.wait_ge(x_ok, k + 1)
                    xs = g.x2[:, bass.ds(k * D, D)]
                    dve.scalar_tensor_tensor(out=xs, in0=o_ps, scalar=1.0 / WS, in1=xs, op0=ALU.mult, op1=ALU.add).then_inc(x_add, 1)

                if ahead(it):
                    fill[2] = low_next
                if not isinstance(it, int) or it + 2 < TILES:
                    fill[0], fill[1] = row_next, self_next
                if on(it, 0):
                    for j in range(8):
                        fill[3 + j] = (lambda j: lambda: maximum(j))(j)
                if on(it, LAG_R):
                    fill[11], fill[12] = invert, times_v
                if on(it, LAG_O):
                    fill[13], fill[15] = out_low, add_out
                scan = on(it, LAG_S)
                k = it - LAG_S
                sg, st, before = step_g[1 - par], state[1 - par], state[par]
                if scan:
                    uses = q - (2 if par == 0 else 1)
                    dve.wait_ge(g_in[1 - par], 16 * BATCH * (uses + 1))
                    if not (isinstance(it, int) and k < 2):
                        dve.wait_ge(yc_ok, k - 1)
                for t in range(STEPS):
                    c = 3 * STEPS * k + 3 * t
                    if scan:
                        prev = st[:, t - 1] if t else before[:, STEPS - 1]
                        if not (isinstance(c, int) and c == 0):
                            dve.wait_ge(sc, c)
                        dve.tensor_tensor(prod, sg[:, t, 0:GATE].rearrange("p (i j) -> p i j", j=M + 1),
                                          prev.unsqueeze(1).broadcast_to((P, M, M + 1)), ALU.mult).then_inc(sc, 1)
                    if t in fill:
                        fill[t]()
                    if scan:
                        dve.wait_ge(sc, c + 1)
                        dve.tensor_reduce(dots, prod, AX.X, ALU.add).then_inc(sc, 1)
                        dve.wait_ge(sc, c + 2)
                        dve.tensor_tensor(st[:, t, 1:], dots, sg[:, t, GATE:ROW], ALU.mult).then_inc(sc, 1)

            iterations(dve, body)


def store_output(nc, g, out):
    with nc.semaphore("stored") as stored, nc.Block() as block:
        @block.sync
        def _(sp):
            for b in range(BATCH):
                sp.dma_start(out[b].rearrange("(n t) d -> t n d", t=STEPS), g.x[b * STEPS:(b + 1) * STEPS]).then_inc(stored, 16)
            sp.wait_ge(stored, 16 * BATCH)


def build(nc, a, out):
    g = Core()
    with ExitStack() as ctx:
        def sb(name, shape, dt):
            return ctx.enter_context(nc.sbuf_tensor(name, shape, dt))[:]

        g.x2 = sb("x_tokens", [P, TILES * D], F32)
        g.x = g.x2.rearrange("p (n d) -> p n d", d=D)
        g.wf = sb("expert_weights", [P, (NE + 1) * WEXP], F16)
        late_words = 2 * KD * HEADS * GATE // 2 + 2 * KD * D
        g.late = sb("gate_weights", [P, late_words], F32)
        g.xn = g.late[:, 0:TILES * D]
        g.work_words = 6144
        g.work = sb("work", [P, g.work_words], F32)
        g.ident = sb("identity", [P, P], F32)
        g.ones = sb("ones", [P, P], F16)
        g.before = sb("before", [P, P], F16)
        g.rw_raw = sb("router_raw", [P, KD, NE], F32)
        g.rw = sb("router_weights", [P, 2, KD, NE], F16)
        g.nw = sb("norm_weights", [P, KD], F32)
        g.bias = sb("router_bias", [P, NE], F32)
        g.eps = sb("eps", [P, 1], F32)
        g.iota_i = g.work[:, 1024:1024 + NE + SHARED + SPARSE].bitcast(I32)
        g.iota = sb("iota", [P, NE + SHARED + SPARSE], F32)
        g.stats = sb("stats", [P, TILES * 6], F32)
        g.mv = sb("mean_var", [P, TILES * 2], F32)
        g.mv3 = g.mv.rearrange("p (t c) -> p t c", c=2)
        g.std, g.rstd, g.rms, g.ms, g.hs, g.xa, g.xb = (sb(n, [P, TILES], F32) for n in (
            "std", "rstd", "rms", "ms", "hs", "xa", "xb"))
        g.cw = sb("expert_shares", [P, 2 * TILES], F32)
        g.slot = sb("slots_of_tokens", [P, 2 * TILES], U32)
        g.texp = sb("experts_of_tiles", [P, SPARSE], I32)
        g.psum = ctx.enter_context(nc.psum_tensor("psum", [P, 8, 512], F32))[:]
        rows = SPARSE * ITEM
        g.slots = nc.dram_tensor("slot_rows", (rows, D), F32, kind="Internal").ap()
        g.outs = nc.dram_tensor("slot_outputs", (rows, D), F32, kind="Internal").ap()
        g.w_dram = nc.dram_tensor("split_weights", (P, (NE - KEPT) * WEXP), F16, kind="Internal").ap()
        gd = [nc.dram_tensor(f"gates{r}", (P, HEADS * ROW), F32, kind="Internal").ap() for r in range(2)]
        g.g_dram = gd
        g.y_dram = nc.dram_tensor("head_outputs", (P, STEPS * M), F32, kind="Internal").ap()
        load_inputs(nc, g, a)
        ffn(nc, g, "f1", False)
        attention(nc, g, a)
        ffn(nc, g, "f2", True)
        store_output(nc, g, out)


_INS = {"L0_attn_x": "x", "L0_attn_norm_w": "norm_w", "L0_attn_W_v": "W_v", "L0_attn_W_a": "W_a",
        "L0_attn_W_out": "W_out", "L0_ffn_router_w": "router_w", "L0_ffn_experts_bias": "bias",
        "L0_ffn_w1": "w1", "L0_ffn_w3": "w3", "L0_ffn_w2": "w2", "L0_ffn_sw1": "sw1", "L0_ffn_sw3": "sw3",
        "L0_ffn_sw2": "sw2"}


def kernel(**inputs):
    import numpy as np
    import concourse.bacc as bacc
    from concourse.bass_utils import run_bass_kernel_spmd

    nc = bacc.Bacc("TRN2", target_bir_lowering=False, num_devices=1)
    arrays, aps = {}, {}
    for name, short in _INS.items():
        arr = np.ascontiguousarray(inputs[name])
        arrays[f"in_{short}"] = arr
        aps[short] = nc.dram_tensor(f"in_{short}", arr.shape, mybir.dt.from_np(arr.dtype), kind="ExternalInput").ap()
    out = nc.dram_tensor("out", (BATCH, TIME, D), F32, kind="ExternalOutput").ap()
    build(nc, aps, out)
    r = run_bass_kernel_spmd(nc, [arrays], core_ids=[0])
    return np.asarray(r.results[0]["out"])
```

```python
from contextlib import ExitStack

import concourse.bass as bass
from concourse import mybir

F32 = mybir.dt.float32
F16 = mybir.dt.float16
I32 = mybir.dt.int32
U32 = mybir.dt.uint32
ALU = mybir.AluOpType
ACT = mybir.ActivationFunctionType
AX = mybir.AxisListType

P = 128
BATCH, TIME, D = 8, 512, 256
STEPS = P // BATCH
TILES = TIME // STEPS
KD = D // P
HID = 512
HC = HID // P
NE = 8
ITEM = 256
SHARED = BATCH * TIME // ITEM
SPARSE = 2 * BATCH * TIME // ITEM + NE - 1
HEADS, M = 16, 16
GATE = M * (M + 1)
ROW = GATE + M
WS = 64.0
AS = 4.0
EPS = 1e-5
WEXP = 2 * (2 * KD * HID + HC * D)
O1H, O1L = 0, KD * HID
O3H, O3L = 2 * KD * HID, 3 * KD * HID
O2H, O2L = 4 * KD * HID, 4 * KD * HID + HC * D
KEPT = 2


class Core:
    pass


def load_inputs(nc, g, a):
    with ExitStack() as ctx:
        sem = lambda n: ctx.enter_context(nc.semaphore(n))
        x_in, small_in, iotas, tri, ident_z, consts, zero_ready = map(sem, (
            "x_in", "small_in", "iotas", "tri", "ident_z", "consts", "zero_ready"))
        raw_in = [sem("raw_in0"), sem("raw_in1")]
        w_hi, w_lo, w_kept, slots_zeroed = map(sem, ("w_hi", "w_lo", "w_kept", "slots_zeroed"))
        raw = [g.late[:, r * 3072:(r + 1) * 3072] for r in range(2)]
        order = [NE] + list(range(NE))
        block = ctx.enter_context(nc.Block())

        @block.sync
        def _(sp):
            for n, e in enumerate(order):
                r = raw[n % 2]
                w1, w3, w2 = (a["sw1"][0], a["sw3"][0], a["sw2"][0]) if e == NE else (
                    a["w1"][e], a["w3"][e], a["w2"][e])
                if n >= 2:
                    sp.wait_ge(w_hi, n - 1)
                    sp.wait_ge(w_lo, n - 1)
                c = KD * HID
                sp.dma_start(r[:, 0:c].rearrange("p (k n) -> p k n", k=KD),
                             w1.rearrange("(k p) n -> p k n", p=P)).then_inc(raw_in[n % 2], 16)
                sp.dma_start(r[:, c:2 * c].rearrange("p (k n) -> p k n", k=KD),
                             w3.rearrange("(k p) n -> p k n", p=P)).then_inc(raw_in[n % 2], 16)
                sp.dma_start(r[:, 2 * c:2 * c + HC * D].rearrange("p (k n) -> p k n", k=HC),
                             w2.rearrange("(k p) n -> p k n", p=P)).then_inc(raw_in[n % 2], 16)
            sp.wait_ge(w_hi, len(order))
            sp.wait_ge(w_lo, len(order))
            sp.dma_start(g.w_dram, g.wf[:, KEPT * WEXP:NE * WEXP]).then_inc(w_kept, 16)
            sp.wait_ge(w_kept, 16)

        @block.gpsimd
        def _(pool):
            for b in range(BATCH):
                pool.dma_start(g.x[b * STEPS:(b + 1) * STEPS],
                               a["x"][b].rearrange("(n t) d -> t n d", t=STEPS)).then_inc(x_in, 16)
            with nc.allow_non_contiguous_dma(reason="2304 words, once"):
                for k in range(KD):
                    pool.dma_start(g.rw_raw[:, k],
                                   a["router_w"][:, k * P:(k + 1) * P].rearrange("e p -> p e")).then_inc(small_in, 16)
                pool.dma_start(g.nw, a["norm_w"].rearrange("(k p) -> p k", p=P)).then_inc(small_in, 16)
            pool.dma_start(g.bias, a["bias"].partition_broadcast(P)).then_inc(small_in, 16)
            pool.memset(g.ident, 0.0).then_inc(ident_z, 1)
            pool.memset(g.ones, 1.0).then_inc(ident_z, 1)
            pool.memset(g.before, 1.0).then_inc(ident_z, 1)
            pool.memset(g.work[:, 0:2 * D], 0.0).then_inc(zero_ready, 1)
            pool.memset(g.eps, EPS).then_inc(tri, 1)
            pool.iota(g.iota_i[:, 0:NE], pattern=[[1, NE]], base=0, channel_multiplier=0).then_inc(iotas, 1)
            pool.iota(g.iota_i[:, NE:NE + SHARED], pattern=[[ITEM, SHARED]], base=0, channel_multiplier=0).then_inc(iotas, 1)
            pool.iota(g.iota_i[:, NE + SHARED:], pattern=[[1, SPARSE]], base=0, channel_multiplier=0).then_inc(iotas, 1)
            pool.wait_ge(ident_z, 3)
            pool.affine_select(out=g.ident, in_=g.ident, compare_op=ALU.not_equal, fill=1.0, base=0,
                               pattern=[[-1, P]], channel_multiplier=1).then_inc(tri, 1)
            pool.affine_select(out=g.before, in_=g.before, compare_op=ALU.is_gt, fill=0.0, base=0,
                               pattern=[[1, P]], channel_multiplier=-1).then_inc(tri, 1)
            pool.wait_ge(zero_ready, 1)
            for n in range(SPARSE):
                pool.dma_start(g.slots[n * ITEM:(n + 1) * ITEM].rearrange("(s p) d -> p s d", p=P),
                               g.work[:, 0:2 * D].rearrange("p (s d) -> p s d", s=2)).then_inc(slots_zeroed, 16)
            pool.wait_ge(slots_zeroed, 16 * SPARSE)
            pool.wait_ge(x_in, 16 * BATCH)
            pool.wait_ge(tri, 3)

        @block.scalar
        def _(act):
            act.wait_ge(small_in, 16 * (KD + 2))
            act.activation(g.rw[:, 0], g.rw_raw, ACT.Copy, scale=WS).then_inc(consts, 1)
            for n, e in enumerate(order):
                act.wait_ge(raw_in[n % 2], 48 * (n // 2 + 1))
                for o_hi, o_raw in ((O1H, 0), (O3H, KD * HID), (O2H, 2 * KD * HID)):
                    last = act.activation(g.wf[:, e * WEXP + o_hi:e * WEXP + o_hi + KD * HID],
                                          raw[n % 2][:, o_raw:o_raw + KD * HID], ACT.Copy, scale=WS)
                last.then_inc(w_hi, 1)

        @block.vector
        def _(dve):
            dve.wait_ge(consts, 1)
            dve.scalar_tensor_tensor(out=g.rw[:, 1], in0=g.rw_raw, scalar=WS, in1=g.rw[:, 0],
                                     op0=ALU.mult, op1=ALU.subtract)
            dve.wait_ge(iotas, 3)
            dve.tensor_copy(g.iota, g.iota_i)
            dve.tensor_scalar(g.nws, g.nw, WS, None, ALU.mult)
            for n, e in enumerate(order):
                dve.wait_ge(w_hi, n + 1)
                for o_hi, o_lo, o_raw in ((O1H, O1L, 0), (O3H, O3L, KD * HID), (O2H, O2L, 2 * KD * HID)):
                    w = e * WEXP
                    last = dve.scalar_tensor_tensor(
                        out=g.wf[:, w + o_lo:w + o_lo + KD * HID], in0=raw[n % 2][:, o_raw:o_raw + KD * HID],
                        scalar=WS, in1=g.wf[:, w + o_hi:w + o_hi + KD * HID], op0=ALU.mult, op1=ALU.subtract)
                last.then_inc(w_lo, 1)


def token_statistics(nc, g, dve, stat):
    with dve.Fori(0, TILES) as t:
        dve.bn_stats(g.stats[:, bass.ds(t * 6, 6)], g.x2[:, bass.ds(t * D, D)]).then_inc(stat, 1)
    dve.wait_ge(stat, TILES)
    for t in range(TILES):
        last = dve.bn_aggr(g.mv3[:, t], g.stats[:, t * 6:(t + 1) * 6])
    last.then_inc(stat, 1)


def refined_rsqrt(dve, out, root, value, eps, tmp, then):
    then(dve.reciprocal(out, root))
    then(dve.tensor_tensor(tmp, out, out, ALU.mult))
    then(dve.scalar_tensor_tensor(out=tmp, in0=value, scalar=eps, in1=tmp, op0=ALU.add, op1=ALU.mult))
    then(dve.tensor_scalar(tmp, tmp, -0.5, 1.5, ALU.mult, ALU.add))
    then(dve.tensor_tensor(out, out, tmp, ALU.mult))


def ffn(nc, g, tag, reload):
    with ExitStack() as ctx:
        def sem(n):
            return ctx.enter_context(nc.semaphore(f"{tag}_{n}"))

        w = g.work
        rows = [w[:, r * 512:(r + 1) * 512] for r in range(2)]
        xt = [w[:, 1024 + r * 512:1536 + r * 512].bitcast(F16).rearrange("p (l k t) -> p l k t", l=2, k=KD) for r in range(2)]
        th = [w[:, 2048 + r * 512:2560 + r * 512] for r in range(2)]
        hid = [w[:, 3072 + r * 512:3584 + r * 512] for r in range(2)]
        hb = [w[:, 4096 + r * 512:4608 + r * 512].bitcast(F16).rearrange("p (l c t) -> p l c t", l=2, c=2) for r in range(4)]
        yst = [g.late[:, 8192 + r * 512:8704 + r * 512] for r in range(2)]
        gat = [g.late[:, 8192 + r * 256:8448 + r * 256] for r in range(4)]
        at = [3072]

        def temp(n):
            at[0] += n
            assert at[0] <= 6144
            return w[:, at[0] - n:at[0]]

        logit, best, oh0, oh1 = temp(256), temp(256), temp(256), temp(256)
        besti = temp(256).bitcast(U32)
        chosen = temp(64)
        member = temp(128).bitcast(F16)
        cum, slot_of, prod = temp(256), temp(256), temp(256)
        fills = temp(NE * SHARED)
        ntile, tend, count = temp(NE), temp(NE), temp(NE)
        passed = temp(SPARSE * NE)
        slot_f, ediff = temp(64), temp(32)
        logit3, best3, besti3 = (v.rearrange("p (t e) -> p t e", e=NE) for v in (logit, best, besti))
        chosen3 = chosen.rearrange("p (k t) -> p k t", k=2)

        gp, up_, yp = (g.psum[:, 0:2], g.psum[:, 2:4], g.psum[:, 4:6])
        tp, rp = g.psum[:, 6], g.psum[:, 7]
        router_ps = rp[:, 0:256]

        (stat, var_ok, std, r_rows, r_t, r_hi, r_lo, r_mm, xn_copied, logits_ok, rt, diff_ok, e_ok,
         member_ok, rank_ok, slots_ok, scattered, rows_sh, t_done, x_hi, x_lo, up_done, tanh_ok,
         s_ok, hid_ok, h_hi, h_lo, dn_done, y_sh, y_sp, gathered, added, texp_ok, w_back) = map(sem, (
             "stat", "var_ok", "std", "r_rows", "r_t", "r_hi", "r_lo", "r_mm", "xn_copied", "logits_ok",
             "rt", "diff_ok", "e_ok", "member_ok", "rank_ok", "slots_ok", "scattered", "rows_sh", "t_done",
             "x_hi", "x_lo", "up_done", "tanh_ok", "s_ok", "hid_ok", "h_hi", "h_lo", "dn_done", "y_sh",
             "y_sp", "gathered", "added", "texp_ok", "w_back"))
        rows_sp = [sem("rows_sp0"), sem("rows_sp1")]
        y_out = [sem("y_out0"), sem("y_out1")]
        gat_in = [sem(f"gat_in{r}") for r in range(4)]
        block = ctx.enter_context(nc.Block())

        @block.tensor
        def _(pe):
            def transposes(par, done):
                for k in range(KD):
                    for s in range(2):
                        c = (k * 2 + s) * P
                        last = pe.transpose(tp[:, c:c + P], rows[par][:, s * D + k * P:s * D + (k + 1) * P], g.ident)
                last.then_inc(done, 1)

            def router(n, par):
                pe.wait_ge(r_rows, n + 1)
                transposes_wait = n
                pe.wait_ge(r_lo, transposes_wait)
                transposes(par, r_t)
                pe.wait_ge(r_lo, n + 1)
                for s in range(2):
                    col = n * 2 * NE + s * NE
                    i = 0
                    for k in range(KD):
                        for lx, lw in ((0, 0), (0, 1), (1, 0)):
                            last = pe.matmul(router_ps[:, bass.ds(col, NE)], xt[par][:, lx, k, s * P:(s + 1) * P],
                                             g.rw[:, lw, k], start=(i == 0), stop=(i == 5))
                            i += 1
                last.then_inc(r_mm, 1)

            with pe.Fori(0, SHARED // 2) as q:
                router(2 * q, 0)
                router(2 * q + 1, 1)

            pe.wait_ge(member_ok, 1)
            pe.matmul(rp[:, 0:256], g.before, member, start=True, stop=True)
            pe.matmul(rp[:, 256:512], g.ones, member, start=True, stop=True).then_inc(rank_ok, 1)

            def first_rows(gi, par):
                pe.wait_ge(rows_sh, gi + 1)
                if not (isinstance(gi, int) and gi == 0):
                    pe.wait_ge(x_lo, gi)
                transposes(par, t_done)

            def sparse_rows(gi, half, par):
                pe.wait_ge(rows_sp[par], 16 * (half - SHARED // 2) + 16)
                pe.wait_ge(x_lo, gi)
                transposes(par, t_done)

            def up(gi, par, h, wbase):
                m = 2 * gi + h
                if h == 0:
                    pe.wait_ge(x_lo, gi + 1)
                if not (isinstance(gi, int) and gi == 0):
                    pe.wait_ge(hid_ok, m - 1)
                for ps, o_hi, o_lo in ((gp, O1H, O1L), (up_, O3H, O3L)):
                    for c in range(2):
                        i = 0
                        for k in range(KD):
                            for lx, o in ((0, o_hi), (0, o_lo), (1, o_hi)):
                                off = o + k * HID + (2 * h + c) * P
                                last = pe.matmul(ps[:, h, c * ITEM:(c + 1) * ITEM], g.wf[:, bass.ds(wbase + off, P)],
                                                 xt[par][:, lx, k], start=(i == 0), stop=(i == 5))
                                i += 1
                last.then_inc(up_done, 1)

            def down(gi, par, h, wbase):
                m = 2 * gi + h
                pe.wait_ge(h_lo, m + 1)
                i = 0
                for c in range(2):
                    for lh, o in ((0, O2H), (0, O2L), (1, O2H)):
                        for s in range(2):
                            off = o + (2 * h + c) * D
                            last = pe.matmul(yp[:, par, s * D:(s + 1) * D],
                                             hb[2 * par + h][:, lh, c, s * P:(s + 1) * P],
                                             g.wf[:, bass.ds(wbase + off, D)],
                                             start=(h == 0 and i == 0), stop=(h == 1 and c == 1 and lh == 1),
                                             skip_group_check=True)
                            i += 1
                last.then_inc(dn_done, 1)

            def item(gi, par, wu, wd, rows_next, y_free):
                up(gi, par, 0, wu)
                rows_next()
                if wd is not None:
                    y_free()
                    down(gi - 1, 1 - par, 0, wd)
                up(gi, par, 1, wu)
                if wd is not None:
                    down(gi - 1, 1 - par, 1, wd)

            ws = NE * WEXP
            nothing = lambda: None
            first_rows(0, 0)
            item(0, 0, ws, None, lambda: first_rows(1, 1), nothing)
            item(1, 1, ws, ws, lambda: first_rows(2, 0), nothing)
            item(2, 0, ws, ws, lambda: first_rows(3, 1), nothing)
            with pe.Fori(0, (SHARED - 4) // 2) as q:
                a, b = 2 * q + 3, 2 * q + 4
                item(a, 1, ws, ws, lambda: first_rows(a + 1, 0), lambda: pe.wait_ge(y_sh, a - 2))
                item(b, 0, ws, ws, lambda: first_rows(b + 1, 1), lambda: pe.wait_ge(y_sh, b - 2))
            gi = SHARED - 1
            item(gi, 1, ws, ws, lambda: sparse_rows(SHARED, SHARED // 2, 0), lambda: pe.wait_ge(y_sh, gi - 2))

            reg = [pe.alloc_register(f"{tag}_expert{r}") for r in range(2)]

            def load_expert(n, par):
                pe.reg_load(reg[par], g.texp[0:1, bass.ds(n, 1)])

            def expert(par):
                return pe.snap(reg[par], min_val=0, max_val=NE - 1) * WEXP

            pe.wait_ge(texp_ok, 1)
            if reload:
                pe.wait_ge(w_back, 16)
            load_expert(0, 0)
            before = ws
            for n in range(3):
                gi, par = SHARED + n, n % 2
                cur = expert(par)

                def ahead():
                    sparse_rows(gi + 1, (gi + 1) // 2, 1 - par)
                    load_expert(n + 1, 1 - par)

                item(gi, par, cur, before, ahead, lambda: pe.wait_ge(y_sh, gi - 2))
                before = cur
            with pe.Fori(0, (SPARSE - 5) // 2) as q:
                n = 2 * q + 3
                gi = SHARED + n
                before, cur = expert(0), expert(1)

                def ahead_of_even():
                    sparse_rows(gi + 1, q + SHARED // 2 + 2, 0)
                    load_expert(n + 1, 0)

                def ahead_of_odd():
                    sparse_rows(gi + 2, q + SHARED // 2 + 2, 1)
                    load_expert(n + 2, 1)

                item(gi, 1, cur, before, ahead_of_even, lambda: pe.wait_ge(y_sp, n - 2))
                item(gi + 1, 0, expert(0), cur, ahead_of_odd, lambda: pe.wait_ge(y_sp, n - 1))
            n, gi = SPARSE - 2, SHARED + SPARSE - 2
            before, cur = expert(0), expert(1)

            def ahead_of_last():
                sparse_rows(gi + 1, (gi + 1) // 2, 0)
                load_expert(n + 1, 0)

            item(gi, 1, cur, before, ahead_of_last, lambda: pe.wait_ge(y_sp, n - 2))
            last_e = expert(0)
            item(gi + 1, 0, last_e, cur, nothing, lambda: pe.wait_ge(y_sp, n - 1))
            pe.wait_ge(y_sp, n)
            down(gi + 1, 0, 0, last_e)
            down(gi + 1, 0, 1, last_e)

        @block.scalar
        def _(act):
            act.wait_ge(var_ok, 1)
            act.activation(g.std, g.mv3[:, :, 1], ACT.Sqrt, bias=g.eps, scale=1.0).then_inc(std, 1)

            def router(n, par):
                act.wait_ge(r_t, n + 1)
                if not (isinstance(n, int) and n < 2):
                    act.wait_ge(r_mm, n - 1)
                act.activation(xt[par][:, 0].rearrange("p k t -> p (k t)"), tp, ACT.Copy).then_inc(r_hi, 1)

            router(0, 0)
            router(1, 1)
            with act.Fori(1, SHARED // 2) as q:
                router(2 * q, 0)
                router(2 * q + 1, 1)
            act.wait_ge(diff_ok, 1)
            act.activation(ediff, ediff, ACT.Exp).then_inc(e_ok, 1)

            def x_high(gi, par, last_up):
                act.wait_ge(t_done, gi + 1)
                if last_up is not None:
                    act.wait_ge(up_done, last_up)
                act.activation(xt[par][:, 0].rearrange("p k t -> p (k t)"), tp, ACT.Copy).then_inc(x_hi, 1)

            def half(gi, par, h):
                m = 2 * gi + h
                act.wait_ge(up_done, m + 1)
                if not (isinstance(gi, int) and gi == 0):
                    act.wait_ge(hid_ok, m - 1)
                act.activation(th[h], gp[:, h], ACT.Tanh, scale=0.5 / WS).then_inc(tanh_ok, 1)

            def hid_high(gi, par, h):
                m = 2 * gi + h
                act.wait_ge(hid_ok, m + 1)
                if not (isinstance(gi, int) and gi < 2):
                    act.wait_ge(dn_done, m - 3)
                act.activation(hb[2 * par + h][:, 0].rearrange("p c t -> p (c t)"), hid[h], ACT.Copy).then_inc(h_hi, 1)

            def item(gi, par, nxt, y_copy):
                half(gi, par, 0)
                if nxt:
                    x_high(gi + 1, 1 - par, None if isinstance(gi, int) and gi == 0 else 2 * gi)
                hid_high(gi, par, 0)
                half(gi, par, 1)
                hid_high(gi, par, 1)
                y_copy()

            def y_stage(gi, par, n, first):
                act.wait_ge(dn_done, 2 * gi + 2)
                if not first:
                    act.wait_ge(y_out[par], first_free(n))
                act.activation(yst[par], yp[:, par], ACT.Copy).then_inc(y_sp, 1)

            def first_free(nh):
                return 16 * nh

            nothing = lambda: None
            x_high(0, 0, None)
            item(0, 0, True, nothing)
            item(1, 1, True, nothing)
            item(2, 0, True, nothing)
            with act.Fori(0, (SHARED - 4) // 2) as q:
                item(2 * q + 3, 1, True, nothing)
                item(2 * q + 4, 0, True, nothing)
            item(SHARED - 1, 1, True, nothing)
            gi = SHARED
            item(gi, 0, True, nothing)
            item(gi + 1, 1, True, lambda: y_stage(gi, 0, 0, True))
            item(gi + 2, 0, True, lambda: y_stage(gi + 1, 1, 0, True))
            with act.Fori(0, (SPARSE - 5) // 2) as q:
                b = SHARED + 2 * q + 3
                item(b, 1, True, lambda: y_stage(b - 1, 0, q + 1, False))
                item(b + 1, 0, True, lambda: y_stage(b, 1, q + 1, False))
            gi = SHARED + SPARSE - 2
            item(gi, 1, True, lambda: y_stage(gi - 1, 0, SPARSE // 2 - 1, False))
            item(gi + 1, 0, False, lambda: y_stage(gi, 1, SPARSE // 2 - 1, False))
            y_stage(SHARED + SPARSE - 1, 0, SPARSE // 2, False)

        @block.vector
        def _(dve):
            token_statistics(nc, g, dve, stat)
            dve.wait_ge(stat, TILES + 1)
            dve.engine_nop().then_inc(var_ok, 1)
            chain = [0]

            def then(ins):
                ins.then_inc(rt, 1)
                chain[0] += 1
                dve.wait_ge(rt, chain[0])

            dve.wait_ge(std, 1)
            refined_rsqrt(dve, g.rstd, g.std, g.mv3[:, :, 1], EPS, g.ms, then)

            def normalise(par, n, done):
                for s in range(2):
                    t = 2 * n + s
                    last = dve.tensor_scalar(rows[par][:, s * D:(s + 1) * D], g.x2[:, bass.ds(t * D, D)],
                                             g.mv[:, bass.ds(2 * t, 1)], g.rstd[:, bass.ds(t, 1)], ALU.subtract, ALU.mult)
                last.then_inc(done, 1)

            def low(par, hi_done, n, lo_done):
                dve.wait_ge(hi_done, n + 1)
                dve.tensor_tensor(xt[par][:, 1].rearrange("p k t -> p (k t)"), tp,
                                  xt[par][:, 0].rearrange("p k t -> p (k t)"), ALU.subtract).then_inc(lo_done, 1)

            normalise(0, 0, r_rows)
            normalise(1, 1, r_rows)
            with dve.Fori(0, SHARED // 2 - 1) as q:
                for u in range(2):
                    n = 2 * q + u
                    low(u, r_hi, n, r_lo)
                    dve.wait_ge(xn_copied, n + 1)
                    normalise(u, n + 2, r_rows)
            low(0, r_hi, SHARED - 2, r_lo)
            low(1, r_hi, SHARED - 1, r_lo)

            dve.wait_ge(r_mm, SHARED)
            then(dve.scalar_tensor_tensor(out=logit3, in0=router_ps.rearrange("p (t e) -> p t e", e=NE), scalar=1.0 / WS,
                                          in1=g.bias.unsqueeze(1).broadcast_to((P, TILES, NE)), op0=ALU.mult, op1=ALU.add))
            for t in range(TILES):
                last = dve.max(best3[:, t], logit3[:, t])
            then(last)
            for t in range(TILES):
                last = dve.max_index(besti3[:, t], best3[:, t], logit3[:, t])
            then(last)
            dve.tensor_tensor(ediff, best3[:, :, 1], best3[:, :, 0], ALU.subtract).then_inc(diff_ok, 1)
            then(dve.tensor_copy(chosen3, besti3[:, :, 0:2].rearrange("p t k -> p k t")))
            iota_e = g.iota[:, 0:NE].unsqueeze(1).broadcast_to((P, TILES, NE))
            for k, oh in ((0, oh0), (1, oh1)):
                then(dve.tensor_tensor(oh.rearrange("p (t e) -> p t e", e=NE), iota_e,
                                       chosen3[:, k].unsqueeze(2).broadcast_to((P, TILES, NE)), ALU.is_equal))
            dve.tensor_tensor(member, oh0, oh1, ALU.add).then_inc(member_ok, 1)
            dve.wait_ge(e_ok, 1)
            then(dve.tensor_scalar(slot_f[:, 0:TILES], ediff, 1.0, None, ALU.add))
            then(dve.reciprocal(slot_f[:, 32:32 + TILES], slot_f[:, 0:TILES]))
            then(dve.tensor_scalar(g.cw[:, 0:TILES], slot_f[:, 32:32 + TILES], 0.5 / (WS * AS), None, ALU.mult))
            then(dve.tensor_tensor(g.cw[:, TILES:2 * TILES], g.cw[:, 0:TILES], ediff, ALU.mult))
            dve.wait_ge(rank_ok, 1)
            tot3 = rp[:, 256:512].rearrange("p (t e) -> p e t", e=NE)
            cum3 = cum.rearrange("p (e t) -> p e t", e=NE)
            then(dve.memset(prod[:, 0:TILES], 0.0))
            for e in range(NE):
                last = dve.tensor_tensor_scan(cum3[:, e], tot3[:, e], prod[:, 0:TILES], 0.0, ALU.add, ALU.add)
            then(last)
            then(dve.tensor_copy(count, cum3[:, :, TILES - 1]))
            fills3 = fills.rearrange("p (e j) -> p e j", e=NE)
            then(dve.tensor_tensor(fills3, count.unsqueeze(2).broadcast_to((P, NE, SHARED)),
                                   g.iota[:, NE:NE + SHARED].unsqueeze(1).broadcast_to((P, NE, SHARED)), ALU.is_gt))
            then(dve.tensor_reduce(ntile, fills3, AX.X, ALU.add))
            then(dve.tensor_tensor_scan(tend, ntile, prod[:, 0:NE], 0.0, ALU.add, ALU.add))
            then(dve.tensor_tensor(count, tend, ntile, ALU.subtract))
            slot3 = slot_of.rearrange("p (t e) -> p t e", e=NE)
            then(dve.tensor_tensor(slot3, cum3.rearrange("p e t -> p t e"), rp[:, 256:512].rearrange("p (t e) -> p t e", e=NE), ALU.subtract))
            then(dve.tensor_tensor(slot3, slot3, rp[:, 0:256].rearrange("p (t e) -> p t e", e=NE), ALU.add))
            then(dve.scalar_tensor_tensor(out=slot3, in0=count.unsqueeze(1).broadcast_to((P, TILES, NE)), scalar=float(ITEM),
                                          in1=slot3, op0=ALU.mult, op1=ALU.add))
            for k, oh in ((0, oh0), (1, oh1)):
                then(dve.tensor_tensor(prod, oh, slot_of, ALU.mult))
                then(dve.tensor_reduce(slot_f[:, k * TILES:(k + 1) * TILES], prod.rearrange("p (t e) -> p t e", e=NE), AX.X, ALU.add))
            then(dve.tensor_copy(g.slot, slot_f))
            dve.engine_nop().then_inc(slots_ok, 1)
            passed3 = passed.rearrange("p (n e) -> p n e", e=NE)
            then(dve.tensor_tensor(passed3, g.iota[:, NE + SHARED:].unsqueeze(2).broadcast_to((P, SPARSE, NE)),
                                   tend.unsqueeze(1).broadcast_to((P, SPARSE, NE)), ALU.is_ge))
            then(dve.tensor_reduce(prod[:, 0:SPARSE], passed3, AX.X, ALU.add))
            then(dve.tensor_scalar(g.texp, prod[:, 0:SPARSE], NE - 1.0, None, ALU.min))
            dve.engine_nop().then_inc(texp_ok, 1)

            def half(gi, par, h):
                m = 2 * gi + h
                dve.wait_ge(tanh_ok, m + 1)
                dve.scalar_tensor_tensor(out=th[h], in0=th[h], scalar=1.0, in1=gp[:, h], op0=ALU.add, op1=ALU.mult).then_inc(s_ok, 1)
                dve.wait_ge(s_ok, m + 1)
                dve.scalar_tensor_tensor(out=hid[h], in0=th[h], scalar=AS / (2 * WS * WS), in1=up_[:, h],
                                         op0=ALU.mult, op1=ALU.mult).then_inc(hid_ok, 1)

            def hid_low(gi, par, h):
                m = 2 * gi + h
                dve.wait_ge(h_hi, m + 1)
                dve.tensor_tensor(hb[2 * par + h][:, 1].rearrange("p c t -> p (c t)"), hid[h],
                                  hb[2 * par + h][:, 0].rearrange("p c t -> p (c t)"), ALU.subtract).then_inc(h_lo, 1)

            def add_y(gi, par):
                dve.wait_ge(dn_done, 2 * gi + 2)
                xs = g.x2[:, bass.ds(gi * 2 * D, 2 * D)]
                dve.scalar_tensor_tensor(out=xs, in0=yp[:, par], scalar=0.5 / (WS * AS), in1=xs,
                                         op0=ALU.mult, op1=ALU.add).then_inc(y_sh, 1)

            def item(gi, par, nxt, rows_after, add):
                half(gi, par, 0)
                if nxt:
                    low(1 - par, x_hi, gi + 1, x_lo)
                hid_low(gi, par, 0)
                half(gi, par, 1)
                if rows_after:
                    dve.wait_ge(t_done, gi + 1)
                    normalise(par, gi + 2, rows_sh)
                hid_low(gi, par, 1)
                if add:
                    add_y(gi - 1, 1 - par)

            dve.wait_ge(xn_copied, SHARED)
            normalise(0, 0, rows_sh)
            normalise(1, 1, rows_sh)
            low(0, x_hi, 0, x_lo)
            item(0, 0, True, True, False)
            with dve.Fori(0, (SHARED - 4) // 2) as q:
                item(2 * q + 1, 1, True, True, True)
                item(2 * q + 2, 0, True, True, True)
            item(SHARED - 3, 1, True, True, True)
            item(SHARED - 2, 0, True, False, True)
            item(SHARED - 1, 1, True, False, True)
            item(SHARED, 0, True, False, True)
            with dve.Fori(0, (SPARSE - 3) // 2) as q:
                b = SHARED + 2 * q + 1
                item(b, 1, True, False, False)
                item(b + 1, 0, True, False, False)
            item(SHARED + SPARSE - 2, 1, True, False, False)
            item(SHARED + SPARSE - 1, 0, False, False, False)

            def combine(t, r, k, cnt):
                dve.wait_ge(gat_in[r], cnt)
                xs = g.x2[:, bass.ds(t * D, D)]
                if k == 1:
                    dve.wait_ge(added, 2 * t + 1)
                dve.scalar_tensor_tensor(out=xs, in0=gat[r], scalar=g.cw[:, bass.ds(t + k * TILES, 1)], in1=xs,
                                         op0=ALU.mult, op1=ALU.add).then_inc(added, 1)

            with dve.Fori(0, TILES // 2) as q:
                for u in range(2):
                    for k in range(2):
                        combine(2 * q + u, 2 * u + k, k, 16 * q + 16)

        @block.gpsimd
        def _(pool):
            def copy_rows(n, par):
                pool.wait_ge(r_rows, n + 1)
                pool.tensor_copy(g.xn[:, bass.ds(n * 2 * D, 2 * D)], rows[par]).then_inc(xn_copied, 1)

            with pool.Fori(0, SHARED // 2) as q:
                copy_rows(2 * q, 0)
                copy_rows(2 * q + 1, 1)
            pool.wait_ge(xn_copied, SHARED)
            pool.wait_ge(slots_ok, 1)
            for t in range(TILES):
                for k in range(2):
                    pool.indirect_dma_start(g.slots, bass.IndirectOffsetOnAxis(ap=g.slot[:, k * TILES + t:k * TILES + t + 1], axis=0),
                                            g.xn[:, t * D:(t + 1) * D], None).then_inc(scattered, 16)

            def store(n, par):
                first = pool.snap(n * ITEM)
                pool.wait_ge(y_sp, n + 1)
                pool.dma_start(g.outs[bass.ds(first, ITEM)].rearrange("(s p) d -> p s d", p=P),
                               yst[par].rearrange("p (s d) -> p s d", s=2)).then_inc(y_out[par], 16)

            with pool.Fori(0, SPARSE // 2) as q:
                store(2 * q, 0)
                store(2 * q + 1, 1)
            store(SPARSE - 1, 0)
            pool.wait_ge(y_out[0], 16 * (SPARSE // 2 + 1))
            pool.wait_ge(y_out[1], 16 * (SPARSE // 2))
            for t in range(TILES):
                for k in range(2):
                    r = 2 * (t % 2) + k
                    if t >= 2:
                        pool.wait_ge(added, 2 * (t - 2) + k + 1)
                    pool.indirect_dma_start(gat[r], None, g.outs,
                                            bass.IndirectOffsetOnAxis(ap=g.slot[:, k * TILES + t:k * TILES + t + 1], axis=0)
                                            ).then_inc(gat_in[r], 16)

        @block.sync
        def _(sp):
            if reload:
                sp.dma_start(g.wf[:, KEPT * WEXP:NE * WEXP], g.w_dram).then_inc(w_back, 16)
            sp.wait_ge(scattered, 16 * 2 * TILES)

            def load(n, par, gi):
                first = sp.snap(n * ITEM)
                sp.wait_ge(t_done, gi - 1)
                sp.dma_start(rows[par].rearrange("p (s d) -> p s d", s=2),
                             g.slots[bass.ds(first, ITEM)].rearrange("(s p) d -> p s d", p=P)).then_inc(rows_sp[par], 16)

            load(0, 0, SHARED)
            load(1, 1, SHARED + 1)
            with sp.Fori(0, (SPARSE - 3) // 2) as q:
                n = 2 * q
                load(n + 2, 0, SHARED + n + 2)
                load(n + 3, 1, SHARED + n + 3)
            load(SPARSE - 1, 0, SHARED + SPARSE - 1)


def attention(nc, g, a):
    with ExitStack() as ctx:
        def sem(n):
            return ctx.enter_context(nc.semaphore(f"att_{n}"))

        w = g.work
        at = [0]

        def take(n):
            at[0] += n
            assert at[0] <= g.work_words
            return w[:, at[0] - n:at[0]]

        hrow = [take(D) for _ in range(2)]
        ht = [take(D).bitcast(F16).rearrange("p (l k t) -> p l k t", l=2, k=KD) for _ in range(2)]
        vs = [take(D) for _ in range(2)]
        mx = [take(D) for _ in range(2)]
        tree = take(64 * 8).rearrange("p (g c) -> p g c", c=8)
        zsum = take(D)
        dots = take(M)
        state = [take(STEPS * M).rearrange("p (t j) -> p t j", j=M) for _ in range(2)]
        yc = take(D)
        ho = take(D)
        ot = take(D).bitcast(F16).rearrange("p (l k t) -> p l k t", l=2, k=KD)
        over = g.wf[:, KEPT * WEXP:NE * WEXP].bitcast(F32)
        n_e = HEADS * ROW
        gate = [over[:, r * n_e:(r + 1) * n_e].rearrange("p (h c) -> p h c", h=HEADS) for r in range(2)]
        step_g = [over[:, (2 + r) * n_e:(3 + r) * n_e].rearrange("p (t c) -> p t c", t=STEPS) for r in range(2)]
        raw = [over[:, r * 512:(r + 1) * 512] for r in range(4)]
        late = g.late.bitcast(F16)
        na = HEADS * GATE
        wa = [late[:, l * KD * na:(l + 1) * KD * na].rearrange("p (k n) -> p k n", k=KD) for l in range(2)]
        o = 2 * KD * na
        wv = [late[:, o + l * KD * D:o + (l + 1) * KD * D].rearrange("p (k n) -> p k n", k=KD) for l in range(2)]
        o += 2 * KD * D
        wo = [late[:, o + l * KD * D:o + (l + 1) * KD * D].rearrange("p (k n) -> p k n", k=KD) for l in range(2)]
        lp = [g.psum[:, 2 * r:2 * r + 2] for r in range(3)]
        tp, vo = g.psum[:, 6], g.psum[:, 7]
        v_ps, o_ps = vo[:, 0:D], vo[:, D:2 * D]
        tph, tpo = tp[:, 0:D], tp[:, D:2 * D]
        groups = [("a", n) for n in range(na // 256)] + [("v", 0), ("o", 0)]
        src = {"a": a["W_a"], "v": a["W_v"], "o": a["W_out"]}
        dst = {"a": wa, "v": wv, "o": wo}

        raw_in = [sem(f"raw_in{r}") for r in range(4)]
        (p_t, p_hi, p_lo, stat, var_ok, std, rc, ms_ok, scales_ok, rms, h_ok, x_ok, ht_ps, ht_hi, ht_lo, v_ok,
         v_sb, l_ps, l_ev, mx_ok, sub_ok, ex_ok, z_ok, tr, zr_ok, sc, yc_ok, ot_ps, ot_hi,
         ot_lo, o_ok, x_add) = map(sem, (
             "p_t", "p_hi", "p_lo", "stat", "var_ok", "std", "rc", "ms_ok", "scales_ok", "rms", "h_ok", "x_ok", "ht_ps",
             "ht_hi", "ht_lo", "v_ok", "v_sb", "l_ps", "l_ev", "mx_ok", "sub_ok", "ex_ok", "z_ok", "tr",
             "zr_ok", "sc", "yc_ok", "ot_ps", "ot_hi", "ot_lo", "o_ok", "x_add"))
        g_out = [[sem(f"g_out{r}_{j}") for j in range(4)] for r in range(2)]
        g_in = [sem("g_in0"), sem("g_in1")]
        y_out, y_in = sem("y_out"), sem("y_in")
        block = ctx.enter_context(nc.Block())

        LAG_R, LAG_S, LAG_O = 1, 3, 4

        def iterations(eng, body):
            for it in range(LAG_O):
                body(it, it // 2, it % 2)
            with eng.Fori(LAG_O // 2, TILES // 2 - 1) as q:
                body(2 * q, q, 0)
                body(2 * q + 1, q, 1)
            for it in range(TILES - 2, TILES + LAG_O):
                body(it, it // 2, it % 2)

        def on(it, lag):
            return not isinstance(it, int) or 0 <= it - lag < TILES

        def ahead(it):
            return not isinstance(it, int) or it + 1 < TILES

        @block.sync
        def _(sp):
            for n, (what, i) in enumerate(groups):
                r = n % 4
                if n >= 4:
                    sp.wait_ge(p_t, n - 3)
                sp.dma_start(raw[r].rearrange("p (s d) -> p s d", s=2),
                             src[what][i * 256:(i + 1) * 256].rearrange("(s p) d -> p s d", p=P)).then_inc(raw_in[r], 16)

            def body(it, q, par):
                if on(it, LAG_O):
                    k = it - LAG_O
                    read_back = 16 * BATCH * it - 16 * BATCH * LAG_O
                    sp.wait_ge(yc_ok, k + 1)
                    if not (isinstance(it, int) and k == 0):
                        sp.wait_ge(y_in, read_back)
                    sp.dma_start(g.y_dram, yc).then_inc(y_out, 16)
                    sp.wait_ge(y_out, 16 * k + 16)
                    if not (isinstance(it, int) and k == 0):
                        sp.wait_ge(ot_ps, k)
                    for b in range(BATCH):
                        sp.dma_start(ho[b * STEPS:(b + 1) * STEPS].rearrange("p (h i) -> p h i", h=HEADS),
                                     g.y_dram[b * STEPS:(b + 1) * STEPS].rearrange("h (t i) -> t h i", i=M)).then_inc(y_in, 16)
                if on(it, LAG_R):
                    k, kpar = it - LAG_R, 1 - par
                    uses = q - (1 if par == 0 else 0)
                    read_back = 8 * BATCH * it - 8 * BATCH * (2 - par)
                    landed = 16 * uses + 16
                    if not (isinstance(it, int) and k < 2):
                        sp.wait_ge(g_in[kpar], read_back)
                    for j in range(4):
                        sp.wait_ge(zr_ok, 8 * it - (6 - 2 * j))
                        cols = slice(4 * j * ROW, 4 * (j + 1) * ROW)
                        sp.dma_start(g.g_dram[kpar][:, cols],
                                     gate[kpar].rearrange("p h c -> p (h c)")[:, cols]).then_inc(g_out[kpar][j], 16)
                    for j in range(4):
                        sp.wait_ge(g_out[kpar][j], landed)
                    if not (isinstance(it, int) and k < 2):
                        sp.wait_ge(sc, 3 * STEPS * (k - 1))
                    for b in range(BATCH):
                        sp.dma_start(step_g[kpar][b * STEPS:(b + 1) * STEPS],
                                     g.g_dram[kpar][b * STEPS:(b + 1) * STEPS].rearrange("t (h c) -> h t c", h=HEADS)
                                     ).then_inc(g_in[kpar], 16)

            iterations(sp, body)

        @block.tensor
        def _(pe):
            for n, (what, i) in enumerate(groups):
                pe.wait_ge(raw_in[n % 4], 16 * (n // 4 + 1))
                if n >= 6:
                    pe.wait_ge(p_lo, n - 5)
                bank = g.psum[:, n % 6]
                for k in range(KD):
                    for s in range(2):
                        last = pe.transpose(bank[:, (k * 2 + s) * P:(k * 2 + s + 1) * P],
                                            raw[n % 4][:, s * D + k * P:s * D + (k + 1) * P], g.ident)
                last.then_inc(p_t, 1)

            def h_transpose(k, par):
                pe.wait_ge(h_ok, k + 1)
                if not (isinstance(k, int) and k < 6):
                    pe.wait_ge(ot_lo, k - 5)
                for c in range(KD):
                    last = pe.transpose(tph[:, c * P:(c + 1) * P], hrow[par][:, c * P:(c + 1) * P], g.ident)
                last.then_inc(ht_ps, 1)

            def product(out, left, right):
                i = 0
                for k in range(KD):
                    for l, r in ((0, 0), (0, 1), (1, 0)):
                        last = pe.matmul(out, left[:, l, k], right[r][:, k], start=(i == 0), stop=(i == 5))
                        i += 1
                return last

            pe.wait_ge(p_lo, len(groups))
            h_transpose(0, 0)

            def body(it, q, par):
                if on(it, 0):
                    pe.wait_ge(ht_lo, it + 1)
                    if not (isinstance(it, int) and it < 5):
                        pe.wait_ge(x_add, it - 4)
                    product(v_ps, ht[par], wv).then_inc(v_ok, 1)
                    if ahead(it):
                        h_transpose(it + 1, 1 - par)
                    for j in range(HEADS // 2):
                        slot = j % 3
                        done = it * 8 + j - (1 if j < 2 else 2)
                        if not (isinstance(done, int) and done < 1):
                            pe.wait_ge(l_ev, done)
                        for s in range(2):
                            h = 2 * j + s
                            last = product(lp[slot][:, s, 0:GATE], ht[par],
                                           [x[:, :, h * GATE:(h + 1) * GATE] for x in wa])
                        last.then_inc(l_ps, 1)
                if on(it, LAG_O):
                    k = it - LAG_O
                    pe.wait_ge(y_in, 16 * BATCH * (k + 1))
                    if isinstance(it, int) and it + 1 >= TILES:
                        pe.wait_ge(ht_lo, TILES)
                    else:
                        pe.wait_ge(ht_lo, it + 2)
                    for c in range(KD):
                        last = pe.transpose(tpo[:, c * P:(c + 1) * P], ho[:, c * P:(c + 1) * P], g.ident)
                    last.then_inc(ot_ps, 1)
                    pe.wait_ge(ot_lo, k + 1)
                    if isinstance(it, int) and it >= TILES:
                        pe.wait_ge(v_sb, TILES)
                    else:
                        pe.wait_ge(v_sb, it + 1)
                    product(o_ps, ot, wo).then_inc(o_ok, 1)

            iterations(pe, body)

        @block.scalar
        def _(act):
            for n, (what, i) in enumerate(groups):
                act.wait_ge(p_t, n + 1)
                for k in range(KD):
                    scale = WS if what == "o" else g.nws[:, k:k + 1]
                    last = act.activation(dst[what][0][:, k, i * 256:(i + 1) * 256],
                                          g.psum[:, n % 6, k * 256:(k + 1) * 256], ACT.Copy, scale=scale)
                last.then_inc(p_hi, 1)
            act.wait_ge(var_ok, 1)
            act.activation(g.std, g.mv3[:, :, 1], ACT.Sqrt, bias=g.eps, scale=1.0).then_inc(std, 1)
            act.wait_ge(ms_ok, 1)
            act.activation(g.rms, g.ms, ACT.Sqrt, bias=g.eps, scale=1.0).then_inc(rms, 1)

            def h_high(k, par):
                act.wait_ge(ht_ps, k + 1)
                if not (isinstance(k, int) and k < 2):
                    act.wait_ge(l_ps, 8 * k - 8)
                act.activation(ht[par][:, 0].rearrange("p k t -> p (k t)"), tph, ACT.Copy).then_inc(ht_hi, 1)

            def h_row(k, par):
                if not (isinstance(k, int) and k < 2):
                    act.wait_ge(ht_ps, k - 1)
                act.activation(hrow[par], g.x2[:, bass.ds(k * D, D)], ACT.Identity, bias=g.hb[:, bass.ds(k, 1)],
                               scale=g.hs[:, bass.ds(k, 1)]).then_inc(h_ok, 1)

            def x_self(k):
                act.wait_ge(h_ok, k + 1)
                xs = g.x2[:, bass.ds(k * D, D)]
                act.activation(xs, xs, ACT.Identity, bias=g.xb[:, bass.ds(k, 1)], scale=g.xa[:, bass.ds(k, 1)]).then_inc(x_ok, 1)

            act.wait_ge(scales_ok, 1)
            for k in range(2):
                h_row(k, k)
                x_self(k)
            h_high(0, 0)

            def body(it, q, par):
                def exponential(k, kpar, j):
                    act.wait_ge(sub_ok, k * 4 + j + 1)
                    e = gate[kpar][:, 4 * j:4 * j + 4, 0:GATE]
                    act.activation(e, e, ACT.Exp).then_inc(ex_ok, 1)

                def logits(j):
                    if not (isinstance(it, int) and it < 2) and j % 2 == 0:
                        act.wait_ge(g_out[par][j // 2], 16 * q)
                    act.wait_ge(l_ps, it * 8 + j + 1)
                    act.activation(gate[par][:, 2 * j:2 * j + 2, 0:GATE], lp[j % 3][:, :, 0:GATE],
                                   ACT.Copy, scale=1.0 / WS).then_inc(l_ev, 1)

                if on(it, 0):
                    act.wait_ge(v_ok, it + 1)
                    if not (isinstance(it, int) and it < 2):
                        act.wait_ge(zr_ok, 8 * it - 8)
                    act.activation(vs[par], v_ps, ACT.Copy, scale=1.0 / WS).then_inc(v_sb, 1)
                    logits(0)
                    if ahead(it):
                        h_high(it + 1, 1 - par)
                    logits(1)
                if on(it, 1):
                    exponential(it - 1, 1 - par, 3)
                if on(it, LAG_O):
                    k = it - LAG_O
                    act.wait_ge(sc, 3 * STEPS * (k + 1))
                    if not (isinstance(it, int) and k == 0):
                        act.wait_ge(y_out, 16 * k)
                    act.activation(yc.rearrange("p (t i) -> p t i", i=M), state[par], ACT.Copy).then_inc(yc_ok, 1)
                if on(it, 0):
                    for j in range(2, HEADS // 2):
                        logits(j)
                    if not isinstance(it, int) or it + 2 < TILES:
                        h_row(it + 2, par)
                        x_self(it + 2)
                if on(it, LAG_O):
                    k = it - LAG_O
                    act.wait_ge(ot_ps, k + 1)
                    if not (isinstance(it, int) and k == 0):
                        act.wait_ge(o_ok, k)
                    act.activation(ot[:, 0].rearrange("p k t -> p (k t)"), tpo, ACT.Copy).then_inc(ot_hi, 1)
                if on(it, 0):
                    for j in range(3):
                        exponential(it, par, j)

            iterations(act, body)

        @block.gpsimd
        def _(pool):
            def body(it, q, par):
                if on(it, LAG_R):
                    k = it - LAG_R
                    gv = gate[1 - par][:, :, 0:GATE].rearrange("p h (i j) -> p h i j", j=M + 1)
                    for j in range(4):
                        pool.wait_ge(ex_ok, k * 4 + j + 1)
                        e = gv[:, 4 * j:4 * j + 4]
                        c = (k * 4 + j) * 4
                        t4 = tree.rearrange("p (h i) c -> p h i c", h=4)
                        pool.tensor_tensor(t4, e[:, :, :, 1:9], e[:, :, :, 9:17], ALU.add).then_inc(tr, 1)
                        for n, wd in enumerate((4, 2, 1)):
                            pool.wait_ge(tr, c + n + 1)
                            pool.tensor_tensor(tree[:, :, 0:wd], tree[:, :, 0:wd], tree[:, :, wd:2 * wd], ALU.add).then_inc(tr, 1)
                        pool.wait_ge(tr, c + 4)
                        if j == 0 and not (isinstance(it, int) and k == 0):
                            pool.wait_ge(zr_ok, 8 * k)
                        pool.tensor_tensor(zsum[:, 64 * j:64 * j + 64].rearrange("p (h i) -> p h i", h=4),
                                           t4[:, :, :, 0], e[:, :, :, 0], ALU.add).then_inc(z_ok, 1)
                        pool.wait_ge(z_ok, k * 4 + j + 1)
                if on(it, 0):
                    gv = gate[par][:, :, 0:GATE].rearrange("p h (i j) -> p h i j", j=M + 1)
                    for j in range(4):
                        pool.wait_ge(mx_ok, it * 16 + 4 * j + 4)
                        e = gv[:, 4 * j:4 * j + 4]
                        m = mx[par][:, 64 * j:64 * j + 64].rearrange("p (h i) -> p h i", h=4)
                        pool.tensor_tensor(e, e, m.unsqueeze(3).broadcast_to((P, 4, M, M + 1)), ALU.subtract).then_inc(sub_ok, 1)

            iterations(pool, body)

        @block.vector
        def _(dve):
            dve.memset(state[1][:, STEPS - 1], 0.0).then_inc(rc, 1)
            token_statistics(nc, g, dve, stat)
            dve.wait_ge(stat, TILES + 1)
            dve.engine_nop().then_inc(var_ok, 1)
            for n, (what, i) in enumerate(groups):
                dve.wait_ge(p_hi, n + 1)
                for k in range(KD):
                    scale = WS if what == "o" else g.nws[:, k:k + 1]
                    last = dve.scalar_tensor_tensor(out=dst[what][1][:, k, i * 256:(i + 1) * 256],
                                                    in0=g.psum[:, n % 6, k * 256:(k + 1) * 256], scalar=scale,
                                                    in1=dst[what][0][:, k, i * 256:(i + 1) * 256],
                                                    op0=ALU.mult, op1=ALU.subtract)
                last.then_inc(p_lo, 1)
            chain = [1]

            def then(ins):
                ins.then_inc(rc, 1)
                chain[0] += 1
                dve.wait_ge(rc, chain[0])

            dve.wait_ge(std, 1)
            refined_rsqrt(dve, g.rstd, g.std, g.mv3[:, :, 1], EPS, g.ms, then)
            then(dve.tensor_tensor(g.ms, g.rstd, g.rstd, ALU.mult))
            then(dve.tensor_tensor(g.ms, g.ms, g.mv3[:, :, 1], ALU.mult))
            dve.engine_nop().then_inc(ms_ok, 1)
            dve.wait_ge(rms, 1)
            refined_rsqrt(dve, g.hs, g.rms, g.ms, EPS, g.xa, then)
            then(dve.tensor_copy(g.rms, g.hs))
            then(dve.tensor_tensor(g.hs, g.rms, g.rstd, ALU.mult))
            then(dve.tensor_scalar(g.xa, g.rstd, 1.0, None, ALU.add))
            then(dve.scalar_tensor_tensor(out=g.xb, in0=g.mv3[:, :, 0], scalar=-1.0, in1=g.rstd, op0=ALU.mult, op1=ALU.mult))
            then(dve.scalar_tensor_tensor(out=g.hb, in0=g.mv3[:, :, 0], scalar=-1.0, in1=g.hs, op0=ALU.mult, op1=ALU.mult))

            def h_low(k, par):
                dve.wait_ge(ht_hi, k + 1)
                dve.tensor_tensor(ht[par][:, 1].rearrange("p k t -> p (k t)"), tph,
                                  ht[par][:, 0].rearrange("p k t -> p (k t)"), ALU.subtract).then_inc(ht_lo, 1)

            dve.engine_nop().then_inc(scales_ok, 1)
            h_low(0, 0)

            def body(it, q, par):
                def low_next():
                    h_low(it + 1, 1 - par)

                def maximum(h):
                    if h % 2 == 0:
                        dve.wait_ge(l_ev, it * 8 + h // 2 + 1)
                    if h == 0 and not (isinstance(it, int) and it < 2):
                        dve.wait_ge(sub_ok, 4 * it - 4)
                    dve.tensor_reduce(mx[par][:, M * h:M * h + M],
                                      gate[par][:, h, 0:GATE].rearrange("p (i j) -> p i j", j=M + 1),
                                      AX.X, ALU.max).then_inc(mx_ok, 1)

                def invert(j):
                    k = it - LAG_R
                    dve.wait_ge(z_ok, 4 * k + j + 1)
                    dve.reciprocal(gate[1 - par][:, 4 * j:4 * j + 4, GATE:ROW],
                                   zsum[:, 64 * j:64 * j + 64].rearrange("p (h i) -> p h i", h=4)).then_inc(zr_ok, 1)

                def times_v(j):
                    k = it - LAG_R
                    if j == 0:
                        dve.wait_ge(v_sb, k + 1)
                    e0 = gate[1 - par][:, 4 * j:4 * j + 4, 0:GATE:M + 1]
                    dve.tensor_tensor(e0, e0, vs[1 - par][:, 64 * j:64 * j + 64].rearrange("p (h i) -> p h i", h=4),
                                      ALU.mult).then_inc(zr_ok, 1)

                def finish(j):
                    invert(j)
                    times_v(j)

                def out_low():
                    k = it - LAG_O
                    dve.wait_ge(ot_hi, k + 1)
                    dve.tensor_tensor(ot[:, 1].rearrange("p k t -> p (k t)"), tpo, ot[:, 0].rearrange("p k t -> p (k t)"),
                                      ALU.subtract).then_inc(ot_lo, 1)

                def add_out():
                    k = it - LAG_O
                    dve.wait_ge(o_ok, k + 1)
                    dve.wait_ge(x_ok, k + 1)
                    xs = g.x2[:, bass.ds(k * D, D)]
                    dve.scalar_tensor_tensor(out=xs, in0=o_ps, scalar=1.0 / WS, in1=xs, op0=ALU.mult, op1=ALU.add).then_inc(x_add, 1)

                logits = [(maximum, h) for h in range(HEADS)] if on(it, 0) else []
                sums = [(finish, j) for j in range(4)] if on(it, LAG_R) else []
                next_h = [(low_next,)] if ahead(it) else []
                outputs = [(out_low,), (add_out,)] if on(it, LAG_O) else []
                todo = (logits[0:2] + next_h + logits[2:4] + sums[0:1] + logits[4:7] + sums[1:2] + logits[7:10]
                        + sums[2:3] + logits[10:11] + outputs[0:1] + logits[11:12] + sums[3:4] + outputs[1:2]
                        + logits[12:])

                def other_work(place):
                    if place % 2 == 1 and place // 2 < len(todo):
                        todo[place // 2][0](*todo[place // 2][1:])

                scan = on(it, LAG_S)
                k = it - LAG_S
                sg, st, before = step_g[1 - par], state[1 - par], state[par]
                if scan:
                    uses = q - (2 if par == 0 else 1)
                    dve.wait_ge(g_in[1 - par], 16 * BATCH * (uses + 1))
                    if not (isinstance(it, int) and k < 2):
                        dve.wait_ge(yc_ok, k - 1)
                for t in range(STEPS):
                    c = 3 * STEPS * k + 3 * t
                    rows = sg[:, t, 0:GATE].rearrange("p (i j) -> p i j", j=M + 1)
                    prev = st[:, t - 1] if t else before[:, STEPS - 1]
                    if scan:
                        if not (isinstance(c, int) and c == 0):
                            dve.wait_ge(sc, c)
                        dve.tensor_tensor(rows[:, :, 1:], rows[:, :, 1:],
                                          prev.unsqueeze(1).broadcast_to((P, M, M)), ALU.mult).then_inc(sc, 1)
                    other_work(3 * t)
                    if scan:
                        dve.wait_ge(sc, c + 1)
                        dve.tensor_reduce(dots, rows, AX.X, ALU.add).then_inc(sc, 1)
                    other_work(3 * t + 1)
                    if scan:
                        dve.wait_ge(sc, c + 2)
                        dve.tensor_tensor(st[:, t], dots, sg[:, t, GATE:ROW], ALU.mult).then_inc(sc, 1)
                    other_work(3 * t + 2)

            iterations(dve, body)


def store_output(nc, g, out):
    with nc.semaphore("stored") as stored, nc.Block() as block:
        @block.sync
        def _(sp):
            for b in range(BATCH):
                sp.dma_start(out[b].rearrange("(n t) d -> t n d", t=STEPS), g.x[b * STEPS:(b + 1) * STEPS]).then_inc(stored, 16)
            sp.wait_ge(stored, 16 * BATCH)


def build(nc, a, out):
    g = Core()
    with ExitStack() as ctx:
        def sb(name, shape, dt):
            return ctx.enter_context(nc.sbuf_tensor(name, shape, dt))[:]

        g.x2 = sb("x_tokens", [P, TILES * D], F32)
        g.x = g.x2.rearrange("p (n d) -> p n d", d=D)
        g.wf = sb("expert_weights", [P, (NE + 1) * WEXP], F16)
        late_words = 2 * KD * HEADS * GATE // 2 + 2 * KD * D
        g.late = sb("gate_weights", [P, late_words], F32)
        g.xn = g.late[:, 0:TILES * D]
        g.work_words = 6144
        g.work = sb("work", [P, g.work_words], F32)
        g.ident = sb("identity", [P, P], F32)
        g.ones = sb("ones", [P, P], F16)
        g.before = sb("before", [P, P], F16)
        g.rw_raw = sb("router_raw", [P, KD, NE], F32)
        g.rw = sb("router_weights", [P, 2, KD, NE], F16)
        g.nw = sb("norm_weights", [P, KD], F32)
        g.nws = sb("scaled_norm_weights", [P, KD], F32)
        g.bias = sb("router_bias", [P, NE], F32)
        g.eps = sb("eps", [P, 1], F32)
        g.iota_i = g.work[:, 1024:1024 + NE + SHARED + SPARSE].bitcast(I32)
        g.iota = sb("iota", [P, NE + SHARED + SPARSE], F32)
        g.stats = sb("stats", [P, TILES * 6], F32)
        g.mv = sb("mean_var", [P, TILES * 2], F32)
        g.mv3 = g.mv.rearrange("p (t c) -> p t c", c=2)
        g.std, g.rstd, g.rms, g.ms, g.hs, g.xa, g.xb, g.hb = (sb(n, [P, TILES], F32) for n in (
            "std", "rstd", "rms", "ms", "hs", "xa", "xb", "hb"))
        g.cw = sb("expert_shares", [P, 2 * TILES], F32)
        g.slot = sb("slots_of_tokens", [P, 2 * TILES], U32)
        g.texp = sb("experts_of_tiles", [P, SPARSE], I32)
        g.psum = ctx.enter_context(nc.psum_tensor("psum", [P, 8, 512], F32))[:]
        rows = SPARSE * ITEM
        g.slots = nc.dram_tensor("slot_rows", (rows, D), F32, kind="Internal").ap()
        g.outs = nc.dram_tensor("slot_outputs", (rows, D), F32, kind="Internal").ap()
        g.w_dram = nc.dram_tensor("split_weights", (P, (NE - KEPT) * WEXP), F16, kind="Internal").ap()
        gd = [nc.dram_tensor(f"gates{r}", (P, HEADS * ROW), F32, kind="Internal").ap() for r in range(2)]
        g.g_dram = gd
        g.y_dram = nc.dram_tensor("head_outputs", (P, STEPS * M), F32, kind="Internal").ap()
        load_inputs(nc, g, a)
        ffn(nc, g, "f1", False)
        attention(nc, g, a)
        ffn(nc, g, "f2", True)
        store_output(nc, g, out)


_INS = {"L0_attn_x": "x", "L0_attn_norm_w": "norm_w", "L0_attn_W_v": "W_v", "L0_attn_W_a": "W_a",
        "L0_attn_W_out": "W_out", "L0_ffn_router_w": "router_w", "L0_ffn_experts_bias": "bias",
        "L0_ffn_w1": "w1", "L0_ffn_w3": "w3", "L0_ffn_w2": "w2", "L0_ffn_sw1": "sw1", "L0_ffn_sw3": "sw3",
        "L0_ffn_sw2": "sw2"}


def kernel(**inputs):
    import numpy as np
    import concourse.bacc as bacc
    from concourse.bass_utils import run_bass_kernel_spmd

    nc = bacc.Bacc("TRN2", target_bir_lowering=False, num_devices=1)
    arrays, aps = {}, {}
    for name, short in _INS.items():
        arr = np.ascontiguousarray(inputs[name])
        arrays[f"in_{short}"] = arr
        aps[short] = nc.dram_tensor(f"in_{short}", arr.shape, mybir.dt.from_np(arr.dtype), kind="ExternalInput").ap()
    out = nc.dram_tensor("out", (BATCH, TIME, D), F32, kind="ExternalOutput").ap()
    build(nc, aps, out)
    r = run_bass_kernel_spmd(nc, [arrays], core_ids=[0])
    return np.asarray(r.results[0]["out"])
```

```python
from contextlib import ExitStack

import concourse.bass as bass
from concourse import mybir

F32 = mybir.dt.float32
F16 = mybir.dt.float16
I32 = mybir.dt.int32
U32 = mybir.dt.uint32
ALU = mybir.AluOpType
ACT = mybir.ActivationFunctionType
AX = mybir.AxisListType

P = 128
BATCH, TIME, D = 8, 512, 256
STEPS = P // BATCH
TILES = TIME // STEPS
KD = D // P
HID = 512
HC = HID // P
NE = 8
ITEM = 256
SHARED = BATCH * TIME // ITEM
SPARSE = 2 * BATCH * TIME // ITEM + NE - 1
HEADS, M = 16, 16
GATE = M * (M + 1)
ROW = GATE + M
WS = 64.0
AS = 4.0
EPS = 1e-5
WEXP = 2 * (2 * KD * HID + HC * D)
O1H, O1L = 0, KD * HID
O3H, O3L = 2 * KD * HID, 3 * KD * HID
O2H, O2L = 4 * KD * HID, 4 * KD * HID + HC * D
KEPT = 2
GATHERS = 8
ROUND = 8
SLOT_TILES = SPARSE * ITEM // P
PAIRS = 2 * TILES
CHUNK = 16
BY_VECTOR = 4
PART = KD * HID


class Core:
    pass


def split_weights_high(act, g, base, raw, parts):
    for n, o_hi in enumerate(parts):
        last = act.activation(g.wf[:, base + o_hi:base + o_hi + PART], raw[:, n * PART:(n + 1) * PART], ACT.Copy, scale=WS)
    return last


def scale_weights(act, raw, parts):
    n = len(parts) * PART
    return act.activation(raw[:, 0:n], raw[:, 0:n], ACT.Copy, scale=WS)


def split_scaled(act, pool, g, base, raw, parts, high):
    for n, o_hi in enumerate(parts):
        w = base + o_hi
        if high:
            last = act.activation(g.wf[:, w:w + PART], raw[:, n * PART:(n + 1) * PART], ACT.Copy)
        else:
            last = pool.tensor_tensor(g.wf[:, w + PART:w + 2 * PART], raw[:, n * PART:(n + 1) * PART],
                                      g.wf[:, w:w + PART], ALU.subtract)
    return last


def split_weights_low(dve, g, base, raw, parts):
    for n, o_hi in enumerate(parts):
        w = base + o_hi
        last = dve.scalar_tensor_tensor(out=g.wf[:, w + PART:w + 2 * PART], in0=raw[:, n * PART:(n + 1) * PART],
                                        scalar=WS, in1=g.wf[:, w:w + PART], op0=ALU.mult, op1=ALU.subtract)
    return last


ALL_PARTS = (O1H, O3H, O2H)


def staged(g, e):
    place = NE - 1 if e == NE else e - 2
    return g.wf[:, place * WEXP:(place + 1) * WEXP].bitcast(F32)


def load_weight(eng, a, e, n, to, done):
    name = ("w1", "w3", "w2")[n]
    src = a["s" + name][0] if e == NE else a[name][e]
    eng.dma_start(to.rearrange("p (k n) -> p k n", n=D if n == 2 else HID),
                  src.rearrange("(k p) n -> p k n", p=P)).then_inc(done, 16)


def load_inputs(nc, g, a):
    with ExitStack() as ctx:
        sem = lambda n: ctx.enter_context(nc.semaphore(n))
        x_in, small_in, iotas, tri, ident_z, consts, shared_in, shared_hi = map(sem, (
            "x_in", "small_in", "iotas", "tri", "ident_z", "consts", "shared_in", "shared_hi"))
        block = ctx.enter_context(nc.Block())

        @block.sync
        def _(sp):
            for b in range(BATCH):
                sp.dma_start(g.x[b * STEPS:(b + 1) * STEPS],
                             a["x"][b].rearrange("(n t) d -> t n d", t=STEPS)).then_inc(x_in, 16)
            for n in range(3):
                load_weight(sp, a, NE, n, staged(g, NE)[:, n * PART:(n + 1) * PART], shared_in)
            for e in range(NE - 1, KEPT - 1, -1):
                for n in range(3):
                    load_weight(sp, a, e, n, staged(g, e)[:, n * PART:(n + 1) * PART], g.raw_in[e])
            sp.wait_ge(x_in, 16 * BATCH)

        @block.gpsimd
        def _(pool):
            with nc.allow_non_contiguous_dma(reason="2304 words, once"):
                for k in range(KD):
                    pool.dma_start(g.rw_raw[:, k],
                                   a["router_w"][:, k * P:(k + 1) * P].rearrange("e p -> p e")).then_inc(small_in, 16)
                pool.dma_start(g.nw, a["norm_w"].rearrange("(k p) -> p k", p=P)).then_inc(small_in, 16)
            pool.dma_start(g.bias, a["bias"].partition_broadcast(P)).then_inc(small_in, 16)
            pool.memset(g.ident, 0.0).then_inc(ident_z, 1)
            pool.memset(g.ones, 1.0).then_inc(ident_z, 1)
            pool.memset(g.before, 1.0).then_inc(ident_z, 1)
            pool.memset(g.eps, EPS).then_inc(tri, 1)
            pool.iota(g.iota_i[:, 0:NE], pattern=[[1, NE]], base=0, channel_multiplier=0).then_inc(iotas, 1)
            pool.iota(g.iota_i[:, NE:NE + SHARED], pattern=[[ITEM, SHARED]], base=0, channel_multiplier=0).then_inc(iotas, 1)
            c = NE + SHARED + SPARSE
            pool.iota(g.iota_i[:, NE + SHARED:c], pattern=[[1, SPARSE]], base=0, channel_multiplier=0).then_inc(iotas, 1)
            pool.iota(g.iota_i[:, c:c + TILES], pattern=[[P, TILES]], base=-BATCH * TIME // 2,
                      channel_multiplier=1).then_inc(iotas, 1)
            pool.iota(g.iota_i[:, c + TILES:c + TILES + P], pattern=[[1, P]], base=0, channel_multiplier=0).then_inc(iotas, 1)
            pool.wait_ge(ident_z, 3)
            pool.affine_select(out=g.ident, in_=g.ident, compare_op=ALU.not_equal, fill=1.0, base=0,
                               pattern=[[-1, P]], channel_multiplier=1).then_inc(tri, 1)
            pool.affine_select(out=g.before, in_=g.before, compare_op=ALU.is_gt, fill=0.0, base=0,
                               pattern=[[1, P]], channel_multiplier=-1).then_inc(tri, 1)
            pool.wait_ge(tri, 3)

        @block.scalar
        def _(act):
            act.wait_ge(small_in, 16 * (KD + 2))
            act.activation(g.rw[:, 0], g.rw_raw, ACT.Copy, scale=WS).then_inc(consts, 1)
            act.wait_ge(shared_in, 48)
            split_weights_high(act, g, NE * WEXP, staged(g, NE), ALL_PARTS).then_inc(shared_hi, 1)

        @block.vector
        def _(dve):
            dve.wait_ge(consts, 1)
            dve.scalar_tensor_tensor(out=g.rw[:, 1], in0=g.rw_raw, scalar=WS, in1=g.rw[:, 0],
                                     op0=ALU.mult, op1=ALU.subtract)
            dve.wait_ge(iotas, 5)
            c = NE + SHARED + SPARSE
            dve.tensor_copy(g.iota, g.iota_i[:, 0:c])
            dve.tensor_copy(g.token, g.iota_i[:, c:c + TILES])
            dve.tensor_copy(g.lanes, g.iota_i[:, c + TILES:c + TILES + P])
            dve.tensor_scalar(g.nws, g.nw, WS, None, ALU.mult)
            dve.wait_ge(tri, 3)
            dve.tensor_copy(g.ident16, g.ident)
            dve.wait_ge(shared_hi, 1)
            split_weights_low(dve, g, NE * WEXP, staged(g, NE), ALL_PARTS)


def tile_statistics(g, dve, t, stat):
    dve.bn_stats(g.stats[:, bass.ds(t * 6, 6)], g.x2[:, bass.ds(t * D, D)]).then_inc(stat, 1)


def mean_and_variance(g, dve, stat):
    dve.wait_ge(stat, TILES)
    for t in range(TILES):
        last = dve.bn_aggr(g.mv3[:, t], g.stats[:, t * 6:(t + 1) * 6])
    last.then_inc(stat, 1)
    dve.wait_ge(stat, TILES + 1)


def refined_rsqrt(dve, out, root, value, eps, tmp, then):
    then(dve.reciprocal(out, root))
    then(dve.tensor_tensor(tmp, out, out, ALU.mult))
    then(dve.scalar_tensor_tensor(out=tmp, in0=value, scalar=eps, in1=tmp, op0=ALU.add, op1=ALU.mult))
    then(dve.tensor_scalar(tmp, tmp, -0.5, 1.5, ALU.mult, ALU.add))
    then(dve.tensor_tensor(out, out, tmp, ALU.mult))


class GateWeights:

    def __init__(self, g, a, sem):
        self.g = g
        over = g.wf[:, KEPT * WEXP:NE * WEXP].bitcast(F32)
        self.raw = [over[:, r * 512:(r + 1) * 512] for r in range(4)]
        late, na = g.late.bitcast(F16), HEADS * GATE
        self.dst, o = {}, 0
        for what, n in (("a", na), ("v", D), ("o", D)):
            self.dst[what] = [late[:, o + l * KD * n:o + (l + 1) * KD * n].rearrange("p (k n) -> p k n", k=KD)
                              for l in range(2)]
            o += 2 * KD * n
        self.groups = [("a", n) for n in range(na // 256)] + [("v", 0), ("o", 0)]
        self.src = {"a": a["W_a"], "v": a["W_v"], "o": a["W_out"]}
        self.raw_in = [sem(f"gate_raw_in{r}") for r in range(4)]
        self.p_t, self.p_hi, self.p_lo = sem("gate_transposed"), sem("gate_high"), sem("gate_low")

    def load(self, sp, n):
        what, i = self.groups[n]
        if n >= 4:
            sp.wait_ge(self.p_t, n - 3)
        sp.dma_start(self.raw[n % 4].rearrange("p (s d) -> p s d", s=2),
                     self.src[what][i * 256:(i + 1) * 256].rearrange("(s p) d -> p s d", p=P)).then_inc(self.raw_in[n % 4], 16)

    def transpose(self, pe, n):
        pe.wait_ge(self.raw_in[n % 4], 16 * (n // 4 + 1))
        if n >= 6:
            pe.wait_ge(self.p_lo, n - 5)
        bank = self.g.psum[:, n % 6]
        for k in range(KD):
            for s in range(2):
                last = pe.transpose(bank[:, (k * 2 + s) * P:(k * 2 + s + 1) * P],
                                    self.raw[n % 4][:, s * D + k * P:s * D + (k + 1) * P], self.g.ident)
        last.then_inc(self.p_t, 1)

    def scale(self, n, k):
        return WS if self.groups[n][0] == "o" else self.g.nws[:, k:k + 1]

    def high(self, act, n):
        what, i = self.groups[n]
        act.wait_ge(self.p_t, n + 1)
        for k in range(KD):
            last = act.activation(self.dst[what][0][:, k, i * 256:(i + 1) * 256],
                                  self.g.psum[:, n % 6, k * 256:(k + 1) * 256], ACT.Copy, scale=self.scale(n, k))
        last.then_inc(self.p_hi, 1)

    def low(self, dve, n):
        what, i = self.groups[n]
        dve.wait_ge(self.p_hi, n + 1)
        for k in range(KD):
            last = dve.scalar_tensor_tensor(out=self.dst[what][1][:, k, i * 256:(i + 1) * 256],
                                            in0=self.g.psum[:, n % 6, k * 256:(k + 1) * 256], scalar=self.scale(n, k),
                                            in1=self.dst[what][0][:, k, i * 256:(i + 1) * 256],
                                            op0=ALU.mult, op1=ALU.subtract)
        last.then_inc(self.p_lo, 1)


def ffn(nc, g, tag, a, out):
    first, final = a is not None, out is not None
    early = 12 if first else 8
    with ExitStack() as ctx:
        def sem(n):
            return ctx.enter_context(nc.semaphore(f"{tag}_{n}"))

        w = g.work
        rows = [w[:, r * 512:(r + 1) * 512] for r in range(2)]
        xt = [w[:, 1024 + r * 512:1536 + r * 512].bitcast(F16).rearrange("p (l k t) -> p l k t", l=2, k=KD) for r in range(2)]
        hid = [w[:, 2048 + r * 512:2560 + r * 512] for r in range(2)]
        hb = [w[:, 4096 + r * 512:4608 + r * 512].bitcast(F16).rearrange("p (l c t) -> p l c t", l=2, c=2) for r in range(4)]
        yst = [g.late[:, 8192 + r * 512:8704 + r * 512] for r in range(2)]
        gat = [w[:, c:c + D] for c in [*range(0, 1024, D), *range(3072, 4096, D)]]
        spare = [[w, 0, 1024], [g.late, 8192, 9472], [w, 3072, 4096]]

        def temp(n):
            for s in spare:
                if s[1] + n <= s[2]:
                    s[1] += n
                    return s[0][:, s[1] - n:s[1]]
            raise ValueError("no room")

        logit, best, oh0, oh1 = temp(256), temp(256), temp(256), temp(256)
        besti = temp(256).bitcast(U32)
        chosen = temp(64)
        member = temp(128).bitcast(F16)
        cum, slot_of, prod = temp(256), temp(256), temp(256)
        fills = temp(NE * SHARED)
        ntile, tend, count = temp(NE), temp(NE), temp(NE)
        passed = temp(SPARSE * NE)
        ediff = temp(32)
        slot_f, slot_a, slot_b = (g.late[:, 9472 + n * PAIRS:9472 + (n + 1) * PAIRS] for n in range(3))
        lane_hot = [v.bitcast(F16).rearrange("p (c l) -> p c l", l=P) for v in (w[:, 0:1024], w[:, 3072:4096])]
        tile_hot = [g.late[:, 8192 + r * 640:8192 + r * 640 + CHUNK * SLOT_TILES // 2].bitcast(F16).rearrange(
            "p (c a) -> p c a", a=SLOT_TILES) for r in range(2)]
        logit3, best3, besti3 = (v.rearrange("p (t e) -> p t e", e=NE) for v in (logit, best, besti))
        chosen3 = chosen.rearrange("p (k t) -> p k t", k=2)
        cum3 = cum.rearrange("p (e t) -> p e t", e=NE)

        gp, up_, yp = (g.psum[:, 0:2], g.psum[:, 2:4], g.psum[:, 4:6])
        tp, rp = g.psum[:, 6], g.psum[:, 7]
        tbank = [b.bitcast(F16).rearrange("p (l k t) -> p l k t", l=2, k=KD) for b in (tp, g.psum[:, 4])]
        router_ps = rp[:, 0:256]

        def xn_part(n, l):
            return g.xn16[:, bass.ds(n * 4 * D, 4 * D)].rearrange("p (s l d) -> p s l d", s=2, l=2)[:, :, l]

        (stat, var_ok, std, r_rows, r_t, r_xt, r_hi, r_lo, r_mm, rt, diff_ok, e_ok, member_ok, rank_ok, slots_ok,
         lanes_ok, tiles_ok, inv_ok, tok_ok, xn_saved, t_done, xt_ok, up_done, tanh_ok, s_ok, hid_ok, h_hi, h_lo, dn_done, y_sh, y_sp,
         added) = map(sem, (
             "stat", "var_ok", "std", "r_rows", "r_t", "r_xt", "r_hi", "r_lo", "r_mm", "rt", "diff_ok", "e_ok",
             "member_ok", "rank_ok", "slots_ok", "lanes_ok", "tiles_ok", "inv_ok", "tok_ok", "xn_saved", "t_done", "xt_ok", "up_done",
             "tanh_ok", "s_ok", "hid_ok", "h_hi", "h_lo", "dn_done", "y_sh", "y_sp", "added"))
        if first:
            w_saved, scaled, split_hi, split_lo, new_stat = map(sem, ("w_saved", "scaled", "split_hi", "split_lo", "new_stat"))
            piece_in = [g.raw_in[NE - 1], g.raw_in[NE - 2]]
        else:
            w_back = sem("w_back")
        if final:
            stored = sem("stored")
        rows_sp = [sem("rows_sp0"), sem("rows_sp1")]
        y_out = [sem("y_out0"), sem("y_out1")]
        gat_in = g.gat_in

        def gathers_with(r):
            return len(range(r, PAIRS, GATHERS))

        piece = [w[:, 0:PART], g.late[:, 8192:8192 + PART]]
        n_whole, n_pieces = NE - KEPT, 3 * KEPT
        units = {item: [] for item in range(SHARED)}
        for n in range(n_whole):
            units[(0,1,2,4,5,6)[n]].append(("expert", NE - 1 - n))
        for n in range(n_pieces):
            units[7 + n // 2].append(("piece", n))
        in_turn = [u for item in range(SHARED) for u in units[item]]

        def unit(u):
            kind, n = u
            if kind == "expert":
                return in_turn.index(u), n * WEXP, staged(g, n), ALL_PARTS
            return in_turn.index(u), (KEPT - 1 - n // 3) * WEXP, piece[n % 2], ALL_PARTS[n % 3:n % 3 + 1]

        token_f = g.late[:, 9472:9472 + SLOT_TILES]

        def tile_one_hot(eng, c, n):
            j = c * CHUNK + n
            t = j % TILES
            return eng.tensor_scalar(tile_hot[c % 2][:, n], g.lanes[:, 0:SLOT_TILES], slot_a[:, j:j + 1],
                                     g.token[:, t:t + 1], ALU.is_equal, ALU.mult)

        block = ctx.enter_context(nc.Block())

        @block.tensor
        def _(pe):
            def transposes(src, bank, done):
                for l in range(2):
                    for k in range(KD):
                        for s in range(2):
                            last = pe.transpose(bank[:, l, k, s * P:(s + 1) * P], src((s * 2 + l) * D + k * P), g.ident16)
                last.then_inc(done, 1)

            def token_rows(n):
                return lambda c: g.xn16[:, bass.ds(n * 4 * D + c, P)]

            def router_rows(n, par):
                pe.wait_ge(r_lo, n + 1)
                if not (isinstance(n, int) and n < 2):
                    pe.wait_ge(r_xt, n - 1)
                transposes(token_rows(n), tbank[par], r_t)

            def router(n, par):
                pe.wait_ge(r_xt, n + 1)
                for s in range(2):
                    col = n * 2 * NE + s * NE
                    i = 0
                    for k in range(KD):
                        for lx, lw in ((0, 0), (0, 1), (1, 0)):
                            last = pe.matmul(router_ps[:, bass.ds(col, NE)], xt[par][:, lx, k, s * P:(s + 1) * P],
                                             g.rw[:, lw, k], start=(i == 0), stop=(i == 5))
                            i += 1
                last.then_inc(r_mm, 1)

            router_rows(0, 0)
            router_rows(1, 1)
            with pe.Fori(0, SHARED // 2 - 1) as q:
                router(2 * q, 0)
                router_rows(2 * q + 2, 0)
                router(2 * q + 1, 1)
                router_rows(2 * q + 3, 1)
            router(SHARED - 2, 0)
            router(SHARED - 1, 1)

            def ranks():
                pe.wait_ge(member_ok, 1)
                pe.matmul(rp[:, 0:256], g.before, member, start=True, stop=True)
                pe.matmul(rp[:, 256:512], g.ones, member, start=True, stop=True).then_inc(rank_ok, 1)

            def tokens_of_slots(c):
                pe.wait_ge(lanes_ok, c + 1)
                pe.wait_ge(tiles_ok, c + 1)
                for n in range(CHUNK):
                    last = pe.matmul(rp[:, 0:SLOT_TILES], lane_hot[c % 2][:, n], tile_hot[c % 2][:, n],
                                     start=(c == 0 and n == 0), stop=((c + 1) * CHUNK == PAIRS and n == CHUNK - 1),
                                     skip_group_check=True)
                last.then_inc(inv_ok, 1)

            def shared_rows(gi, n):
                if not (isinstance(gi, int) and gi == 0):
                    pe.wait_ge(xt_ok, gi)
                transposes(token_rows(n), tbank[0], t_done)

            def sparse_rows(gi, half, par):
                pe.wait_ge(rows_sp[par], 32 * (half - early // 2) + 32)
                pe.wait_ge(xt_ok, gi)
                transposes(lambda c: rows[par].bitcast(F16)[:, c:c + P], tbank[0], t_done)

            def up(gi, par, h, wbase):
                m = 2 * gi + h
                if h == 0:
                    pe.wait_ge(xt_ok, gi + 1)
                if not (isinstance(gi, int) and gi == 0):
                    pe.wait_ge(hid_ok, m - 1)
                for ps, o_hi, o_lo in ((gp, O1H, O1L), (up_, O3H, O3L)):
                    for c in range(2):
                        i = 0
                        for k in range(KD):
                            for lx, o in ((0, o_hi), (0, o_lo), (1, o_hi)):
                                off = o + k * HID + (2 * h + c) * P
                                last = pe.matmul(ps[:, h, c * ITEM:(c + 1) * ITEM], g.wf[:, bass.ds(wbase + off, P)],
                                                 xt[par][:, lx, k], start=(i == 0), stop=(i == 5))
                                i += 1
                last.then_inc(up_done, 1)

            def down(gi, par, h, wbase):
                m = 2 * gi + h
                pe.wait_ge(h_lo, m + 1)
                i = 0
                for c in range(2):
                    for lh, o in ((0, O2H), (0, O2L), (1, O2H)):
                        for s in range(2):
                            off = o + (2 * h + c) * D
                            last = pe.matmul(yp[:, par, s * D:(s + 1) * D],
                                             hb[2 * par + h][:, lh, c, s * P:(s + 1) * P],
                                             g.wf[:, bass.ds(wbase + off, D)],
                                             start=(h == 0 and i == 0), stop=(h == 1 and c == 1 and lh == 1),
                                             skip_group_check=True)
                            i += 1
                last.then_inc(dn_done, 1)

            def item(gi, par, wu, wd, rows_next, y_free):
                up(gi, par, 0, wu)
                rows_next()
                if wd is not None:
                    y_free()
                    down(gi - 1, 1 - par, 0, wd)
                up(gi, par, 1, wu)
                if wd is not None:
                    down(gi - 1, 1 - par, 1, wd)

            ws = NE * WEXP
            nothing = lambda: None
            shared_rows(0, 0)
            item(0, 0, ws, None, lambda: shared_rows(1, 1), nothing)
            item(1, 1, ws, ws, lambda: shared_rows(2, 2), nothing)
            ranks()
            item(2, 0, ws, ws, lambda: shared_rows(3, 3), nothing)
            for n in range(3, 7):
                item(n, n % 2, ws, ws, lambda: shared_rows(n + 1, n + 1), lambda: pe.wait_ge(y_sh, n - 2))
                if n >= 5:
                    tokens_of_slots(2 * (n - 5))
                    tokens_of_slots(2 * (n - 5) + 1)
            if early > 8:
                with pe.Fori(0, (early - 8) // 2) as q:
                    m, n = 2 * q + 7, 2 * q + 8
                    item(m, 1, ws, ws, lambda: shared_rows(m + 1, m + 1), lambda: pe.wait_ge(y_sh, m - 2))
                    item(n, 0, ws, ws, lambda: shared_rows(n + 1, n + 1), lambda: pe.wait_ge(y_sh, n - 2))
            gi = early - 1
            item(gi, 1, ws, ws, lambda: sparse_rows(early, early // 2, 0), lambda: pe.wait_ge(y_sh, gi - 2))

            reg = [pe.alloc_register(f"{tag}_expert{r}") for r in range(2)]

            def load_expert(n, par):
                pe.reg_load(reg[par], g.texp[0:1, bass.ds(n, 1)])

            def expert(par):
                return pe.snap(reg[par], min_val=0, max_val=NE - 1) * WEXP

            pe.wait_ge(slots_ok, 1)
            if first:
                pe.wait_ge(split_lo, len(in_turn))
            else:
                pe.wait_ge(w_back, 16)
            load_expert(0, 0)
            before = ws
            for n in range(3):
                gi, par = early + n, n % 2
                cur = expert(par)

                def ahead():
                    sparse_rows(gi + 1, (gi + 1) // 2, 1 - par)
                    load_expert(n + 1, 1 - par)

                item(gi, par, cur, before, ahead, lambda: pe.wait_ge(y_sh, gi - 2))
                before = cur
            with pe.Fori(0, (SPARSE - 5) // 2) as q:
                n = 2 * q + 3
                gi = early + n
                before, cur = expert(0), expert(1)

                def ahead_of_even():
                    sparse_rows(gi + 1, q + early // 2 + 2, 0)
                    load_expert(n + 1, 0)

                def ahead_of_odd():
                    sparse_rows(gi + 2, q + early // 2 + 2, 1)
                    load_expert(n + 2, 1)

                item(gi, 1, cur, before, ahead_of_even, lambda: pe.wait_ge(y_sp, n - 2))
                item(gi + 1, 0, expert(0), cur, ahead_of_odd, lambda: pe.wait_ge(y_sp, n - 1))
            n, gi = SPARSE - 2, early + SPARSE - 2
            before, cur = expert(0), expert(1)

            def ahead_of_last():
                sparse_rows(gi + 1, (gi + 1) // 2, 0)
                load_expert(n + 1, 0)

            item(gi, 1, cur, before, ahead_of_last, lambda: pe.wait_ge(y_sp, n - 2))
            last_e = expert(0)
            g0 = gi + 2
            item(gi + 1, 0, last_e, cur, lambda: shared_rows(g0, early), lambda: pe.wait_ge(y_sp, n - 1))
            item(g0, 1, ws, last_e, lambda: shared_rows(g0 + 1, early + 1), lambda: pe.wait_ge(y_sp, n))
            item(g0 + 1, 0, ws, ws, lambda: shared_rows(g0 + 2, early + 2), lambda: pe.wait_ge(y_sp, n + 1))
            item(g0 + 2, 1, ws, ws, lambda: shared_rows(g0 + 3, early + 3), lambda: pe.wait_ge(y_sp, n + 2))
            for m in range(3, SHARED - early - 1):
                item(g0 + m, 1 - m % 2, ws, ws, lambda: shared_rows(g0 + m + 1, early + m + 1),
                     lambda: pe.wait_ge(y_sh, early + m - 2))
            m = SHARED - early - 1
            item(g0 + m, 0, ws, ws, nothing, lambda: pe.wait_ge(y_sh, early + m - 2))
            pe.wait_ge(y_sh, early + m - 1)
            down(g0 + m, 0, 0, ws)
            down(g0 + m, 0, 1, ws)
            if first:
                pe.wait_ge(hid_ok, 2 * (SHARED + SPARSE))
                pe.wait_ge(y_sh, SHARED)
                for n in range(len(g.gates.groups)):
                    g.gates.transpose(pe, n)

        @block.scalar
        def _(act):
            act.wait_ge(var_ok, 1)
            act.activation(g.std, g.mv3[:, :, 1], ACT.Sqrt, bias=g.eps, scale=1.0).then_inc(std, 1)

            def router(n, par):
                act.wait_ge(r_t, n + 1)
                if not (isinstance(n, int) and n < 2):
                    act.wait_ge(r_mm, n - 1)
                act.activation(xt[par].rearrange("p l k t -> p (l k t)"), tbank[par].rearrange("p l k t -> p (l k t)"),
                               ACT.Copy).then_inc(r_xt, 1)

            def row_high(n, par):
                act.wait_ge(r_rows, n + 1)
                act.activation(xn_part(n, 0), hid[par].rearrange("p (s d) -> p s d", s=2), ACT.Copy).then_inc(r_hi, 1)

            row_high(0, 0)
            row_high(1, 1)
            router(0, 0)
            row_high(2, 0)
            router(1, 1)
            row_high(3, 1)
            with act.Fori(1, SHARED // 2 - 1) as q:
                router(2 * q, 0)
                row_high(2 * q + 2, 0)
                router(2 * q + 1, 1)
                row_high(2 * q + 3, 1)
            router(SHARED - 2, 0)
            router(SHARED - 1, 1)
            def split(u):
                n, base, raw, parts = unit(u)
                if u[0] == "expert":
                    act.wait_ge(g.raw_in[u[1]], 48)
                    if u[1] + 2 < NE:
                        act.wait_ge(split_lo, in_turn.index(("expert", u[1] + 2)) + 1)
                else:
                    act.wait_ge(piece_in[u[1] % 2], 48 + 16 * (u[1] // 2 + 1))
                    if u[1] % 3 == 0:
                        act.wait_ge(split_lo, in_turn.index(("expert", KEPT - 1 - u[1] // 3 + 2)) + 1)
                scale_weights(act, raw, parts).then_inc(scaled, 1)
                act.wait_ge(scaled, n + 1)
                split_scaled(act, None, g, base, raw, parts, True).then_inc(split_hi, 1)

            def x_high(gi, par, last_up):
                act.wait_ge(t_done, gi + 1)
                if last_up is not None:
                    act.wait_ge(up_done, last_up)
                act.activation(xt[par].rearrange("p l k t -> p (l k t)"), tbank[0].rearrange("p l k t -> p (l k t)"),
                               ACT.Copy).then_inc(xt_ok, 1)

            def half(gi, par, h):
                m = 2 * gi + h
                act.wait_ge(up_done, m + 1)
                if not (isinstance(gi, int) and gi == 0):
                    act.wait_ge(h_lo, m - 1)
                act.activation(hid[h], gp[:, h], ACT.Tanh, scale=0.5 / WS).then_inc(tanh_ok, 1)

            def hid_high(gi, par, h):
                m = 2 * gi + h
                act.wait_ge(hid_ok, m + 1)
                if not (isinstance(gi, int) and gi < 2):
                    act.wait_ge(dn_done, m - 3)
                act.activation(hb[2 * par + h][:, 0].rearrange("p c t -> p (c t)"), hid[h], ACT.Copy).then_inc(h_hi, 1)

            def item(gi, par, nxt, y_copy):
                half(gi, par, 0)
                if nxt:
                    x_high(gi + 1, 1 - par, None if isinstance(gi, int) and gi == 0 else 2 * gi)
                hid_high(gi, par, 0)
                half(gi, par, 1)
                hid_high(gi, par, 1)
                y_copy()

            def y_stage(gi, par, n, first):
                act.wait_ge(dn_done, 2 * gi + 2)
                if not first:
                    act.wait_ge(y_out[par], first_free(n))
                act.activation(yst[par], yp[:, par], ACT.Copy).then_inc(y_sp, 1)

            def first_free(nh):
                return 16 * nh

            nothing = lambda: None
            x_high(0, 0, None)
            for n in range(2):
                item(n, n, True, nothing)
                for u in units[n] if first else []:
                    split(u)
            act.wait_ge(diff_ok, 1)
            act.activation(ediff, ediff, ACT.Exp).then_inc(e_ok, 1)
            if first:
                for n in range(2, early):
                    item(n, n % 2, True, nothing)
                    for u in units[n]:
                        split(u)
            else:
                with act.Fori(1, early // 2) as q:
                    item(2 * q, 0, True, nothing)
                    item(2 * q + 1, 1, True, nothing)
            gi = early
            item(gi, 0, True, nothing)
            item(gi + 1, 1, True, lambda: y_stage(gi, 0, 0, True))
            item(gi + 2, 0, True, lambda: y_stage(gi + 1, 1, 0, True))
            with act.Fori(0, (SPARSE - 3) // 2) as q:
                b = early + 2 * q + 3
                item(b, 1, True, lambda: y_stage(b - 1, 0, q + 1, False))
                item(b + 1, 0, True, lambda: y_stage(b, 1, q + 1, False))
            gi = early + SPARSE
            item(gi, 1, True, lambda: y_stage(gi - 1, 0, SPARSE // 2, False))
            for m in range(1, SHARED - early):
                item(gi + m, 1 - m % 2, m < SHARED - early - 1, nothing)
            if first:
                act.wait_ge(t_done, SHARED + SPARSE)
                act.wait_ge(y_out[0], 16 * (SPARSE // 2 + 1))
                act.wait_ge(y_out[1], 16 * (SPARSE // 2))
                for n in range(len(g.gates.groups)):
                    g.gates.high(act, n)

        @block.vector
        def _(dve):
            if first:
                with dve.Fori(0, TILES // 8) as q:
                    for n in range(8):
                        tile_statistics(g, dve, 8 * q + n, stat)
                mean_and_variance(g, dve, stat)
            dve.engine_nop().then_inc(var_ok, 1)
            chain = [0]

            def then(ins):
                ins.then_inc(rt, 1)
                chain[0] += 1
                dve.wait_ge(rt, chain[0])

            dve.wait_ge(std, 1)
            refined_rsqrt(dve, g.rstd, g.std, g.mv3[:, :, 1], EPS, g.ms, then)

            def normalise(n, par):
                for s in range(2):
                    t = 2 * n + s
                    last = dve.tensor_scalar(hid[par][:, s * D:(s + 1) * D], g.x2[:, bass.ds(t * D, D)],
                                             g.mv[:, bass.ds(2 * t, 1)], g.rstd[:, bass.ds(t, 1)], ALU.subtract, ALU.mult)
                last.then_inc(r_rows, 1)

            def row_low(n, par):
                dve.wait_ge(r_hi, n + 1)
                dve.tensor_tensor(xn_part(n, 1), hid[par].rearrange("p (s d) -> p s d", s=2), xn_part(n, 0),
                                  ALU.subtract).then_inc(r_lo, 1)

            normalise(0, 0)
            normalise(1, 1)
            with dve.Fori(0, SHARED // 2 - 1) as q:
                for u in range(2):
                    row_low(2 * q + u, u)
                    dve.wait_ge(r_lo, 2 * q + u + 1)
                    normalise(2 * q + u + 2, u)
            row_low(SHARED - 2, 0)
            row_low(SHARED - 1, 1)

            def best_logits():
                dve.wait_ge(r_mm, SHARED)
                then(dve.scalar_tensor_tensor(out=logit3, in0=router_ps.rearrange("p (t e) -> p t e", e=NE), scalar=1.0 / WS,
                                              in1=g.bias.unsqueeze(1).broadcast_to((P, TILES, NE)), op0=ALU.mult, op1=ALU.add))
                for t in range(TILES):
                    last = dve.max(best3[:, t], logit3[:, t])
                then(last)

            def best_experts():
                for t in range(TILES):
                    last = dve.max_index(besti3[:, t], best3[:, t], logit3[:, t])
                then(last)
                dve.tensor_tensor(ediff, best3[:, :, 1], best3[:, :, 0], ALU.subtract).then_inc(diff_ok, 1)

            def members():
                then(dve.tensor_copy(chosen3, besti3[:, :, 0:2].rearrange("p t k -> p k t")))
                iota_e = g.iota[:, 0:NE].unsqueeze(1).broadcast_to((P, TILES, NE))
                for k, oh in ((0, oh0), (1, oh1)):
                    then(dve.tensor_tensor(oh.rearrange("p (t e) -> p t e", e=NE), iota_e,
                                           chosen3[:, k].unsqueeze(2).broadcast_to((P, TILES, NE)), ALU.is_equal))
                dve.tensor_tensor(member, oh0, oh1, ALU.add).then_inc(member_ok, 1)

            def shares():
                dve.wait_ge(e_ok, 1)
                then(dve.tensor_scalar(slot_f[:, 0:TILES], ediff, 1.0, None, ALU.add))
                then(dve.reciprocal(slot_f[:, 32:32 + TILES], slot_f[:, 0:TILES]))
                then(dve.tensor_scalar(g.cw[:, 0:TILES], slot_f[:, 32:32 + TILES], 0.5 / (WS * AS), None, ALU.mult))
                then(dve.tensor_tensor(g.cw[:, TILES:2 * TILES], g.cw[:, 0:TILES], ediff, ALU.mult))

            def counts():
                dve.wait_ge(rank_ok, 1)
                tot3 = rp[:, 256:512].rearrange("p (t e) -> p e t", e=NE)
                then(dve.memset(prod[:, 0:TILES], 0.0))
                for e in range(NE):
                    last = dve.tensor_tensor_scan(cum3[:, e], tot3[:, e], prod[:, 0:TILES], 0.0, ALU.add, ALU.add)
                then(last)
                then(dve.tensor_copy(count, cum3[:, :, TILES - 1]))
                fills3 = fills.rearrange("p (e j) -> p e j", e=NE)
                then(dve.tensor_tensor(fills3, count.unsqueeze(2).broadcast_to((P, NE, SHARED)),
                                       g.iota[:, NE:NE + SHARED].unsqueeze(1).broadcast_to((P, NE, SHARED)), ALU.is_gt))
                then(dve.tensor_reduce(ntile, fills3, AX.X, ALU.add))
                then(dve.tensor_tensor_scan(tend, ntile, prod[:, 0:NE], 0.0, ALU.add, ALU.add))
                then(dve.tensor_tensor(count, tend, ntile, ALU.subtract))

            def slots():
                slot3 = slot_of.rearrange("p (t e) -> p t e", e=NE)
                then(dve.tensor_tensor(slot3, cum3.rearrange("p e t -> p t e"), rp[:, 256:512].rearrange("p (t e) -> p t e", e=NE), ALU.subtract))
                then(dve.tensor_tensor(slot3, slot3, rp[:, 0:256].rearrange("p (t e) -> p t e", e=NE), ALU.add))
                then(dve.scalar_tensor_tensor(out=slot3, in0=count.unsqueeze(1).broadcast_to((P, TILES, NE)), scalar=float(ITEM),
                                              in1=slot3, op0=ALU.mult, op1=ALU.add))
                for k, oh in ((0, oh0), (1, oh1)):
                    then(dve.tensor_tensor(prod, oh, slot_of, ALU.mult))
                    then(dve.tensor_reduce(slot_f[:, k * TILES:(k + 1) * TILES], prod.rearrange("p (t e) -> p t e", e=NE), AX.X, ALU.add))
                then(dve.tensor_copy(g.slot, slot_f))

            def tiles():
                passed3 = passed.rearrange("p (n e) -> p n e", e=NE)
                then(dve.tensor_tensor(passed3, g.iota[:, NE + SHARED:].unsqueeze(2).broadcast_to((P, SPARSE, NE)),
                                       tend.unsqueeze(1).broadcast_to((P, SPARSE, NE)), ALU.is_ge))
                then(dve.tensor_reduce(prod[:, 0:SPARSE], passed3, AX.X, ALU.add))
                then(dve.tensor_scalar(g.texp, prod[:, 0:SPARSE], NE - 1.0, None, ALU.min))

            def places():
                then(dve.tensor_scalar(slot_a, slot_f, 1.0 / P, 0.5 - 0.5 / P, ALU.mult, ALU.subtract))
                then(dve.tensor_scalar(slot_a, slot_a, 12582912.0, None, ALU.add))
                then(dve.tensor_scalar(slot_a, slot_a, 12582912.0, None, ALU.subtract))
                then(dve.scalar_tensor_tensor(out=slot_b, in0=slot_a, scalar=-float(P), in1=slot_f, op0=ALU.mult, op1=ALU.add))
                dve.engine_nop().then_inc(slots_ok, 1)

            def one_hots(c):
                if c >= 2:
                    dve.wait_ge(inv_ok, c - 1)
                for n in range(CHUNK):
                    j = c * CHUNK + n
                    last = dve.tensor_scalar(lane_hot[c % 2][:, n], g.lanes, slot_b[:, j:j + 1], None, ALU.is_equal)
                    if n % BY_VECTOR == 0:
                        last = tile_one_hot(dve, c, n)
                last.then_inc(lanes_ok, 1)

            def decode():
                dve.wait_ge(inv_ok, PAIRS // CHUNK)
                then(dve.tensor_scalar(token_f, rp[:, 0:SLOT_TILES], BATCH * TIME / 2.0, None, ALU.add))
                then(dve.tensor_copy(g.tok, token_f))
                dve.engine_nop().then_inc(tok_ok, 1)

            def half(gi, par, h):
                m = 2 * gi + h
                dve.wait_ge(tanh_ok, m + 1)
                dve.scalar_tensor_tensor(out=hid[h], in0=hid[h], scalar=1.0, in1=gp[:, h], op0=ALU.add, op1=ALU.mult).then_inc(s_ok, 1)
                dve.wait_ge(s_ok, m + 1)
                dve.scalar_tensor_tensor(out=hid[h], in0=hid[h], scalar=AS / (2 * WS * WS), in1=up_[:, h],
                                         op0=ALU.mult, op1=ALU.mult).then_inc(hid_ok, 1)

            def hid_low(gi, par, h):
                m = 2 * gi + h
                dve.wait_ge(h_hi, m + 1)
                dve.tensor_tensor(hb[2 * par + h][:, 1].rearrange("p c t -> p (c t)"), hid[h],
                                  hb[2 * par + h][:, 0].rearrange("p c t -> p (c t)"), ALU.subtract).then_inc(h_lo, 1)

            def add_y(gi, n, par):
                dve.wait_ge(dn_done, 2 * gi + 2)
                xs = g.x2[:, bass.ds(n * 2 * D, 2 * D)]
                dve.scalar_tensor_tensor(out=xs, in0=yp[:, par], scalar=0.5 / (WS * AS), in1=xs,
                                         op0=ALU.mult, op1=ALU.add).then_inc(y_sh, 1)

            def item(gi, par, add, extra=(None, None)):
                half(gi, par, 0)
                hid_low(gi, par, 0)
                if extra[0]:
                    extra[0]()
                half(gi, par, 1)
                hid_low(gi, par, 1)
                if add is not None:
                    add_y(gi - 1, add, 1 - par)
                if extra[1]:
                    extra[1]()

            item(0, 0, None, (best_logits, best_experts))
            item(1, 1, 0, (members, None))
            item(2, 0, 1, (shares, counts))
            item(3, 1, 2, (slots, tiles))
            places()
            item(4, 0, 3, (lambda: one_hots(0), lambda: one_hots(1)))
            item(5, 1, 4, (None, lambda: one_hots(2)))
            item(6, 0, 5, (lambda: one_hots(3), decode))
            item(7, 1, 6)
            if early > 8:
                with dve.Fori(4, early // 2) as q:
                    item(2 * q, 0, 2 * q - 1)
                    item(2 * q + 1, 1, 2 * q)
            item(early, 0, early - 1)
            with dve.Fori(0, (SPARSE - 1) // 2) as q:
                b = early + 2 * q + 1
                item(b, 1, None)
                item(b + 1, 0, None)

            def combine(t):
                for k in range(2):
                    n = 2 * t + k
                    r = n % GATHERS
                    earlier = n // GATHERS + (0 if first else gathers_with(r))
                    dve.wait_ge(gat_in[r], 16 * earlier + 16)
                    xs = g.x2[:, t * D:(t + 1) * D]
                    if k == 1:
                        dve.wait_ge(added, n)
                    dve.scalar_tensor_tensor(out=xs, in0=gat[r], scalar=g.cw[:, t + k * TILES:t + k * TILES + 1], in1=xs,
                                             op0=ALU.mult, op1=ALU.add).then_inc(added, 1)
                if first:
                    dve.wait_ge(added, 2 * t + 2)
                    tile_statistics(g, dve, t, new_stat)

            b, per_item = early + SPARSE, 3 if first else 4
            item(b, 1, None)
            for m in range(1, SHARED - early):
                item(b + m, 1 - m % 2, early + m - 1)
                for t in range(per_item * (m - 1), per_item * m):
                    combine(t)
            add_y(b + SHARED - early - 1, SHARED - 1, 0)
            groups_done = 0
            for t in range(per_item * (SHARED - early - 1), TILES):
                combine(t)
                if first and groups_done < len(g.gates.groups):
                    g.gates.low(dve, groups_done)
                    groups_done += 1
            if first:
                mean_and_variance(g, dve, new_stat)

        @block.gpsimd
        def _(pool):
            def split(u):
                n, base, raw, parts = unit(u)
                pool.wait_ge(split_hi, n + 1)
                split_scaled(None, pool, g, base, raw, parts, False).then_inc(split_lo, 1)

            before_slots = 3
            if first:
                for u in in_turn[:before_slots]:
                    split(u)
            pool.wait_ge(slots_ok, 1)
            for c in range(PAIRS // CHUNK):
                if c >= 2:
                    pool.wait_ge(inv_ok, c - 1)
                for n in [n for n in range(CHUNK) if n % BY_VECTOR]:
                    last = tile_one_hot(pool, c, n)
                last.then_inc(tiles_ok, 1)
            if first:
                for u in in_turn[before_slots:]:
                    split(u)
                pool.wait_ge(split_lo, len(in_turn))
            pool.wait_ge(tok_ok, 1)
            pool.wait_ge(xn_saved, 16)
            for n in range(SPARSE):
                if n >= 2:
                    pool.wait_ge(t_done, early + n - 1)
                for s in range(2):
                    c = 2 * n + s
                    pool.indirect_dma_start(rows[n % 2][:, s * D:(s + 1) * D], None, g.xn_dram,
                                            bass.IndirectOffsetOnAxis(ap=g.tok[:, c:c + 1], axis=0)).then_inc(rows_sp[n % 2], 16)
            pool.wait_ge(y_out[0], 16 * (SPARSE // 2 + 1))
            pool.wait_ge(y_out[1], 16 * (SPARSE // 2))
            for t in range(TILES):
                for k in range(2):
                    n = 2 * t + k
                    r = n % GATHERS
                    if n >= GATHERS:
                        pool.wait_ge(added, n - GATHERS + 1)
                    pool.indirect_dma_start(gat[r], None, g.outs,
                                            bass.IndirectOffsetOnAxis(ap=g.slot[:, k * TILES + t:k * TILES + t + 1], axis=0)
                                            ).then_inc(gat_in[r], 16)

        @block.sync
        def _(sp):
            sp.wait_ge(r_lo, SHARED)
            sp.dma_start(g.xn_dram.rearrange("(t p) d -> p t d", p=P),
                         g.xn.rearrange("p (t d) -> p t d", d=D)).then_inc(xn_saved, 16)
            if first:
                sp.wait_ge(inv_ok, PAIRS // CHUNK)
                for n in range(n_pieces):
                    if n >= 2:
                        sp.wait_ge(split_lo, in_turn.index(("piece", n - 2)) + 1)
                    load_weight(sp, a, KEPT - 1 - n // 3, n % 3, piece[n % 2], piece_in[n % 2])
                sp.wait_ge(split_lo, len(in_turn))
            else:
                sp.dma_start(g.wf[:, KEPT * WEXP:NE * WEXP], g.w_dram).then_inc(w_back, 16)

            def store(n, par):
                start = sp.snap(n * ITEM)
                sp.wait_ge(y_sp, n + 1)
                sp.dma_start(g.outs[bass.ds(start, ITEM)].rearrange("(s p) d -> p s d", p=P),
                             yst[par].rearrange("p (s d) -> p s d", s=2)).then_inc(y_out[par], 16)

            loops = (SPARSE - 3) // 2
            with sp.Fori(0, loops) as q:
                store(2 * q, 0)
                store(2 * q + 1, 1)
                if first:
                    bit = (NE - KEPT) * WEXP // loops
                    sp.dma_start(g.w_dram[:, bass.ds(q * bit, bit)],
                                 g.wf[:, bass.ds(q * bit + KEPT * WEXP, bit)]).then_inc(w_saved, 16)
            store(SPARSE - 3, 0)
            store(SPARSE - 2, 1)
            store(SPARSE - 1, 0)
            if first:
                sp.wait_ge(w_saved, 16 * loops)
                sp.wait_ge(dn_done, 2 * (early + SPARSE))
                for n in range(len(g.gates.groups)):
                    g.gates.load(sp, n)
            if final:
                sp.wait_ge(y_sh, SHARED)
                per_round = ROUND
                for r in range(TILES // per_round):
                    sp.wait_ge(added, 2 * per_round * (r + 1))
                    for b in range(BATCH):
                        t0 = r * per_round * STEPS
                        sp.dma_start(out[b, t0:t0 + per_round * STEPS].rearrange("(n t) d -> t n d", t=STEPS),
                                     g.x[b * STEPS:(b + 1) * STEPS, r * per_round:(r + 1) * per_round]).then_inc(stored, 16)
                sp.wait_ge(stored, 16 * BATCH * (TILES // per_round))


MAX_PARTS = 2
SPECIAL = {5: ("low_next", 0), 11: ("invert", 0), 12: ("times_v", 0), 19: ("invert", 1), 20: ("times_v", 1), 27: ("invert", 2), 28: ("times_v", 2), 31: ("out_low", 0), 35: ("invert", 3), 36: ("times_v", 3), 37: ("add_out", 0)}
FREE = [place for place in range(47) if place not in SPECIAL]
FILLERS = dict(SPECIAL)
FILLERS.update({FREE[n * len(FREE) // (HEADS * MAX_PARTS)]: ("maximum", n) for n in range(HEADS * MAX_PARTS)})


def attention(nc, g, a):
    with ExitStack() as ctx:
        def sem(n):
            return ctx.enter_context(nc.semaphore(f"att_{n}"))

        w = g.work
        at = [0]

        def take(n):
            at[0] += n
            assert at[0] <= g.work_words
            return w[:, at[0] - n:at[0]]

        hrow = [take(D) for _ in range(2)]
        ht = [take(D).bitcast(F16).rearrange("p (l k t) -> p l k t", l=2, k=KD) for _ in range(2)]
        vs = [take(D) for _ in range(2)]
        mx = [take(D) for _ in range(2)]
        tree = take(64 * 8).rearrange("p (g c) -> p g c", c=8)
        zsum = take(D)
        dots = take(M)
        state = [take(STEPS * M).rearrange("p (t j) -> p t j", j=M) for _ in range(2)]
        yc = take(D)
        ho = take(D)
        ot = take(D).bitcast(F16).rearrange("p (l k t) -> p l k t", l=2, k=KD)
        over = g.wf[:, KEPT * WEXP:NE * WEXP].bitcast(F32)
        n_e = HEADS * ROW
        gate = [over[:, r * n_e:(r + 1) * n_e].rearrange("p (h c) -> p h c", h=HEADS) for r in range(2)]
        step_g = [over[:, (2 + r) * n_e:(3 + r) * n_e].rearrange("p (t c) -> p t c", t=STEPS) for r in range(2)]
        wa, wv, wo = g.gates.dst["a"], g.gates.dst["v"], g.gates.dst["o"]
        lp = [g.psum[:, 2 * r:2 * r + 2] for r in range(3)]
        tp, vo = g.psum[:, 6], g.psum[:, 7]
        v_ps, o_ps = vo[:, 0:D], vo[:, D:2 * D]
        tph, tpo = tp[:, 0:D], tp[:, D:2 * D]
        (stat, var_ok, std, rc, ms_ok, scales_ok, rms, h_ok, x_ok, ht_ps, ht_hi, ht_lo, v_ok,
         v_sb, l_ps, l_ev, mx_ok, sub_ok, ex_ok, z_ok, tr, zr_ok, sc, yc_ok, ot_ps, ot_hi,
         ot_lo, o_ok, x_add) = map(sem, (
             "stat", "var_ok", "std", "rc", "ms_ok", "scales_ok", "rms", "h_ok", "x_ok", "ht_ps",
             "ht_hi", "ht_lo", "v_ok", "v_sb", "l_ps", "l_ev", "mx_ok", "sub_ok", "ex_ok", "z_ok", "tr",
             "zr_ok", "sc", "yc_ok", "ot_ps", "ot_hi", "ot_lo", "o_ok", "x_add"))
        g_out = [[sem(f"g_out{r}_{j}") for j in range(4)] for r in range(2)]
        g_in = [sem("g_in0"), sem("g_in1")]
        y_out, y_in = sem("y_out"), sem("y_in")
        block = ctx.enter_context(nc.Block())

        LAG_R, LAG_S, LAG_O = 1, 3, 4

        def iterations(eng, body):
            for it in range(LAG_O):
                body(it, it // 2, it % 2)
            with eng.Fori(LAG_O // 2, TILES // 2 - 1) as q:
                body(2 * q, q, 0)
                body(2 * q + 1, q, 1)
            for it in range(TILES - 2, TILES + LAG_O):
                body(it, it // 2, it % 2)

        def on(it, lag):
            return not isinstance(it, int) or 0 <= it - lag < TILES

        def ahead(it):
            return not isinstance(it, int) or it + 1 < TILES

        def by_vector(it):
            return isinstance(it, int) and it < LAG_S

        def subtract_maxima(eng, it, par, j):
            eng.wait_ge(mx_ok, (4 * it + j + 1) * 4 * MAX_PARTS)
            e = gate[par][:, 4 * j:4 * j + 4, 0:GATE].rearrange("p h (i j) -> p h i j", j=M + 1)
            m = mx[par][:, 64 * j:64 * j + 64].rearrange("p (h i) -> p h i", h=4)
            eng.tensor_tensor(e, e, m.unsqueeze(3).broadcast_to((P, 4, M, M + 1)), ALU.subtract).then_inc(sub_ok, 1)

        @block.sync
        def _(sp):
            def body(it, q, par):
                if on(it, LAG_O):
                    k = it - LAG_O
                    read_back = 16 * BATCH * it - 16 * BATCH * LAG_O
                    sp.wait_ge(yc_ok, k + 1)
                    if not (isinstance(it, int) and k == 0):
                        sp.wait_ge(y_in, read_back)
                    sp.dma_start(g.y_dram, yc).then_inc(y_out, 16)
                    sp.wait_ge(y_out, 16 * k + 16)
                    if not (isinstance(it, int) and k == 0):
                        sp.wait_ge(ot_ps, k)
                    for b in range(BATCH):
                        sp.dma_start(ho[b * STEPS:(b + 1) * STEPS].rearrange("p (h i) -> p h i", h=HEADS),
                                     g.y_dram[b * STEPS:(b + 1) * STEPS].rearrange("h (t i) -> t h i", i=M)).then_inc(y_in, 16)
                if on(it, LAG_R):
                    k, kpar = it - LAG_R, 1 - par
                    uses = q - (1 if par == 0 else 0)
                    read_back = 8 * BATCH * it - 8 * BATCH * (2 - par)
                    landed = 16 * uses + 16
                    if not (isinstance(it, int) and k < 2):
                        sp.wait_ge(g_in[kpar], read_back)
                    for j in range(4):
                        sp.wait_ge(zr_ok, 8 * it - (6 - 2 * j))
                        cols = slice(4 * j * ROW, 4 * (j + 1) * ROW)
                        sp.dma_start(g.g_dram[kpar][:, cols],
                                     gate[kpar].rearrange("p h c -> p (h c)")[:, cols]).then_inc(g_out[kpar][j], 16)
                    for j in range(4):
                        sp.wait_ge(g_out[kpar][j], landed)
                    if not (isinstance(it, int) and k < 2):
                        sp.wait_ge(sc, 3 * STEPS * (k - 1))
                    for b in range(BATCH):
                        sp.dma_start(step_g[kpar][b * STEPS:(b + 1) * STEPS],
                                     g.g_dram[kpar][b * STEPS:(b + 1) * STEPS].rearrange("t (h c) -> h t c", h=HEADS)
                                     ).then_inc(g_in[kpar], 16)

            iterations(sp, body)

        @block.tensor
        def _(pe):
            def h_transpose(k, par):
                pe.wait_ge(h_ok, k + 1)
                if not (isinstance(k, int) and k < 6):
                    pe.wait_ge(ot_lo, k - 5)
                for c in range(KD):
                    last = pe.transpose(tph[:, c * P:(c + 1) * P], hrow[par][:, c * P:(c + 1) * P], g.ident)
                last.then_inc(ht_ps, 1)

            def product(out, left, right):
                i = 0
                for k in range(KD):
                    for l, r in ((0, 0), (0, 1), (1, 0)):
                        last = pe.matmul(out, left[:, l, k], right[r][:, k], start=(i == 0), stop=(i == 5))
                        i += 1
                return last

            h_transpose(0, 0)

            def body(it, q, par):
                if on(it, 0):
                    pe.wait_ge(ht_lo, it + 1)
                    if not (isinstance(it, int) and it < 5):
                        pe.wait_ge(x_add, it - 4)
                    product(v_ps, ht[par], wv).then_inc(v_ok, 1)
                    if ahead(it):
                        h_transpose(it + 1, 1 - par)
                    for j in range(HEADS // 2):
                        slot = j % 3
                        done = it * 8 + j - (1 if j < 2 else 2)
                        if not (isinstance(done, int) and done < 1):
                            pe.wait_ge(l_ev, done)
                        for s in range(2):
                            h = 2 * j + s
                            last = product(lp[slot][:, s, 0:GATE], ht[par],
                                           [x[:, :, h * GATE:(h + 1) * GATE] for x in wa])
                        last.then_inc(l_ps, 1)
                if on(it, LAG_O):
                    k = it - LAG_O
                    pe.wait_ge(y_in, 16 * BATCH * (k + 1))
                    if isinstance(it, int) and it + 1 >= TILES:
                        pe.wait_ge(ht_lo, TILES)
                    else:
                        pe.wait_ge(ht_lo, it + 2)
                    for c in range(KD):
                        last = pe.transpose(tpo[:, c * P:(c + 1) * P], ho[:, c * P:(c + 1) * P], g.ident)
                    last.then_inc(ot_ps, 1)
                    pe.wait_ge(ot_lo, k + 1)
                    if isinstance(it, int) and it >= TILES:
                        pe.wait_ge(v_sb, TILES)
                    else:
                        pe.wait_ge(v_sb, it + 1)
                    product(o_ps, ot, wo).then_inc(o_ok, 1)

            iterations(pe, body)

        @block.scalar
        def _(act):
            act.wait_ge(var_ok, 1)
            act.activation(g.std, g.mv3[:, :, 1], ACT.Sqrt, bias=g.eps, scale=1.0).then_inc(std, 1)
            act.wait_ge(ms_ok, 1)
            act.activation(g.rms, g.ms, ACT.Sqrt, bias=g.eps, scale=1.0).then_inc(rms, 1)

            def h_high(k, par):
                act.wait_ge(ht_ps, k + 1)
                if not (isinstance(k, int) and k < 2):
                    act.wait_ge(l_ps, 8 * k - 8)
                act.activation(ht[par][:, 0].rearrange("p k t -> p (k t)"), tph, ACT.Copy).then_inc(ht_hi, 1)

            def h_row(k, par):
                if not (isinstance(k, int) and k < 2):
                    act.wait_ge(ht_ps, k - 1)
                act.activation(hrow[par], g.x2[:, bass.ds(k * D, D)], ACT.Identity, bias=g.hb[:, bass.ds(k, 1)],
                               scale=g.hs[:, bass.ds(k, 1)]).then_inc(h_ok, 1)

            def x_self(k):
                act.wait_ge(h_ok, k + 1)
                xs = g.x2[:, bass.ds(k * D, D)]
                act.activation(xs, xs, ACT.Identity, bias=g.xb[:, bass.ds(k, 1)], scale=g.xa[:, bass.ds(k, 1)]).then_inc(x_ok, 1)

            act.wait_ge(scales_ok, 1)
            for k in range(2):
                h_row(k, k)
                x_self(k)
            h_high(0, 0)

            def body(it, q, par):
                def exponential(k, kpar, j):
                    act.wait_ge(sub_ok, k * 4 + j + 1)
                    e = gate[kpar][:, 4 * j:4 * j + 4, 0:GATE]
                    act.activation(e, e, ACT.Exp).then_inc(ex_ok, 1)

                def logits(j):
                    if not (isinstance(it, int) and it < 2) and j % 2 == 0:
                        act.wait_ge(g_out[par][j // 2], 16 * q)
                    act.wait_ge(l_ps, it * 8 + j + 1)
                    act.activation(gate[par][:, 2 * j:2 * j + 2, 0:GATE], lp[j % 3][:, :, 0:GATE],
                                   ACT.Copy, scale=1.0 / WS).then_inc(l_ev, 1)

                if on(it, 0):
                    act.wait_ge(v_ok, it + 1)
                    if not (isinstance(it, int) and it < 2):
                        act.wait_ge(zr_ok, 8 * it - 8)
                    act.activation(vs[par], v_ps, ACT.Copy, scale=1.0 / WS).then_inc(v_sb, 1)
                    logits(0)
                    if ahead(it):
                        h_high(it + 1, 1 - par)
                    logits(1)
                if on(it, 1):
                    exponential(it - 1, 1 - par, 3)
                if on(it, LAG_O):
                    k = it - LAG_O
                    act.wait_ge(sc, 3 * STEPS * (k + 1))
                    if not (isinstance(it, int) and k == 0):
                        act.wait_ge(y_out, 16 * k)
                    act.activation(yc.rearrange("p (t i) -> p t i", i=M), state[par], ACT.Copy).then_inc(yc_ok, 1)
                if on(it, 0):
                    for j in range(2, HEADS // 2):
                        logits(j)
                    if not isinstance(it, int) or it + 2 < TILES:
                        h_row(it + 2, par)
                        x_self(it + 2)
                if on(it, LAG_O):
                    k = it - LAG_O
                    act.wait_ge(ot_ps, k + 1)
                    if not (isinstance(it, int) and k == 0):
                        act.wait_ge(o_ok, k)
                    act.activation(ot[:, 0].rearrange("p k t -> p (k t)"), tpo, ACT.Copy).then_inc(ot_hi, 1)
                if on(it, 0):
                    for j in range(3):
                        exponential(it, par, j)

            iterations(act, body)

        @block.gpsimd
        def _(pool):
            def body(it, q, par):
                if on(it, LAG_R):
                    k = it - LAG_R
                    gv = gate[1 - par][:, :, 0:GATE].rearrange("p h (i j) -> p h i j", j=M + 1)
                    for j in range(4):
                        pool.wait_ge(ex_ok, k * 4 + j + 1)
                        e = gv[:, 4 * j:4 * j + 4]
                        c = (k * 4 + j) * 4
                        t4 = tree.rearrange("p (h i) c -> p h i c", h=4)
                        pool.tensor_tensor(t4, e[:, :, :, 1:9], e[:, :, :, 9:17], ALU.add).then_inc(tr, 1)
                        for n, wd in enumerate((4, 2, 1)):
                            pool.wait_ge(tr, c + n + 1)
                            pool.tensor_tensor(tree[:, :, 0:wd], tree[:, :, 0:wd], tree[:, :, wd:2 * wd], ALU.add).then_inc(tr, 1)
                        pool.wait_ge(tr, c + 4)
                        if j == 0 and not (isinstance(it, int) and k == 0):
                            pool.wait_ge(zr_ok, 8 * k)
                        pool.tensor_tensor(zsum[:, 64 * j:64 * j + 64].rearrange("p (h i) -> p h i", h=4),
                                           t4[:, :, :, 0], e[:, :, :, 0], ALU.add).then_inc(z_ok, 1)
                        pool.wait_ge(z_ok, k * 4 + j + 1)
                if on(it, 0) and not by_vector(it):
                    for j in range(4):
                        subtract_maxima(pool, it, par, j)

            iterations(pool, body)

        @block.vector
        def _(dve):
            dve.memset(state[1][:, STEPS - 1], 0.0).then_inc(rc, 1)
            dve.engine_nop().then_inc(var_ok, 1)
            chain = [1]

            def then(ins):
                ins.then_inc(rc, 1)
                chain[0] += 1
                dve.wait_ge(rc, chain[0])

            dve.wait_ge(std, 1)
            refined_rsqrt(dve, g.rstd, g.std, g.mv3[:, :, 1], EPS, g.ms, then)
            then(dve.tensor_tensor(g.ms, g.rstd, g.rstd, ALU.mult))
            then(dve.tensor_tensor(g.ms, g.ms, g.mv3[:, :, 1], ALU.mult))
            dve.engine_nop().then_inc(ms_ok, 1)
            dve.wait_ge(rms, 1)
            refined_rsqrt(dve, g.hs, g.rms, g.ms, EPS, g.xa, then)
            then(dve.tensor_copy(g.rms, g.hs))
            then(dve.tensor_tensor(g.hs, g.rms, g.rstd, ALU.mult))
            then(dve.tensor_scalar(g.xa, g.rstd, 1.0, None, ALU.add))
            then(dve.scalar_tensor_tensor(out=g.xb, in0=g.mv3[:, :, 0], scalar=-1.0, in1=g.rstd, op0=ALU.mult, op1=ALU.mult))
            then(dve.scalar_tensor_tensor(out=g.hb, in0=g.mv3[:, :, 0], scalar=-1.0, in1=g.hs, op0=ALU.mult, op1=ALU.mult))

            def h_low(k, par):
                dve.wait_ge(ht_hi, k + 1)
                dve.tensor_tensor(ht[par][:, 1].rearrange("p k t -> p (k t)"), tph,
                                  ht[par][:, 0].rearrange("p k t -> p (k t)"), ALU.subtract).then_inc(ht_lo, 1)

            dve.engine_nop().then_inc(scales_ok, 1)
            h_low(0, 0)

            def body(it, q, par):
                def low_next():
                    h_low(it + 1, 1 - par)

                def maximum(n):
                    h, rows_of = n // MAX_PARTS, M // MAX_PARTS
                    first_row = n % MAX_PARTS * rows_of
                    if n % (2 * MAX_PARTS) == 0:
                        dve.wait_ge(l_ev, it * 8 + h // 2 + 1)
                    if n == 0 and not (isinstance(it, int) and it < 2):
                        dve.wait_ge(sub_ok, 4 * it - 4)
                    dve.tensor_reduce(mx[par][:, rows_of * n:rows_of * (n + 1)],
                                      gate[par][:, h, 0:GATE].rearrange("p (i j) -> p i j", j=M + 1)[
                                          :, first_row:first_row + rows_of],
                                      AX.X, ALU.max).then_inc(mx_ok, 1)

                def invert(j):
                    k = it - LAG_R
                    dve.wait_ge(z_ok, 4 * k + j + 1)
                    dve.reciprocal(gate[1 - par][:, 4 * j:4 * j + 4, GATE:ROW],
                                   zsum[:, 64 * j:64 * j + 64].rearrange("p (h i) -> p h i", h=4)).then_inc(zr_ok, 1)

                def times_v(j):
                    k = it - LAG_R
                    if j == 0:
                        dve.wait_ge(v_sb, k + 1)
                    e0 = gate[1 - par][:, 4 * j:4 * j + 4, 0:GATE:M + 1]
                    dve.tensor_tensor(e0, e0, vs[1 - par][:, 64 * j:64 * j + 64].rearrange("p (h i) -> p h i", h=4),
                                      ALU.mult).then_inc(zr_ok, 1)

                def out_low():
                    k = it - LAG_O
                    dve.wait_ge(ot_hi, k + 1)
                    dve.tensor_tensor(ot[:, 1].rearrange("p k t -> p (k t)"), tpo, ot[:, 0].rearrange("p k t -> p (k t)"),
                                      ALU.subtract).then_inc(ot_lo, 1)

                def add_out():
                    k = it - LAG_O
                    dve.wait_ge(o_ok, k + 1)
                    dve.wait_ge(x_ok, k + 1)
                    xs = g.x2[:, bass.ds(k * D, D)]
                    dve.scalar_tensor_tensor(out=xs, in0=o_ps, scalar=1.0 / WS, in1=xs, op0=ALU.mult, op1=ALU.add).then_inc(x_add, 1)

                def other_work(place):
                    what, n = FILLERS.get(place, (None, 0))
                    if what == "maximum" and on(it, 0):
                        maximum(n)
                        if by_vector(it) and (n + 1) % (4 * MAX_PARTS) == 0:
                            subtract_maxima(dve, it, par, n // (4 * MAX_PARTS))
                    if what == "maximum" and isinstance(it, int) and it >= TILES and n < HEADS:
                        new_statistics(HEADS * (it - TILES) + n)
                    if what == "invert" and on(it, LAG_R):
                        invert(n)
                    if what == "times_v" and on(it, LAG_R):
                        times_v(n)
                    if what == "low_next" and ahead(it):
                        low_next()
                    if what == "out_low" and on(it, LAG_O):
                        out_low()
                    if what == "add_out" and on(it, LAG_O):
                        add_out()

                def new_statistics(t):
                    if t <= it - LAG_O - 1:
                        dve.wait_ge(x_add, t + 1)
                        tile_statistics(g, dve, t, stat)

                scan = on(it, LAG_S)
                k = it - LAG_S
                sg, st, before = step_g[1 - par], state[1 - par], state[par]
                if scan:
                    uses = q - (2 if par == 0 else 1)
                    dve.wait_ge(g_in[1 - par], 16 * BATCH * (uses + 1))
                    if not (isinstance(it, int) and k < 2):
                        dve.wait_ge(yc_ok, k - 1)
                for t in range(STEPS):
                    c = 3 * STEPS * k + 3 * t
                    rows = sg[:, t, 0:GATE].rearrange("p (i j) -> p i j", j=M + 1)
                    prev = st[:, t - 1] if t else before[:, STEPS - 1]
                    if scan:
                        if not (isinstance(c, int) and c == 0):
                            dve.wait_ge(sc, c)
                        dve.tensor_tensor(rows[:, :, 1:], rows[:, :, 1:],
                                          prev.unsqueeze(1).broadcast_to((P, M, M)), ALU.mult).then_inc(sc, 1)
                    other_work(3 * t)
                    if scan:
                        dve.wait_ge(sc, c + 1)
                        dve.tensor_reduce(dots, rows, AX.X, ALU.add).then_inc(sc, 1)
                    other_work(3 * t + 1)
                    if scan:
                        dve.wait_ge(sc, c + 2)
                        dve.tensor_tensor(st[:, t], dots, sg[:, t, GATE:ROW], ALU.mult).then_inc(sc, 1)
                    other_work(3 * t + 2)

            iterations(dve, body)
            for t in range(TILES - 3, TILES):
                dve.wait_ge(x_add, t + 1)
                tile_statistics(g, dve, t, stat)
            mean_and_variance(g, dve, stat)



def build(nc, a, out):
    g = Core()
    with ExitStack() as ctx:
        def sb(name, shape, dt):
            return ctx.enter_context(nc.sbuf_tensor(name, shape, dt))[:]

        g.x2 = sb("x_tokens", [P, TILES * D], F32)
        g.x = g.x2.rearrange("p (n d) -> p n d", d=D)
        g.wf = sb("expert_weights", [P, (NE + 1) * WEXP], F16)
        late_words = 2 * KD * HEADS * GATE // 2 + 2 * KD * D
        g.late = sb("gate_weights", [P, late_words], F32)
        g.xn = g.late[:, 0:TILES * D]
        g.xn16 = g.xn.bitcast(F16)
        g.work_words = 6144
        g.work = sb("work", [P, g.work_words], F32)
        g.ident = sb("identity", [P, P], F32)
        g.ident16 = sb("identity16", [P, P], F16)
        g.ones = sb("ones", [P, P], F16)
        g.before = sb("before", [P, P], F16)
        g.rw_raw = sb("router_raw", [P, KD, NE], F32)
        g.rw = sb("router_weights", [P, 2, KD, NE], F16)
        g.nw = sb("norm_weights", [P, KD], F32)
        g.nws = sb("scaled_norm_weights", [P, KD], F32)
        g.bias = sb("router_bias", [P, NE], F32)
        g.eps = sb("eps", [P, 1], F32)
        g.iota_i = g.work[:, 1024:1024 + NE + SHARED + SPARSE + TILES + P].bitcast(I32)
        g.token = sb("token_numbers", [P, TILES], F32)
        g.lanes = sb("lanes", [P, P], F16)
        g.tok = sb("tokens_of_slots", [P, SLOT_TILES], U32)
        g.iota = sb("iota", [P, NE + SHARED + SPARSE], F32)
        g.stats = sb("stats", [P, TILES * 6], F32)
        g.mv = sb("mean_var", [P, TILES * 2], F32)
        g.mv3 = g.mv.rearrange("p (t c) -> p t c", c=2)
        g.std, g.rstd, g.rms, g.ms, g.hs, g.xa, g.xb, g.hb = (sb(n, [P, TILES], F32) for n in (
            "std", "rstd", "rms", "ms", "hs", "xa", "xb", "hb"))
        g.cw = sb("expert_shares", [P, 2 * TILES], F32)
        g.slot = sb("slots_of_tokens", [P, 2 * TILES], U32)
        g.texp = sb("experts_of_tiles", [P, SPARSE], I32)
        g.psum = ctx.enter_context(nc.psum_tensor("psum", [P, 8, 512], F32))[:]
        rows = SPARSE * ITEM
        g.xn_dram = nc.dram_tensor("token_rows", (BATCH * TIME, D), F32, kind="Internal").ap()
        g.outs = nc.dram_tensor("slot_outputs", (rows, D), F32, kind="Internal").ap()
        g.w_dram = nc.dram_tensor("split_weights", (P, (NE - KEPT) * WEXP), F16, kind="Internal").ap()
        gd = [nc.dram_tensor(f"gates{r}", (P, HEADS * ROW), F32, kind="Internal").ap() for r in range(2)]
        g.g_dram = gd
        g.y_dram = nc.dram_tensor("head_outputs", (P, STEPS * M), F32, kind="Internal").ap()
        g.raw_in = {e: ctx.enter_context(nc.semaphore(f"raw_in{e}")) for e in range(KEPT, NE)}
        g.gat_in = [ctx.enter_context(nc.semaphore(f"gat_in{r}")) for r in range(GATHERS)]
        g.gates = GateWeights(g, a, lambda n: ctx.enter_context(nc.semaphore(n)))
        load_inputs(nc, g, a)
        ffn(nc, g, "f1", a, None)
        attention(nc, g, a)
        ffn(nc, g, "f2", None, out)


_INS = {"L0_attn_x": "x", "L0_attn_norm_w": "norm_w", "L0_attn_W_v": "W_v", "L0_attn_W_a": "W_a",
        "L0_attn_W_out": "W_out", "L0_ffn_router_w": "router_w", "L0_ffn_experts_bias": "bias",
        "L0_ffn_w1": "w1", "L0_ffn_w3": "w3", "L0_ffn_w2": "w2", "L0_ffn_sw1": "sw1", "L0_ffn_sw3": "sw3",
        "L0_ffn_sw2": "sw2"}


def kernel(**inputs):
    import numpy as np
    import concourse.bacc as bacc
    from concourse.bass_utils import run_bass_kernel_spmd

    nc = bacc.Bacc("TRN2", target_bir_lowering=False, num_devices=1)
    arrays, aps = {}, {}
    for name, short in _INS.items():
        arr = np.ascontiguousarray(inputs[name])
        arrays[f"in_{short}"] = arr
        aps[short] = nc.dram_tensor(f"in_{short}", arr.shape, mybir.dt.from_np(arr.dtype), kind="ExternalInput").ap()
    out = nc.dram_tensor("out", (BATCH, TIME, D), F32, kind="ExternalOutput").ap()
    build(nc, aps, out)
    r = run_bass_kernel_spmd(nc, [arrays], core_ids=[0])
    return np.asarray(r.results[0]["out"])
```
